# Optimizing a Trainium2 kernel written in Bass

```python
import numpy as np
import jax
import jax.numpy as jnp

def _softmax(x, axis=-1):
    return jax.nn.softmax(x, axis=axis)

def _gelu(x):
    return jax.nn.gelu(x, approximate=True)

def _silu(x):
    return jax.nn.silu(x)

def _sigmoid(x):
    return jax.nn.sigmoid(x)

def _layernorm(x, axis=-1, eps=1e-05):
    m = jnp.mean(x, axis=axis, keepdims=True)
    v = jnp.var(x, axis=axis, keepdims=True)
    return (x - m) / jnp.sqrt(v + eps)

def _scatter_add(tgt, idx, src, axis=0):
    return tgt.at[idx].add(src)

def _segment_sum(src, seg, n):
    return jax.ops.segment_sum(src, seg, n)
kernel_name = 'mk_hybrid_d1_jaxref_r8_dd9ccc'

def setup_inputs(seed: int=0):
    np.random.seed(seed)
    _w = jnp.asarray

    def _L0_attn_a_setup():
        import jax, jax.numpy as jnp
        import numpy as np
        D_MODEL = 128
        N_HEAD = 16
        HEAD_DIM = D_MODEL // N_HEAD
        LN_EPS = 1e-05

        def _split_heads(y, B, T):
            return y.reshape(B, T, N_HEAD, HEAD_DIM).transpose(1, 0, 2, 3)

        def _layernorm(y, gamma, beta):
            mu = jnp.mean(y, axis=-1, keepdims=True)
            var = jnp.mean(jnp.square(y - mu), axis=-1, keepdims=True)
            return (y - mu) * jax.lax.rsqrt(var + LN_EPS) * gamma + beta
        key = jax.random.key(seed)
        ks = jax.random.split(key, 8)
        B, T = (2, 256)
        s = 1.0 / np.sqrt(D_MODEL)
        x = jax.random.normal(ks[0], (B, T, D_MODEL), dtype=jnp.float32)
        Wq = jax.random.uniform(ks[1], (D_MODEL, D_MODEL), jnp.float32, -s, s)
        Wk = jax.random.uniform(ks[2], (D_MODEL, D_MODEL), jnp.float32, -s, s)
        Wv = jax.random.uniform(ks[3], (D_MODEL, D_MODEL), jnp.float32, -s, s)
        Wg = jax.random.uniform(ks[4], (D_MODEL, D_MODEL), jnp.float32, -s, s)
        Wo = jax.random.uniform(ks[5], (D_MODEL, D_MODEL), jnp.float32, -s, s)
        gamma = jnp.ones((D_MODEL,), jnp.float32)
        beta = jnp.zeros((D_MODEL,), jnp.float32)
        return {'x': x, 'Wq': Wq, 'Wk': Wk, 'Wv': Wv, 'Wg': Wg, 'Wo': Wo, 'gamma': gamma, 'beta': beta}
    _L0_attn_a_in = _L0_attn_a_setup()

    def _L0_attn_b_setup():
        import jax, jax.numpy as jnp
        import numpy as np
        NUM_HEADS = 16

        def _sinusoid_rel_pos(seq_len, dim):
            pos = jnp.arange(seq_len - 1, -1, -1, dtype=jnp.float32)
            inv_freq = 1.0 / 10000.0 ** (jnp.arange(0, dim, 2, dtype=jnp.float32) / dim)
            ang = pos[:, None] * inv_freq[None, :]
            return jnp.concatenate([jnp.sin(ang), jnp.cos(ang)], axis=-1)

        def _rel_shift(x):
            B, H, S, L = x.shape
            x = jnp.pad(x, ((0, 0), (0, 0), (0, 0), (1, 0)))
            x = x.reshape(B, H, L + 1, S)
            return x[:, :, 1:S + 1, :]
        key = jax.random.key(seed)
        ks = jax.random.split(key, 8)
        B, S, C = (2, 256, 128)
        Dk, Dv, H = (128, 128, NUM_HEADS)
        dk = Dk // H
        scale = 0.02
        return {'x': jax.random.normal(ks[0], (B, S, C), dtype=jnp.float32), 'Wq': jax.random.normal(ks[1], (C, Dk), dtype=jnp.float32) * scale, 'Wk': jax.random.normal(ks[2], (C, Dk), dtype=jnp.float32) * scale, 'Wv': jax.random.normal(ks[3], (C, Dv), dtype=jnp.float32) * scale, 'u': jax.random.normal(ks[4], (H, dk), dtype=jnp.float32) * scale, 'v': jax.random.normal(ks[5], (H, dk), dtype=jnp.float32) * scale, 'Wo': jax.random.normal(ks[6], (Dv, C), dtype=jnp.float32) * scale, 'bo': jnp.zeros((C,), dtype=jnp.float32)}
    _L0_attn_b_in = _L0_attn_b_setup()

    def _L0_ffn_setup():
        import jax, jax.numpy as jnp
        import numpy as np
        HIDDEN = 128
        INTER = 512
        N_EXPERTS = 8

        def geglu(x, w1, w2, w3):
            return jax.nn.gelu(x @ w1, approximate=False) * (x @ w2) @ w3
        key = jax.random.key(seed)
        ks = jax.random.split(key, 8)
        s = 0.02
        x = jax.random.normal(ks[0], (2, 256, HIDDEN), dtype=jnp.float32)
        w1s = jax.random.normal(ks[1], (HIDDEN, INTER), dtype=jnp.float32) * s
        w2s = jax.random.normal(ks[2], (HIDDEN, INTER), dtype=jnp.float32) * s
        w3s = jax.random.normal(ks[3], (INTER, HIDDEN), dtype=jnp.float32) * s
        W1 = jax.random.normal(ks[4], (N_EXPERTS, HIDDEN, INTER), dtype=jnp.float32) * s
        W2 = jax.random.normal(ks[5], (N_EXPERTS, HIDDEN, INTER), dtype=jnp.float32) * s
        W3 = jax.random.normal(ks[6], (N_EXPERTS, INTER, HIDDEN), dtype=jnp.float32) * s
        Wg = jax.random.normal(ks[7], (HIDDEN, N_EXPERTS), dtype=jnp.float32) * s
        return {'x': x, 'w1s': w1s, 'w2s': w2s, 'w3s': w3s, 'W1': W1, 'W2': W2, 'W3': W3, 'Wg': Wg}
    _L0_ffn_in = _L0_ffn_setup()
    _d = {'L0_attn_a_x': _L0_attn_a_in['x'], 'L0_attn_a_Wq': _L0_attn_a_in['Wq'], 'L0_attn_a_Wk': _L0_attn_a_in['Wk'], 'L0_attn_a_Wv': _L0_attn_a_in['Wv'], 'L0_attn_a_Wg': _L0_attn_a_in['Wg'], 'L0_attn_a_Wo': _L0_attn_a_in['Wo'], 'L0_attn_a_gamma': _L0_attn_a_in['gamma'], 'L0_attn_a_beta': _L0_attn_a_in['beta'], 'L0_attn_b_Wq': _L0_attn_b_in['Wq'], 'L0_attn_b_Wk': _L0_attn_b_in['Wk'], 'L0_attn_b_Wv': _L0_attn_b_in['Wv'], 'L0_attn_b_u': _L0_attn_b_in['u'], 'L0_attn_b_v': _L0_attn_b_in['v'], 'L0_attn_b_Wo': _L0_attn_b_in['Wo'], 'L0_attn_b_bo': _L0_attn_b_in['bo'], 'L0_ffn_w1s': _L0_ffn_in['w1s'], 'L0_ffn_w2s': _L0_ffn_in['w2s'], 'L0_ffn_w3s': _L0_ffn_in['w3s'], 'L0_ffn_W1': _L0_ffn_in['W1'], 'L0_ffn_W2': _L0_ffn_in['W2'], 'L0_ffn_W3': _L0_ffn_in['W3'], 'L0_ffn_Wg': _L0_ffn_in['Wg']}
    _x0 = _d['L0_attn_a_x']
    _d['L0_attn_a_x'] = jax.random.normal(jax.random.fold_in(jax.random.key(seed), 1), (8, 256, 128), dtype=_x0.dtype)
    del _x0
    return _d

def reference(L0_attn_a_x, L0_attn_a_Wq, L0_attn_a_Wk, L0_attn_a_Wv, L0_attn_a_Wg, L0_attn_a_Wo, L0_attn_a_gamma, L0_attn_a_beta, L0_attn_b_Wq, L0_attn_b_Wk, L0_attn_b_Wv, L0_attn_b_u, L0_attn_b_v, L0_attn_b_Wo, L0_attn_b_bo, L0_ffn_w1s, L0_ffn_w2s, L0_ffn_w3s, L0_ffn_W1, L0_ffn_W2, L0_ffn_W3, L0_ffn_Wg):

    def _L0_attn_a_ref(x, Wq, Wk, Wv, Wg, Wo, gamma, beta):
        import jax, jax.numpy as jnp
        import numpy as np
        D_MODEL = 128
        N_HEAD = 16
        HEAD_DIM = D_MODEL // N_HEAD
        LN_EPS = 1e-05

        def _split_heads(y, B, T):
            return y.reshape(B, T, N_HEAD, HEAD_DIM).transpose(1, 0, 2, 3)

        def _layernorm(y, gamma, beta):
            mu = jnp.mean(y, axis=-1, keepdims=True)
            var = jnp.mean(jnp.square(y - mu), axis=-1, keepdims=True)
            return (y - mu) * jax.lax.rsqrt(var + LN_EPS) * gamma + beta
        B, T, D = x.shape
        q = _split_heads(jnp.einsum('btd,ed->bte', x, Wq), B, T)
        k = _split_heads(jnp.einsum('btd,ed->bte', x, Wk), B, T)
        v = _split_heads(jnp.einsum('btd,ed->bte', x, Wv), B, T)
        a = jax.nn.sigmoid(_split_heads(jnp.einsum('btd,ed->bte', x, Wg), B, T))

        def step(h, inp):
            q_t, k_t, v_t, a_t = inp
            h = a_t[..., None] * h + k_t[..., None] * v_t[..., None, :]
            y_t = jnp.einsum('bhd,bhde->bhe', q_t, h)
            return (h, y_t)
        h0 = jnp.zeros((B, N_HEAD, HEAD_DIM, HEAD_DIM), x.dtype)
        _, y = jax.lax.scan(step, h0, (q, k, v, a))
        y = y.transpose(1, 0, 2, 3).reshape(B, T, D)
        y = _layernorm(y, gamma, beta)
        return jnp.einsum('btd,ed->bte', y, Wo)

    def _L0_attn_b_ref(x, Wq, Wk, Wv, u, v, Wo, bo):
        import jax, jax.numpy as jnp
        import numpy as np
        NUM_HEADS = 16

        def _sinusoid_rel_pos(seq_len, dim):
            pos = jnp.arange(seq_len - 1, -1, -1, dtype=jnp.float32)
            inv_freq = 1.0 / 10000.0 ** (jnp.arange(0, dim, 2, dtype=jnp.float32) / dim)
            ang = pos[:, None] * inv_freq[None, :]
            return jnp.concatenate([jnp.sin(ang), jnp.cos(ang)], axis=-1)

        def _rel_shift(x):
            B, H, S, L = x.shape
            x = jnp.pad(x, ((0, 0), (0, 0), (0, 0), (1, 0)))
            x = x.reshape(B, H, L + 1, S)
            return x[:, :, 1:S + 1, :]
        B, S, C = x.shape
        H = NUM_HEADS
        dk = Wq.shape[1] // H
        dv = Wv.shape[1] // H
        Q = (x @ Wq).reshape(B, S, H, dk).transpose(0, 2, 1, 3)
        K = (x @ Wk).reshape(B, S, H, dk).transpose(0, 2, 1, 3)
        V = (x @ Wv).reshape(B, S, H, dv).transpose(0, 2, 1, 3)
        r = _sinusoid_rel_pos(S, dk)
        term1 = jnp.einsum('bhqd,bhkd->bhqk', Q, K)
        term2 = jnp.einsum('bhqd,kd->bhqk', Q, r)
        term3 = jnp.einsum('hd,bhkd->bhk', u, K)[:, :, None, :]
        term4 = jnp.einsum('hd,kd->hk', v, r)[None, :, None, :]
        scores = (term1 + term3 + _rel_shift(term2 + term4)) / jnp.sqrt(jnp.asarray(dk, dtype=x.dtype))
        attn = jax.nn.softmax(scores, axis=-1)
        out = jnp.einsum('bhqk,bhkd->bqhd', attn, V).reshape(B, S, H * dv)
        return out @ Wo + bo

    def _L0_ffn_ref(x, w1s, w2s, w3s, W1, W2, W3, Wg):
        import jax, jax.numpy as jnp
        import numpy as np
        HIDDEN = 128
        INTER = 512
        N_EXPERTS = 8

        def geglu(x, w1, w2, w3):
            return jax.nn.gelu(x @ w1, approximate=False) * (x @ w2) @ w3
        B, T, C = x.shape
        xf = x.reshape(-1, C)
        shared = geglu(xf, w1s, w2s, w3s)
        logits = xf @ Wg
        idx = jnp.argmax(logits, axis=-1)
        final = jnp.zeros_like(xf)
        for e in range(N_EXPERTS):
            y = geglu(xf, W1[e], W2[e], W3[e])
            final = final + jnp.where((idx == e)[:, None], y, 0.0)
        return (shared + final).reshape(B, T, C)
    x = L0_attn_a_x
    x = x + _L0_attn_a_ref(_layernorm(x, axis=-1), L0_attn_a_Wq, L0_attn_a_Wk, L0_attn_a_Wv, L0_attn_a_Wg, L0_attn_a_Wo, L0_attn_a_gamma, L0_attn_a_beta)
    x = x + _L0_ffn_ref(_layernorm(x, axis=-1), L0_ffn_w1s, L0_ffn_w2s, L0_ffn_w3s, L0_ffn_W1, L0_ffn_W2, L0_ffn_W3, L0_ffn_Wg)
    x = x + _L0_attn_b_ref(_layernorm(x, axis=-1), L0_attn_b_Wq, L0_attn_b_Wk, L0_attn_b_Wv, L0_attn_b_u, L0_attn_b_v, L0_attn_b_Wo, L0_attn_b_bo)
    x = x + _L0_ffn_ref(_layernorm(x, axis=-1), L0_ffn_w1s, L0_ffn_w2s, L0_ffn_w3s, L0_ffn_W1, L0_ffn_W2, L0_ffn_W3, L0_ffn_Wg)
    return x

_drawn_inputs = setup_inputs


def setup_inputs(seed=0):
    import zlib

    import numpy as np

    out = dict(_drawn_inputs(seed))
    spreads = {'L0_attn_a_gamma': (1.0, 0.2), 'L0_attn_a_beta': (0.0, 0.1), 'L0_attn_b_bo': (0.0, 0.1)}
    factors = {'L0_attn_b_Wq': 8.0,
     'L0_attn_b_Wk': 8.0,
     'L0_attn_b_Wv': 8.0,
     'L0_attn_b_u': 8.0,
     'L0_attn_b_v': 8.0,
     'L0_attn_b_Wo': 8.0,
     'L0_ffn_w1s': 2.808,
     'L0_ffn_w2s': 2.76,
     'L0_ffn_w3s': 2.754,
     'L0_ffn_W1': 2.834,
     'L0_ffn_W2': 2.801,
     'L0_ffn_W3': 2.796,
     'L0_ffn_Wg': 2.987}
    for name, (base, spread) in spreads.items():
        noise = np.random.default_rng([zlib.crc32(name.encode()), seed]).standard_normal(out[name].shape)
        drawn = base * np.exp(spread * noise) if base else spread * noise
        out[name] = jnp.asarray(drawn.astype(out[name].dtype))
    for name, factor in factors.items():
        out[name] = (out[name] * factor).astype(out[name].dtype)
    return out
```

```python
from contextlib import ExitStack

import numpy as np

import concourse.bass as bass
from concourse import mybir

ALU = mybir.AluOpType
ACT = mybir.ActivationFunctionType
AX_X = mybir.AxisListType.X
F32 = mybir.dt.float32
BF16 = mybir.dt.bfloat16
U8 = mybir.dt.uint8
U32 = mybir.dt.uint32
I32 = mybir.dt.int32

P = 128
BATCH, SEQ, D = 8, 256, 128
TOK = BATCH * SEQ
NT = TOK // P
QT = SEQ // P
H, DH = 16, 8
INTER = 512
KI = INTER // P
NE = 8
CH = 512
NC = TOK // CH
SPC = CH // SEQ
SLOT_TILES = NT + NE
SLOTS = SLOT_TILES * P
ROWW = D + 1
NO_TOKEN = 1 << 20
EPS = 1e-5
BIG = 1e30
SCALE = float(DH) ** -0.5
Q_PART = [0, 0, 1, 0, 2, 1]
K_PART = [0, 1, 0, 2, 0, 1]
NPROD = len(Q_PART)
HALF = NPROD * DH
STK = 2 * HALF
HG = 4
UPB = QT * (H // HG)
UNITS = BATCH * UPB
BODY = 2 * UPB
VW = 32

C_ID, C_SD, C_TRI, C_ONE = 0, 128, 256, 384
C_IOTA, C_THR, C_SLOT, C_LAST = 512, 520, 648, 840
C_COS1 = 856
C_SIN1, C_COS2, C_SIN2 = C_COS1 + SEQ, C_COS1 + 2 * SEQ, C_COS1 + 3 * SEQ
C_ALL = C_COS1 + 4 * SEQ
W_Q, W_K, W_G, W_O, W_BS, W_BQ, W_BV, W_BK, W_BO, W_R = [128 * j for j in range(10)]
W_COL = W_R + NE
W_ALL = W_COL + 5


class Signal:

    def __init__(self, sem, start=0):
        self.sem, self.start = sem, start

    def item(self, n):
        return n + (self.start + 1)

    def spare(self, n, ring):
        return n + (self.start + 1 - ring)

    def moved(self, n):
        return 16 * n + self.start


def build_program(nc, x_in, weights, spread_w, head_sums, consts, rows, positions, row96,
                  token_ids, clear_row, w1, w2, w3, w1s, w2s, w3s, out, last_phase=4):
    with ExitStack() as ctx:
        def sb(name, shape, dt=F32):
            return ctx.enter_context(nc.sbuf_tensor(name, shape, dt))

        def signal(name, start=0):
            return Signal(ctx.enter_context(nc.semaphore(name)), start)

        def dram(name, shape, dt=F32):
            return nc.dram_tensor(name, shape, dt, kind="Internal").ap()

        def take_in(eng):
            eng.sem_inc(waits_taken.sem, 1)

        x = sb("x", [P, NT, D])
        xn = sb("xn", [P, NT, ROWW])
        xT = sb("xT", [P, TOK + P])
        W = sb("W", [P, W_ALL])
        C = sb("C", [P, C_ALL])
        w12 = sb("w12", [P, NE + 1, 2 * INTER])
        w3t = sb("w3t", [P, NE + 1, KI, D])
        stats = sb("stats", [P, NT, 6])
        small = sb("small", [P, 8, NT])
        cb = sb("cb", [P, 4, P], BF16)
        crow = sb("crow", [P, ROWW])
        one8b = sb("one8b", [P, NT * NE], BF16)
        slotu = sb("slotu", [P, NT], U32)
        slot_ids = sb("slot_ids", [P, SLOT_TILES], U32)
        idsb = sb("idsb", [P, NT], I32)
        eword = sb("eword", [P, SLOT_TILES], I32)
        nsd = sb("nsd", [P, NT, H])
        nmax = sb("nmax", [P, 2, H])
        mxs = sb("mxs", [P, 2, HG])
        esm = sb("esm", [P, 2, 4, H])
        msk = sb("msk", [P, 2, HG, P], U8)
        rowb = sb("rowb", [P, 2, D])
        rpos = sb("rpos", [DH, 2, SEQ])
        rpb = sb("rpb", [DH, 3, SEQ], BF16)
        arena = sb("arena", [P, 24700])
        used = [0]

        def cut(*shape, dt=F32):
            n = int(np.prod(shape))
            words = n if dt == F32 else n // 2
            ap = arena[:, used[0]:used[0] + words]
            used[0] += words
            assert used[0] <= 24700
            if dt != F32:
                ap = ap.bitcast(dt)
            names = "abcd"[:len(shape)]
            if len(shape) == 1:
                return ap
            return ap.rearrange(f"p ({' '.join(names)}) -> p {' '.join(names)}", **dict(zip(names, shape)))

        aT, qT, kT, yT = cut(TOK), cut(TOK), cut(TOK), cut(TOK)
        wv, hsum = cut(DH * P), cut(DH * P)
        kvb, hb, zb = cut(2, CH), cut(4, CH), cut(4, CH)
        ynT = cut(TOK)
        yn = xn[:, :, 0:D]
        used[0] = 0
        gk, hT = cut(2, CH), cut(KI, CH)
        xr, xrT = cut(4, ROWW), cut(4, P)
        eg, eh, ehT, er = cut(2, CH), cut(2, CH), cut(2, CH), cut(SLOT_TILES, D)
        yback = cut(NT, D)
        mx8, ix8f, ixf, one8 = cut(NT, 8), cut(NT, 8), cut(NT), cut(NT, NE)
        ix8 = ix8f.bitcast(U32)
        tot, csum, cmp8 = cut(NE, NT), cut(NE, NT), cut(NE, NT)
        base, work, cnt8 = cut(NE, NT), cut(NT, NE), cut(6, NE)
        slotf, ecmp, eidf = cut(NT), cut(SLOT_TILES, NE), cut(2, SLOT_TILES)
        used[0] = 0
        vnext = cut(NT, D)
        raw = cut(2, 4, CH)
        rot = cut(2, 4, CH)
        rest = cut(2, 4, CH)
        pb = cut(2, 12, CH, dt=BF16)
        vpad = cut(2, H, VW)
        tq = cut(2, 2, D)
        used[0] = NT * D
        kst = cut(2, H, SEQ, dt=BF16)
        qlo = cut(2, H, SEQ, dt=BF16)
        qup = cut(2, H, SEQ, dt=BF16)
        vring = cut(2, QT, H * VW)
        pr, prT = cut(2, HG, SEQ), cut(2, HG, QT * P)
        osb, otok, t4 = cut(2 * HG, P), cut(2, H, 9), cut(4, D)
        on = xn[:, :, 0:D]
        onT = xT[:, 0:TOK]

        PS = ctx.enter_context(nc.psum_tensor("PS", [P, 8, 512], F32))
        ident = C[:, C_ID:C_ID + P]

        slot_rows = dram("slot_rows", [SLOTS, ROWW])
        token_out = dram("token_out", [TOK, D])
        parts = dram("parts", [4, 3, P, TOK + P], BF16)
        pos_parts = dram("pos_parts", [3, DH, SEQ], BF16)
        v_rows = dram("v_rows", [TOK, H * VW])

        x_here, weights_here, consts_here, ids_here = [signal(n) for n in
            ("x_here", "weights_here", "consts_here", "ids_here")]
        a_here, ffn_here, b_here, clear_here = [signal(n) for n in ("a_here", "ffn_here", "b_here", "clear_here")]
        consts_cast, ids_set = signal("consts_cast"), signal("ids_set")
        out_stored = signal("out_stored")
        pad_set = signal("pad_set")
        waits_taken = signal("waits_taken")
        dve_order = signal("dve_order")
        steps = [0]

        ln_var = [signal(f"ln{l}_var") for l in range(5)]
        ln_std = [signal(f"ln{l}_std") for l in range(5)]
        ln_rows = [signal(f"ln{l}_rows") for l in range(5)]
        ln_turned = [signal(f"ln{l}_turned") for l in range(5)]
        ln_cols = [signal(f"ln{l}_cols") for l in range(5)]

        a_proj, a_raw = signal("a_proj"), signal("a_raw", 3)
        a_value = signal("a_value")
        a_kv = signal("a_kv", 4)
        a_state = signal("a_state", 4)
        a_read = signal("a_read", 4)
        a_sum = signal("a_sum", 4)
        a_y = signal("a_y", 1)
        a_yrow, a_out, a_res = signal("a_yrow"), signal("a_out"), signal("a_res")

        def per_layer(name, items, start=0):
            first = signal(f"f_{name}", start)
            return [first, Signal(first.sem, start + items)]

        f_logits, f_onehot, f_prefix = per_layer("logits", 1), per_layer("onehot", 1), per_layer("prefix", 1)
        f_slots, f_experts = per_layer("slots", 1), per_layer("experts", 1)
        f_cleared, f_sent, f_ids = per_layer("cleared", 16), per_layer("sent", 16 * NT), per_layer("ids", 16)
        f_gate, f_up = per_layer("gate", NC * KI), per_layer("up", NC * KI)
        f_gelu, f_hid = per_layer("gelu", NC * KI, 2), per_layer("hid", NC * KI, 4)
        f_out, f_res = per_layer("out", NC * KI, 4), per_layer("res", NC, 1)
        st = SLOT_TILES
        e_in = list(zip(*[per_layer(f"e_in{k}", 4 * st) for k in range(4)]))
        e_turn, e_col = per_layer("e_turn", st), per_layer("e_col", st, 4)
        e_gate, e_up = per_layer("e_gate", st), per_layer("e_up", st, 4)
        e_gelu, e_hid = per_layer("e_gelu", st, 2), per_layer("e_hid", st, 2)
        e_hturn, e_hcol = per_layer("e_hturn", st, 2), per_layer("e_hcol", st, 2)
        e_out, e_row = per_layer("e_out", st, 2), per_layer("e_row", st, 4)
        e_back = per_layer("e_back", 16 * st)
        f_back, f_done = per_layer("back", 16), per_layer("done", NC)

        b_proj, b_raw = signal("b_proj"), signal("b_raw", 3)
        b_rot, b_rotp = signal("b_rot"), signal("b_rotp")
        b_hi, b_mid = signal("b_hi"), signal("b_mid")
        b_rest, b_restp = signal("b_rest"), signal("b_restp")
        b_low, b_lowp = signal("b_low", 6), signal("b_lowp", 2)
        b_parts = [signal(f"b_parts{k}", 64) for k in range(2)]
        b_pos, b_pos_out = signal("b_pos"), signal("b_pos_out")
        b_tok, b_tokv, b_tokd = signal("b_tok"), signal("b_tokv", 2), signal("b_tokd", 2)
        b_tsum = signal("b_tsum")
        b_vpad = signal("b_vpad")
        b_vout = [signal(f"b_vout{k}", 16) for k in range(2)]
        b_stack = [signal(f"b_stack{k}") for k in range(2)]
        s_scores, s_pick, s_max, s_nmax = signal("s_scores"), signal("s_pick", 1), signal("s_max"), signal("s_nmax")
        s_exp = signal("s_exp", 8)
        s_turn, s_col = signal("s_turn", 4), signal("s_col", 4)
        s_av, s_avc = signal("s_av", 2), signal("s_avc", 1)
        s_ot, s_otc = signal("s_ot", 2), signal("s_otc")
        t_arg, t_exp, t_den, t_rden = signal("t_arg"), signal("t_exp"), signal("t_den"), signal("t_rden")
        t_v, t_sum, t_on = signal("t_v"), signal("t_sum"), signal("t_on", 2)
        b_on_turn, b_on_col, b_out, b_res = signal("b_on_turn"), signal("b_on_col"), signal("b_out"), signal("b_res")

        N_CONST = 2 + NPROD
        N_BATCH = 5 * NPROD + 1

        block = ctx.enter_context(nc.Block())

        @block.sync
        def _(sp):
            def load(dst, src, sig):
                sp.dma_start(dst, src).then_inc(sig.sem, 16)

            load(x[:], x_in.rearrange("(n p) d -> p n d", p=P), x_here)
            load(C[:], consts, consts_here)
            load(W[:], weights, weights_here)
            load(wv, spread_w, a_here)
            load(hsum, head_sums, a_here)
            load(idsb[:], token_ids, ids_here)
            load(crow[:], clear_row, clear_here)
            load(w12[:, NE, 0:INTER], w1s, ffn_here)
            load(w12[:, NE, INTER:], w2s, ffn_here)
            load(w3t[:, NE], w3s.rearrange("(k p) n -> p k n", p=P), ffn_here)
            load(w12[:, 0:NE, 0:INTER], w1.rearrange("e d n -> d e n"), ffn_here)
            load(w12[:, 0:NE, INTER:], w2.rearrange("e d n -> d e n"), ffn_here)
            for e in range(NE):
                load(w3t[:, e], w3[e].rearrange("(k p) n -> p k n", p=P), ffn_here)
            load(rowb[:, 0], rows[0:1, :].to_broadcast([P, D]), b_here)
            load(rowb[:, 1], rows[1:2, :].to_broadcast([P, D]), b_here)
            load(rpos[:, 0], positions, b_here)
            rows_v = slot_rows.rearrange("(s p) d -> s p d", p=P)

            def clear(f):
                sp.wait_ge(clear_here.sem, clear_here.moved(1))
                load(slot_rows.rearrange("(s p) d -> p s d", p=P),
                     crow[:].rearrange("p (a d) -> p a d", a=1).to_broadcast([P, SLOT_TILES, ROWW]), f_cleared[f])

            clear(0)

            def ffn(f):
                sp.wait_ge(f_sent[f].sem, f_sent[f].moved(NT))
                for s in range(4):
                    load(xr[:, s], rows_v[s], e_in[f][s])
                with nc.allow_non_contiguous_dma(reason="one number of every slot"):
                    load(slot_ids[:], slot_rows.rearrange("(s p) d -> p s d", p=P)[:, :, D].bitcast(U32), f_ids[f])
                with sp.Fori(1, SLOT_TILES // 4) as i:
                    for k in range(4):
                        sp.wait_ge(e_turn[f].sem, e_turn[f].spare(i * 4 + k, 4))
                        take_in(sp)
                        load(xr[:, k], rows_v[bass.ds(i * 4 + k, 1)].rearrange("a p d -> p (a d)"), e_in[f][k])
                sp.wait_ge(e_back[f].sem, e_back[f].moved(SLOT_TILES))
                load(yback, token_out.rearrange("(n p) d -> p n d", p=P), f_back[f])

            if last_phase >= 2:
                ffn(0)
            if last_phase >= 4:
                for k in range(4):
                    sp.wait_ge(e_in[0][k].sem, e_in[0][k].moved(SLOT_TILES // 4))
                sp.wait_ge(f_ids[0].sem, f_ids[0].moved(1))
                clear(1)
            if last_phase >= 3:
                sp.wait_ge(b_pos.sem, b_pos.item(3))
                load(pos_parts.rearrange("c d t -> d c t"), rpb[:], b_pos_out)
                with sp.Fori(0, NC // 2) as i:
                    for k in range(2):
                        sp.wait_ge(b_mid.sem, b_mid.item(i * 8 + (4 * k + 3)))
                        take_in(sp)
                        sp.wait_ge(b_low.sem, b_low.item(i * 6 + (3 * k + 2)))
                        take_in(sp)
                        sp.wait_ge(b_lowp.sem, b_lowp.item(i * 2 + k))
                        take_in(sp)
                        for t in range(4):
                            load(parts[t].rearrange("c d t -> d c t")[:, :, bass.ds(i * (2 * CH) + k * CH, CH)],
                                 pb[:, k, 3 * t:3 * t + 3], b_parts[k])
                sp.wait_ge(pad_set.sem, pad_set.item(0))
                load(parts[3].rearrange("c d t -> d c t")[:, :, TOK:TOK + P],
                     xT[:, TOK:TOK + P].bitcast(BF16)[:, 0:P].rearrange("p (a t) -> p a t", a=1).to_broadcast([P, 3, P]),
                     b_pos_out)
                for n in range(NT):
                    sp.wait_ge(b_tokv.sem, b_tokv.item(n))
                    load(v_rows[n * P:(n + 1) * P, :], vpad[:, n % 2].rearrange("p a b -> p (a b)"), b_vout[n % 2])
                for k in range(2):
                    sp.wait_ge(b_parts[k].sem, b_parts[k].moved(4 * (NC // 2)))
                    sp.wait_ge(b_vout[k].sem, b_vout[k].moved(NT // 2))
                sp.wait_ge(b_pos_out.sem, b_pos_out.moved(2))
                sp.wait_ge(b_tsum.sem, b_tsum.item(NT - 1))

                pieces = [(kst, 0, 1), (qup, 0, 0), (qup, 1, 3), (qlo, 0, 0), (qlo, 1, 2)]

                def load_batch(b, par):
                    for dst, half, t in pieces:
                        for j in range(NPROD):
                            part = K_PART[j] if t == 1 else Q_PART[j]
                            shift = 1 if t == 3 else 0
                            r0 = half * HALF + j * DH
                            load(dst[r0:r0 + DH, par],
                                 parts[t, part].rearrange("(h d) t -> d h t", d=DH)[:, :, bass.ds(b * SEQ + shift, SEQ)],
                                 b_stack[par])
                    load(vring[:, par], v_rows.rearrange("(n p) d -> p n d", p=P)[:, bass.ds(b * QT, QT), :], b_stack[par])

                for par in range(2):
                    load(qup[STK:STK + 1, par], row96[0:1].rearrange("a (h t) -> a h t", h=H), b_stack[par])
                    load(kst[STK:STK + 1, par], row96[1:2].rearrange("a (h t) -> a h t", h=H), b_stack[par])
                    for j in range(NPROD):
                        r0 = HALF + j * DH
                        load(kst[r0:r0 + DH, par],
                             pos_parts[K_PART[j]].rearrange("d (a t) -> d a t", a=1).to_broadcast([DH, H, SEQ]), b_stack[par])
                    load_batch(par, par)
                with sp.Fori(1, BATCH // 2) as i:
                    for par in range(2):
                        sp.wait_ge(s_scores.sem, s_scores.spare(i * BODY + ((par + 1) * UPB - 1), BODY))
                        take_in(sp)
                        sp.wait_ge(s_av.sem, s_av.spare(i * BODY + ((par + 1) * UPB - 1), BODY))
                        take_in(sp)
                        load_batch(i * 2 + par, par)
            if last_phase >= 4:
                ffn(1)
            sp.wait_ge(b_here.sem, b_here.moved(3))
            sp.wait_ge(ffn_here.sem, ffn_here.moved(5 + NE))
            final = {1: a_res, 2: f_done[0], 3: b_res, 4: f_done[1]}[last_phase]
            for c in range(NC):
                sp.wait_ge(final.sem, final.item(c))
                load(out.rearrange("(n p) d -> p n d", p=P)[:, 4 * c:4 * c + 4], x[:, 4 * c:4 * c + 4], out_stored)
            sp.wait_ge(out_stored.sem, out_stored.moved(NC))

        @block.tensor
        def _(pe):
            def turn_tiles(l, src, bank0=0):
                for n in range(NT):
                    pe.wait_ge(ln_rows[l].sem, ln_rows[l].item(n))
                    ins = nc.tensor.transpose(PS[:, bank0 + n // 4, (n % 4) * P:(n % 4 + 1) * P], src(n), ident)
                    if n % 4 == 3:
                        ins.then_inc(ln_turned[l].sem, 1)

            def stream_turn(l):
                turn_tiles(l, lambda n: xn[:, n, 0:D])

            pe.wait_ge(consts_here.sem, consts_here.moved(1))
            stream_turn(0)
            pe.wait_ge(weights_here.sem, weights_here.moved(1))
            with pe.Fori(0, NC) as c:
                pe.wait_ge(ln_cols[0].sem, ln_cols[0].item(c))
                for j, w in enumerate((W_Q, W_K, W_G)):
                    pe.wait_ge(a_raw.sem, a_raw.spare(c * 3 + j, 3))
                    nc.tensor.matmul(PS[:, 4 + j], W[:, w:w + P], xT[:, bass.ts(c, CH)],
                                     start=True, stop=True).then_inc(a_proj.sem, 1)
            pe.wait_ge(a_raw.sem, a_raw.item(3 * NC - 1))
            pe.wait_ge(a_here.sem, a_here.moved(2))

            def spread(c, e):
                pe.wait_ge(a_kv.sem, a_kv.spare(c * DH + e, 4))
                nc.tensor.matmul(PS[:, e % 4], wv[:, e * P:(e + 1) * P], xT[:, bass.ts(c, CH)],
                                 start=True, stop=True).then_inc(a_value.sem, 1)

            def summed(c, e):
                pe.wait_ge(a_read.sem, a_read.item(c * DH + e))
                if e == 0:
                    pe.wait_ge(a_y.sem, a_y.spare(c, 1))
                nc.tensor.matmul(PS[:, 4], hsum[:, e * P:(e + 1) * P], zb[:, e % 4],
                                 start=(e == 0), stop=(e == DH - 1)).then_inc(a_sum.sem, 1)

            for e in range(4):
                spread(0, e)
            with pe.Fori(0, NC - 1) as c:
                for e in range(DH):
                    spread(c if e < 4 else c + 1, (e + 4) % DH)
                    summed(c, e)
            for e in range(DH):
                if e < 4:
                    spread(NC - 1, e + 4)
                summed(NC - 1, e)
            pe.wait_ge(a_kv.sem, a_kv.item(NC * DH - 1))
            for n in range(NT):
                if n % 4 == 0:
                    pe.wait_ge(a_y.sem, a_y.item(n // 4))
                ins = nc.tensor.transpose(PS[:, n // 4, (n % 4) * P:(n % 4 + 1) * P], yT[:, n * P:(n + 1) * P], ident)
                if n % 4 == 3:
                    ins.then_inc(a_yrow.sem, 1)
            turn_tiles(4, lambda n: yn[:, n], bank0=4)
            for n in range(NT):
                if n % 4 == 0:
                    pe.wait_ge(ln_cols[4].sem, ln_cols[4].item(n // 4))
                ins = nc.tensor.matmul(PS[:, n // 4, (n % 4) * P:(n % 4 + 1) * P], ynT[:, n * P:(n + 1) * P],
                                       W[:, W_O:W_O + D], start=True, stop=True)
                if n % 4 == 3:
                    ins.then_inc(a_out.sem, 1)

            def ffn(f, l):
                stream_turn(l)
                for n in range(NT):
                    if n % 4 == 0:
                        pe.wait_ge(ln_cols[l].sem, ln_cols[l].item(n // 4))
                    ins = nc.tensor.matmul(PS[:, 6, n * NE:(n + 1) * NE], xT[:, n * P:(n + 1) * P],
                                           W[:, W_R:W_R + NE], start=True, stop=True)
                ins.then_inc(f_logits[f].sem, 1)
                pe.wait_ge(ffn_here.sem, ffn_here.moved(5 + NE))

                def shared_out(c, k):
                    pe.wait_ge(f_hid[f].sem, f_hid[f].item(c * KI + k))
                    if k == 0:
                        pe.wait_ge(f_res[f].sem, f_res[f].spare(c, 1))
                    for t in range(4):
                        ins = nc.tensor.matmul(PS[:, 4, t * P:(t + 1) * P], hT[:, k, t * P:(t + 1) * P],
                                               w3t[:, NE, k], start=(k == 0 and t == 0), stop=(k == KI - 1),
                                               skip_group_check=True)
                    ins.then_inc(f_out[f].sem, 1)

                def shared(c):
                    for k in range(KI):
                        pe.wait_ge(f_gelu[f].sem, f_gelu[f].spare(c * KI + k, 2))
                        nc.tensor.matmul(PS[:, k % 2], w12[:, NE, k * P:(k + 1) * P], xT[:, bass.ts(c, CH)],
                                         start=True, stop=True).then_inc(f_gate[f].sem, 1)
                        pe.wait_ge(f_hid[f].sem, f_hid[f].spare(c * KI + k, 2))
                        nc.tensor.matmul(PS[:, 2 + k % 2], w12[:, NE, INTER + k * P:INTER + (k + 1) * P],
                                         xT[:, bass.ts(c, CH)], start=True, stop=True).then_inc(f_up[f].sem, 1)
                        if k > 0:
                            shared_out(c, k - 1)
                    shared_out(c, KI - 1)

                shared(0)
                shared(1)
                pe.wait_ge(f_onehot[f].sem, f_onehot[f].item(0))
                pe.wait_ge(consts_cast.sem, consts_cast.item(3))
                nc.tensor.matmul(PS[:, 6, 0:NT * NE], cb[:, 2], one8b[:], start=True, stop=True)
                nc.tensor.matmul(PS[:, 7, 0:NT * NE], cb[:, 3], one8b[:], start=True,
                                 stop=True).then_inc(f_prefix[f].sem, 1)
                with pe.Fori(2, NC) as c:
                    shared(c)

                def turn_in(s, k):
                    wait_tile(s, k)
                    pe.wait_ge(e_col[f].sem, e_col[f].spare(s, 1))
                    nc.tensor.transpose(PS[:, 6, 0:P], xr[:, k, 0:D], ident).then_inc(e_turn[f].sem, 1)

                def wait_tile(s, k):
                    pe.wait_ge(e_in[f][k].sem, (s - k) * 4 + (16 + e_in[f][k].start))

                def gate(s, k, e):
                    pe.wait_ge(e_col[f].sem, e_col[f].item(s))
                    pe.wait_ge(e_gelu[f].sem, e_gelu[f].spare(s, 2))
                    nc.tensor.matmul(PS[:, k % 2], xrT[:, k], w12[:, e, 0:INTER],
                                     start=True, stop=True).then_inc(e_gate[f].sem, 1)

                def up(s, k, e):
                    pe.wait_ge(e_hid[f].sem, e_hid[f].spare(s, 2))
                    nc.tensor.matmul(PS[:, 2 + k % 2], xrT[:, k], w12[:, e, INTER:2 * INTER],
                                     start=True, stop=True).then_inc(e_up[f].sem, 1)

                def turn_hidden(s, k):
                    pe.wait_ge(e_hid[f].sem, e_hid[f].item(s))
                    pe.wait_ge(e_hcol[f].sem, e_hcol[f].spare(s, 2))
                    for j in range(KI):
                        ins = nc.tensor.transpose(PS[:, 4 + k % 2, j * P:(j + 1) * P], eh[:, k % 2, j * P:(j + 1) * P], ident)
                    ins.then_inc(e_hturn[f].sem, 1)

                def down(s, k, e):
                    pe.wait_ge(e_hcol[f].sem, e_hcol[f].item(s))
                    pe.wait_ge(e_row[f].sem, e_row[f].spare(s, 1))
                    for j in range(KI):
                        ins = nc.tensor.matmul(PS[:, 7, 0:P], ehT[:, k % 2, j * P:(j + 1) * P],
                                               w3t[:, e, j], start=(j == 0), stop=(j == KI - 1))
                    ins.then_inc(e_out[f].sem, 1)

                def expert_of(word, j):
                    return (word // NE ** j) % NE

                def step(i, k, word, j0, s_min=None):
                    s = i * 4 + k
                    free_run = s_min is None
                    if free_run or s_min + 1 < SLOT_TILES:
                        turn_in(s + 1, (k + 1) % 4)
                    enters = free_run or s_min < SLOT_TILES
                    if enters:
                        gate(s, k % 4, expert_of(word, k - j0))
                    if free_run or s_min >= 2:
                        down(s - 2, (k - 2) % 4, expert_of(word, k - 2 - j0))
                    if enters:
                        up(s, k % 4, expert_of(word, k - j0))
                    if free_run or 1 <= s_min < SLOT_TILES + 1:
                        turn_hidden(s - 1, (k - 1) % 4)

                def load_word(s):
                    return pe.value_load(eword[0:1, bass.ds(s, 1)], min_val=0, max_val=NE ** 6 - 1)

                pe.wait_ge(f_experts[f].sem, f_experts[f].item(0))
                pe.wait_ge(f_res[f].sem, f_res[f].item(NC - 1))
                pe.wait_ge(f_slots[f].sem, f_slots[f].item(0))
                word = load_word(0)
                turn_in(0, 0)
                for s in range(2):
                    step(0, s, word, 0, s)
                with pe.Fori(0, SLOT_TILES // 4 - 1) as i:
                    word = load_word(i * 4)
                    for k in range(2, 6):
                        step(i, k, word, 0)
                word = load_word(SLOT_TILES - 4)
                for s in range(SLOT_TILES - 2, SLOT_TILES + 2):
                    step(0, s, word, SLOT_TILES - 4, s)

            if last_phase >= 2:
                ffn(0, 1)

            def attention():
                stream_turn(2)
                pe.wait_ge(ln_cols[2].sem, ln_cols[2].item(NC - 1))
                with pe.Fori(0, NC) as c:
                    for j, w in enumerate((W_BQ, W_BS, W_BK)):
                        pe.wait_ge(b_raw.sem, b_raw.spare(c * 3 + j, 3))
                        nc.tensor.matmul(PS[:, 4 + j], W[:, w:w + P], xT[:, bass.ts(c, CH)],
                                         start=True, stop=True).then_inc(b_proj.sem, 1)
                pe.wait_ge(pad_set.sem, pad_set.item(0))
                for n in range(NT):
                    b = 2 * (n % 2)
                    pe.wait_ge(b_tokd.sem, b_tokd.spare(n, 2))
                    pe.wait_ge(b_tokv.sem, b_tokv.spare(n, 2))
                    for bank, place, ahead, w in ((b, 0, 0, W_BQ), (b, D, 1, W_BK), (b + 1, 0, 0, W_BV), (b + 1, D, 1, W_BV)):
                        ins = nc.tensor.matmul(PS[:, bank, place:place + D], xT[:, n * P + ahead:(n + 1) * P + ahead],
                                               W[:, w:w + D], start=True, stop=True)
                    ins.then_inc(b_tok.sem, 1)
                pe.wait_ge(b_tokd.sem, b_tokd.item(NT - 1))
                pe.wait_ge(b_tokv.sem, b_tokv.item(NT - 1))
                pe.wait_ge(b_raw.sem, b_raw.item(3 * NC - 1))

                def scores(i, k, tile_out):
                    u = i * BODY + k
                    k = k % BODY
                    par, qt, hg = k // UPB, (k // HG) % QT, k % HG
                    if k % UPB == 0:
                        pe.wait_ge(b_stack[par].sem, i * (16 * N_BATCH) + 16 * (N_CONST + N_BATCH))
                    pe.wait_ge(s_exp.sem, s_exp.spare(u * HG + (HG - 1), 2 * HG))
                    main = PS[:, 2 * (k % 2):2 * (k % 2) + 2].rearrange("p a (b j) -> p (a b) j", b=2)
                    q = slice(qt * P, (qt + 1) * P)
                    for a in range(HG):
                        h = HG * hg + a
                        if qt == 0:
                            nc.tensor.matmul(main[:, a], qup[0:STK + 1, par, h, q], kst[0:STK + 1, par, h],
                                             start=(a % 2 == 0), stop=False, skip_group_check=True)
                            nc.tensor.matmul(main[:, a, 0:P], cb[:, 0], cb[:, 1],
                                             start=False, stop=True, skip_group_check=True)
                        else:
                            nc.tensor.matmul(main[:, a], qlo[0:STK, par, h, q], kst[0:STK, par, h],
                                             start=(a % 2 == 0), stop=True, skip_group_check=True)
                    pe.wait_ge(s_pick.sem, s_pick.spare(u, 1))
                    if tile_out is not None:
                        pe.wait_ge(s_otc.sem, s_otc.item(tile_out))
                    for a in range(HG):
                        h = HG * hg + a
                        other = PS[:, 4, a * P:(a + 1) * P]
                        if qt == 0:
                            ins = nc.tensor.matmul(other, qlo[0:STK, par, h, q], kst[0:STK, par, h, q],
                                                   start=(a == 0), stop=True, skip_group_check=True)
                        else:
                            nc.tensor.matmul(other, qup[0:STK + 1, par, h, q], kst[0:STK + 1, par, h, q],
                                             start=(a == 0), stop=False, skip_group_check=True)
                            ins = nc.tensor.matmul(other, cb[:, 0], cb[:, 1], start=False, stop=True,
                                                   skip_group_check=True)
                    ins.then_inc(s_scores.sem, 1)

                def turn(u, k):
                    k = k % BODY
                    for a in range(HG):
                        pe.wait_ge(s_exp.sem, s_exp.item(u * HG + a))
                        if a % 2 == 0:
                            pe.wait_ge(s_col.sem, s_col.spare(u * 2 + a // 2, 2))
                        for j in range(QT):
                            ins = nc.tensor.transpose(PS[:, 5 + a // 2, ((a % 2) * QT + j) * P:((a % 2) * QT + j + 1) * P],
                                                      pr[:, k % 2, a, j * P:(j + 1) * P], ident)
                        if a % 2 == 1:
                            ins.then_inc(s_turn.sem, 1)

                def weigh(u, k):
                    k = k % BODY
                    par, hg = k // UPB, k % HG
                    pe.wait_ge(s_col.sem, s_col.item(u * 2 + 1))
                    pe.wait_ge(s_avc.sem, s_avc.spare(u, 1))
                    for j in range(QT):
                        for a in range(HG):
                            h = HG * hg + a
                            ins = nc.tensor.matmul(PS[VW * a:VW * (a + 1), 7, 0:P],
                                                   vring[:, par, j, h * VW:(h + 1) * VW],
                                                   prT[:, k % 2, a, j * P:(j + 1) * P],
                                                   start=(j == 0), stop=(j == QT - 1), tile_position=(0, VW * a),
                                                   skip_group_check=True)
                    ins.then_inc(s_av.sem, 1)

                def turn_out(i, k, u_min):
                    tile = i * (BODY // HG) + (k - 6) // HG
                    pe.wait_ge(s_avc.sem, s_avc.item(i * BODY + (k - 3)))
                    pe.wait_ge(s_pick.sem, s_pick.item(i * BODY + (k - 1) if u_min is None else min(u_min, UNITS) - 1))
                    for a in range(HG):
                        ins = nc.tensor.transpose(PS[:, 4, a * P:(a + 1) * P], osb[:, (k - 6 + a) % (2 * HG)], ident)
                    ins.then_inc(s_ot.sem, 1)

                def step(i, k, u_min=None):
                    u = i * BODY + k
                    free_run = u_min is None
                    if k % HG == 2 and (free_run or u_min >= 6):
                        turn_out(i, k, u_min)
                    if free_run or u_min < UNITS:
                        tile_out = None
                        if k % HG == 2 and (free_run or u_min >= 6):
                            tile_out = i * (BODY // HG) + (k - 6) // HG
                        if k >= BODY:
                            scores(i + 1, k - BODY, tile_out)
                        else:
                            scores(i, k, tile_out)
                    if free_run or 1 <= u_min < UNITS + 1:
                        turn(u - 1, k - 1)
                    if free_run or 2 <= u_min < UNITS + 2:
                        weigh(u - 2, k - 2)

                for k in range(3):
                    step(0, k, k)
                with pe.Fori(0, UNITS // BODY - 1) as i:
                    for k in range(3, BODY + 3):
                        step(i, k)
                last = UNITS // BODY - 1
                for k in range(3, BODY + 3):
                    step(last, k, last * BODY + k)

                for n in range(NT):
                    if n % 4 == 0:
                        pe.wait_ge(t_on.sem, t_on.item(n + 3))
                    ins = nc.tensor.transpose(PS[:, n // 4, (n % 4) * P:(n % 4 + 1) * P], on[:, n], ident)
                    if n % 4 == 3:
                        ins.then_inc(b_on_turn.sem, 1)
                for n in range(NT):
                    if n % 4 == 0:
                        pe.wait_ge(b_on_col.sem, b_on_col.item(n // 4))
                    ins = nc.tensor.matmul(PS[:, 4 + n // 4, (n % 4) * P:(n % 4 + 1) * P], onT[:, n * P:(n + 1) * P],
                                           W[:, W_BO:W_BO + D], start=True, stop=True)
                    if n % 4 == 3:
                        ins.then_inc(b_out.sem, 1)

            if last_phase >= 3:
                attention()
            if last_phase >= 4:
                ffn(1, 3)

        @block.vector
        def _(dve):
            for sig in [a_kv, a_state, s_pick, b_low, b_tokd, t_on] + \
                    [s[0] for s in (f_res, e_col, e_hid, e_row, f_hid)]:
                dve.sem_inc(sig.sem, sig.start)

            def step():
                steps[0] += 1
                return 1

            nc.vector.memset(xT[:, TOK:TOK + P], 0.0).then_inc(pad_set.sem, 1)

            def spread_stats(l):
                dve.wait_ge(dve_order.sem, steps[0])
                me, mo, qe, qo = [stats[:, :, j] for j in (1, 4, 2, 5)]
                nc.vector.tensor_tensor(small[:, 0], me, mo, ALU.add).then_inc(dve_order.sem, step())
                nc.vector.tensor_tensor(small[:, 1], me, mo, ALU.subtract).then_inc(dve_order.sem, step())
                nc.vector.tensor_tensor(small[:, 2], qe, qo, ALU.add).then_inc(dve_order.sem, step())
                dve.wait_ge(dve_order.sem, steps[0])
                nc.vector.tensor_scalar(small[:, 3], small[:, 0], 0.5, None, ALU.mult).then_inc(dve_order.sem, step())
                nc.vector.scalar_tensor_tensor(out=small[:, 4], in0=small[:, 1], scalar=0.25, in1=small[:, 1],
                                               op0=ALU.mult, op1=ALU.mult).then_inc(dve_order.sem, step())
                nc.vector.tensor_scalar(small[:, 5], small[:, 2], 1.0 / D, EPS, ALU.mult, ALU.add)\
                    .then_inc(dve_order.sem, step())
                dve.wait_ge(dve_order.sem, steps[0])
                nc.vector.tensor_tensor(small[:, 6], small[:, 4], small[:, 5], ALU.add).then_inc(ln_var[l].sem, 1)
                dve.wait_ge(ln_std[l].sem, ln_std[l].item(0))
                nc.vector.reciprocal(small[:, 7], small[:, 0]).then_inc(dve_order.sem, step())
                dve.wait_ge(dve_order.sem, steps[0])

            def norm(l, src, dst):
                for n in range(NT):
                    nc.vector.tensor_scalar(dst(n), src(n), small[:, 3, n:n + 1], small[:, 7, n:n + 1],
                                            ALU.subtract, ALU.mult).then_inc(ln_rows[l].sem, 1)

            def stream_norm(l):
                dve.wait_ge(dve_order.sem, steps[0])
                for n in range(NT):
                    nc.vector.bn_stats(stats[:, n], x[:, n]).then_inc(dve_order.sem, step())
                spread_stats(l)
                norm(l, lambda n: x[:, n], lambda n: xn[:, n, 0:D])

            dve.wait_ge(x_here.sem, x_here.moved(1))
            stream_norm(0)
            dve.wait_ge(ids_here.sem, ids_here.moved(1))
            nc.vector.tensor_copy(xn[:, :, D].bitcast(I32), idsb[:]).then_inc(ids_set.sem, 1)
            dve.wait_ge(consts_here.sem, consts_here.moved(1))
            for j, col in enumerate((C_ID, C_SD, C_TRI, C_ONE)):
                nc.vector.tensor_copy(cb[:, j], C[:, col:col + P]).then_inc(consts_cast.sem, 1)

            tri = C[:, C_TRI:C_TRI + P].rearrange("p (a k) -> p a k", a=1).to_broadcast([P, HG, P])
            nc.vector.tensor_scalar(msk[:, 0], tri, 0.0, None, ALU.is_equal).then_inc(dve_order.sem, step())
            nc.vector.tensor_scalar(msk[:, 1], tri, 0.0, None, ALU.is_gt).then_inc(dve_order.sem, step())

            dve.wait_ge(a_raw.sem, a_raw.item(3 * NC - 1))
            with dve.Fori(0, NC) as c:
                def product(e):
                    n = c * DH + e
                    dve.wait_ge(a_value.sem, a_value.item(n))
                    dve.wait_ge(a_state.sem, a_state.spare(n * 2 + 1, 4))
                    nc.vector.tensor_tensor(kvb[:, e % 2], kT[:, bass.ts(c, CH)], PS[:, e % 4], ALU.mult)\
                        .then_inc(a_kv.sem, 1)

                def state(e):
                    n = c * DH + e
                    dve.wait_ge(a_kv.sem, a_kv.item(n))
                    dve.wait_ge(a_read.sem, a_read.spare(n, 4))
                    for j in range(SPC):
                        nc.vector.tensor_tensor_scan(
                            hb[:, e % 4, j * SEQ:(j + 1) * SEQ], aT[:, bass.ds(c * CH + j * SEQ, SEQ)],
                            kvb[:, e % 2, j * SEQ:(j + 1) * SEQ], 0.0, ALU.mult, ALU.add).then_inc(a_state.sem, 1)

                product(0)
                for e in range(DH):
                    if e + 1 < DH:
                        product(e + 1)
                    state(e)
            for n in range(NT):
                if n % 4 == 0:
                    dve.wait_ge(a_yrow.sem, a_yrow.item(n // 4))
                nc.vector.bn_stats(stats[:, n], PS[:, n // 4, (n % 4) * P:(n % 4 + 1) * P])\
                    .then_inc(dve_order.sem, step())
            spread_stats(4)
            norm(4, lambda n: PS[:, n // 4, (n % 4) * P:(n % 4 + 1) * P], lambda n: yn[:, n])

            def add_banks(sig, done, bank0):
                for c in range(NC):
                    dve.wait_ge(sig.sem, sig.item(c))
                    part = x[:, 4 * c:4 * c + 4].rearrange("p a b -> p (a b)")
                    nc.vector.tensor_tensor(part, part, PS[:, bank0 + c], ALU.add).then_inc(done.sem, 1)
                dve.wait_ge(done.sem, done.item(NC - 1))

            add_banks(a_out, a_res, 0)

            def ffn(f, l):
                stream_norm(l)

                def hidden(c):
                    for k in range(KI):
                        n = c * KI + k
                        dve.wait_ge(f_gelu[f].sem, f_gelu[f].item(n))
                        dve.wait_ge(f_up[f].sem, f_up[f].item(n))
                        dve.wait_ge(f_out[f].sem, f_out[f].spare(n, 4))
                        nc.vector.tensor_tensor(hT[:, k], gk[:, k % 2], PS[:, 2 + k % 2], ALU.mult)\
                            .then_inc(f_hid[f].sem, 1)
                    dve.wait_ge(f_out[f].sem, f_out[f].item(c * KI + KI - 1))
                    part = x[:, bass.ds(c * 4, 4)].rearrange("p a b -> p (a b)")
                    nc.vector.tensor_tensor(part, part, PS[:, 4], ALU.add).then_inc(f_res[f].sem, 1)

                hidden(0)
                dve.wait_ge(f_logits[f].sem, f_logits[f].item(0))
                for n in range(NT):
                    nc.vector.max(mx8[:, n], PS[:, 6, n * NE:(n + 1) * NE]).then_inc(dve_order.sem, step())
                dve.wait_ge(dve_order.sem, steps[0])
                for n in range(NT):
                    nc.vector.max_index(ix8[:, n], mx8[:, n], PS[:, 6, n * NE:(n + 1) * NE])\
                        .then_inc(dve_order.sem, step())
                dve.wait_ge(dve_order.sem, steps[0])
                nc.vector.tensor_copy(ixf, ix8[:, :, 0]).then_inc(dve_order.sem, step())
                dve.wait_ge(dve_order.sem, steps[0])
                iota = C[:, C_IOTA:C_IOTA + NE].rearrange("p (a e) -> p a e", a=1).to_broadcast([P, NT, NE])
                nc.vector.tensor_tensor(one8, iota, ixf.rearrange("p (n a) -> p n a", a=1).to_broadcast([P, NT, NE]),
                                        ALU.is_equal).then_inc(dve_order.sem, step())
                dve.wait_ge(dve_order.sem, steps[0])
                nc.vector.tensor_copy(one8b[:], one8.rearrange("p a b -> p (a b)")).then_inc(f_onehot[f].sem, 1)
                hidden(1)
                dve.wait_ge(f_prefix[f].sem, f_prefix[f].item(0))
                nc.vector.tensor_copy(tot, PS[:, 7, 0:NT * NE].rearrange("p (n e) -> p e n", e=NE))\
                    .then_inc(dve_order.sem, step())
                dve.wait_ge(dve_order.sem, steps[0])
                nc.vector.tensor_tensor_scan(csum.rearrange("p a b -> p (a b)"), C[:, C_ONE:C_ONE + NE * NT],
                                             tot.rearrange("p a b -> p (a b)"), 0.0, ALU.mult, ALU.add)\
                                                 .then_inc(dve_order.sem, step())
                nc.vector.tensor_reduce(cnt8[:, 0], tot, AX_X, ALU.add).then_inc(dve_order.sem, step())
                dve.wait_ge(dve_order.sem, steps[0])
                thr = C[:, C_THR:C_THR + NE * NT].rearrange("p (a b) -> p a b", a=NE)
                nc.vector.tensor_tensor(cmp8, cnt8[:, 0].rearrange("p (e a) -> p e a", a=1).to_broadcast([P, NE, NT]),
                                        thr, ALU.is_gt).then_inc(dve_order.sem, step())
                nc.vector.tensor_tensor(base, csum, tot, ALU.subtract).then_inc(dve_order.sem, step())
                dve.wait_ge(dve_order.sem, steps[0])
                nc.vector.tensor_reduce(cnt8[:, 1], cmp8, AX_X, ALU.add).then_inc(dve_order.sem, step())
                dve.wait_ge(dve_order.sem, steps[0])
                nc.vector.tensor_tensor_scan(cnt8[:, 2], C[:, C_ONE:C_ONE + NE], cnt8[:, 1], 0.0,
                                             ALU.mult, ALU.add).then_inc(dve_order.sem, step())
                dve.wait_ge(dve_order.sem, steps[0])
                nc.vector.tensor_tensor(cnt8[:, 3], cnt8[:, 2], cnt8[:, 1], ALU.subtract)\
                    .then_inc(dve_order.sem, step())
                slot_no = C[:, C_SLOT:C_SLOT + SLOT_TILES * NE].rearrange("p (s e) -> p s e", e=NE)
                nc.vector.tensor_tensor(ecmp, slot_no,
                                        cnt8[:, 2].rearrange("p (a e) -> p a e", a=1).to_broadcast([P, SLOT_TILES, NE]),
                                        ALU.is_ge).then_inc(dve_order.sem, step())
                dve.wait_ge(dve_order.sem, steps[0])
                nc.vector.scalar_tensor_tensor(out=cnt8[:, 4], in0=cnt8[:, 3], scalar=float(P), in1=base[:, :, 0],
                                               op0=ALU.mult, op1=ALU.subtract).then_inc(dve_order.sem, step())
                nc.vector.tensor_reduce(eidf[:, 0], ecmp, AX_X, ALU.add).then_inc(dve_order.sem, step())
                dve.wait_ge(dve_order.sem, steps[0])
                nc.vector.tensor_tensor(cmp8, base, cnt8[:, 4].rearrange("p (e a) -> p e a", a=1).to_broadcast([P, NE, NT]),
                                        ALU.add).then_inc(dve_order.sem, step())
                nc.vector.tensor_scalar(eidf[:, 0], eidf[:, 0], float(NE - 1), None, ALU.min)\
                    .then_inc(dve_order.sem, step())
                dve.wait_ge(dve_order.sem, steps[0])
                nc.vector.tensor_tensor(work, PS[:, 6, 0:NT * NE].rearrange("p (n e) -> p n e", e=NE),
                                        cmp8.rearrange("p e n -> p n e"), ALU.add).then_inc(dve_order.sem, step())
                nc.vector.tensor_copy(eidf[:, 1], eidf[:, 0]).then_inc(dve_order.sem, step())
                dve.wait_ge(dve_order.sem, steps[0])
                nc.vector.tensor_tensor(work, work, one8, ALU.mult).then_inc(dve_order.sem, step())
                for j in range(1, 6):
                    n = SLOT_TILES - j
                    dve.wait_ge(dve_order.sem, steps[0])
                    nc.vector.scalar_tensor_tensor(out=eidf[:, 1, 0:n], in0=eidf[:, 0, j:], scalar=float(NE ** j),
                                                   in1=eidf[:, 1, 0:n], op0=ALU.mult, op1=ALU.add)\
                                                       .then_inc(dve_order.sem, step())
                    if j == 1:
                        nc.vector.tensor_reduce(slotf, work, AX_X, ALU.add).then_inc(dve_order.sem, step())
                    if j == 2:
                        nc.vector.tensor_copy(slotu[:], slotf).then_inc(f_slots[f].sem, 1)
                dve.wait_ge(dve_order.sem, steps[0])
                nc.vector.tensor_copy(eword[:], eidf[:, 1]).then_inc(f_experts[f].sem, 1)
                with dve.Fori(2, NC) as c:
                    hidden(c)

                def columns(s, k):
                    dve.wait_ge(e_turn[f].sem, e_turn[f].item(s))
                    dve.wait_ge(e_up[f].sem, e_up[f].spare(s, 4))
                    nc.vector.tensor_copy(xrT[:, k], PS[:, 6, 0:P]).then_inc(e_col[f].sem, 1)

                def out_rows(s):
                    dve.wait_ge(e_out[f].sem, e_out[f].item(s))
                    nc.vector.tensor_copy(er[:, bass.ds(s, 1)].rearrange("p a d -> p (a d)"), PS[:, 7, 0:P])\
                        .then_inc(e_row[f].sem, 1)

                def product(s, k):
                    dve.wait_ge(e_gelu[f].sem, e_gelu[f].item(s))
                    dve.wait_ge(e_up[f].sem, e_up[f].item(s))
                    dve.wait_ge(e_hturn[f].sem, e_hturn[f].spare(s, 2))
                    nc.vector.tensor_tensor(eh[:, k % 2], eg[:, k % 2], PS[:, 2 + k % 2], ALU.mult)\
                        .then_inc(e_hid[f].sem, 1)

                def expert_step(i, k, s_min=None):
                    s = i * 4 + k
                    if s_min is None or s_min + 1 < SLOT_TILES:
                        columns(s + 1, (k + 1) % 4)
                    if s_min is None or s_min >= 2:
                        out_rows(s - 2)
                    if s_min is None or s_min < SLOT_TILES:
                        product(s, k % 4)

                columns(0, 0)
                for s in range(2):
                    expert_step(0, s, s)
                with dve.Fori(0, SLOT_TILES // 4 - 1) as i:
                    for k in range(2, 6):
                        expert_step(i, k)
                for s in range(SLOT_TILES - 2, SLOT_TILES + 2):
                    expert_step(0, s, s)
                dve.wait_ge(f_res[f].sem, f_res[f].item(NC - 1))
                dve.wait_ge(f_back[f].sem, f_back[f].moved(1))
                for c in range(NC):
                    part = x[:, 4 * c:4 * c + 4]
                    nc.vector.tensor_tensor(part, part, yback[:, 4 * c:4 * c + 4], ALU.add).then_inc(f_done[f].sem, 1)
                dve.wait_ge(f_done[f].sem, f_done[f].item(NC - 1))

            if last_phase >= 2:
                ffn(0, 1)

            def attention():
                dve.wait_ge(b_here.sem, b_here.moved(3))
                stream_norm(2)
                dve.wait_ge(ln_rows[2].sem, ln_rows[2].item(NT - 1))
                nc.vector.tensor_tensor(x[:], x[:], rowb[:, 1].rearrange("p (a d) -> p a d", a=1).to_broadcast([P, NT, D]),
                                        ALU.add).then_inc(dve_order.sem, step())
                nc.vector.tensor_copy(rpb[:, 0], rpos[:, 0]).then_inc(b_pos.sem, 1)
                dve.wait_ge(b_pos.sem, b_pos.item(0))
                nc.vector.tensor_tensor(rpos[:, 1], rpos[:, 0], rpb[:, 0], ALU.subtract).then_inc(b_pos.sem, 1)
                dve.wait_ge(b_pos.sem, b_pos.item(1))
                nc.vector.tensor_copy(rpb[:, 1], rpos[:, 1]).then_inc(b_pos.sem, 1)
                dve.wait_ge(b_pos.sem, b_pos.item(2))
                nc.vector.tensor_tensor(rpb[:, 2], rpos[:, 1], rpb[:, 1], ALU.subtract).then_inc(b_pos.sem, 1)

                def by_seq(ap):
                    return ap.rearrange("p (b t) -> p b t", t=SEQ)

                def table(col):
                    return C[:, col:col + SEQ].rearrange("p (a t) -> p a t", a=1).to_broadcast([P, SPC, SEQ])

                with dve.Fori(0, NC // 2) as i:
                    for k in range(2):
                        dve.wait_ge(b_raw.sem, b_raw.item(i * 6 + (3 * k + 1)))
                        dve.wait_ge(b_low.sem, b_low.spare(i * 6 + (3 * k + 2), 6))
                        nc.vector.tensor_tensor(by_seq(rot[:, k, 0]), by_seq(raw[:, k, 1]), table(C_COS1), ALU.mult)\
                            .then_inc(b_rot.sem, 1)
                        nc.vector.tensor_tensor(by_seq(rot[:, k, 1]), by_seq(raw[:, k, 2]), table(C_SIN1), ALU.mult)\
                            .then_inc(b_rot.sem, 1)
                        dve.wait_ge(b_rot.sem, b_rot.item(i * 6 + (3 * k + 1)))
                        nc.vector.tensor_tensor(rot[:, k, 0], rot[:, k, 0], rot[:, k, 1], ALU.add)\
                            .then_inc(b_rot.sem, 1)
                        srcs = (raw[:, k, 0], raw[:, k, 3], rot[:, k, 0])
                        dve.wait_ge(b_rot.sem, b_rot.item(i * 6 + (3 * k + 2)))
                        for t, src in enumerate(srcs):
                            dve.wait_ge(b_hi.sem, b_hi.item(i * 8 + (4 * k + t)))
                            nc.vector.tensor_tensor(rest[:, k, t], src, pb[:, k, 3 * t], ALU.subtract)\
                                .then_inc(b_rest.sem, 1)
                        for t in range(3):
                            dve.wait_ge(b_mid.sem, b_mid.item(i * 8 + (4 * k + t)))
                            dve.wait_ge(b_rest.sem, b_rest.item(i * 6 + (3 * k + t)))
                            nc.vector.tensor_tensor(pb[:, k, 3 * t + 2], rest[:, k, t], pb[:, k, 3 * t + 1], ALU.subtract)\
                                .then_inc(b_low.sem, 1)
                u_row = rowb[:, 0]
                for n in range(NT):
                    b = 2 * (n % 2)
                    dve.wait_ge(b_tok.sem, b_tok.item(n))
                    if n >= 2:
                        dve.wait_ge(b_tsum.sem, b_tsum.item(n - 2))
                    nc.vector.tensor_tensor(tq[:, n % 2, 0], PS[:, b, 0:D], u_row, ALU.add)\
                        .then_inc(dve_order.sem, step())
                    dve.wait_ge(dve_order.sem, steps[0])
                    nc.vector.tensor_tensor(tq[:, n % 2, 1], tq[:, n % 2, 0], PS[:, b, D:2 * D], ALU.mult)\
                        .then_inc(b_tokd.sem, 1)
                    dve.wait_ge(b_tokd.sem, b_tokd.item(n))
                    nc.vector.tensor_reduce(nsd[:, n], tq[:, n % 2, 1].rearrange("p (h d) -> p h d", h=H), AX_X, ALU.add)\
                        .then_inc(b_tsum.sem, 1)
                dve.wait_ge(b_tsum.sem, b_tsum.item(NT - 1))
                last_q = C[:, C_LAST:C_LAST + NT].rearrange("p (n a) -> p n a", a=1).to_broadcast([P, NT, H])
                nc.vector.tensor_tensor(nsd[:], nsd[:], last_q, ALU.add).then_inc(dve_order.sem, step())
                dve.wait_ge(dve_order.sem, steps[0])
                nc.vector.tensor_scalar(nsd[:], nsd[:], -SCALE, None, ALU.mult).then_inc(dve_order.sem, step())
                dve.wait_ge(dve_order.sem, steps[0])

                def pick_and_max(i, k):
                    u = i * BODY + k
                    kk = k % BODY
                    qt, hg = (kk // HG) % QT, kk % HG
                    tile = (i if k < BODY else i + 1) * (BODY // HG) + kk // HG
                    main = PS[:, 2 * (k % 2):2 * (k % 2) + 2].rearrange("p a (b j) -> p (a b) j", b=2)
                    dve.wait_ge(s_scores.sem, s_scores.item(u))
                    take_in(dve)
                    nc.vector.copy_predicated(main[:, :, qt * P:(qt + 1) * P], msk[:, qt],
                                              PS[:, 4].rearrange("p (a j) -> p a j", a=HG)).then_inc(s_pick.sem, 1)
                    dve.wait_ge(s_pick.sem, s_pick.item(u))
                    nc.vector.tensor_reduce(mxs[:, k % 2], main, AX_X, ALU.max).then_inc(s_max.sem, 1)
                    dve.wait_ge(s_max.sem, s_max.item(u))
                    if hg == 0:
                        dve.wait_ge(t_on.sem, t_on.spare(tile, 2))
                    nc.vector.scalar_tensor_tensor(
                        out=nmax[:, (k // HG) % 2, hg * HG:(hg + 1) * HG], in0=mxs[:, k % 2], scalar=-SCALE,
                        in1=nsd[:, bass.ds(tile, 1), hg * HG:(hg + 1) * HG].rearrange("p a h -> p (a h)"),
                        op0=ALU.mult, op1=ALU.min).then_inc(s_nmax.sem, 1)

                def finish_tile(i, k):
                    kk = k % BODY
                    par = (kk // HG) % 2
                    tile = i * (BODY // HG) + kk // HG
                    one = bass.ds(tile, 1)
                    dve.wait_ge(s_otc.sem, s_otc.item(tile))
                    dve.wait_ge(t_exp.sem, t_exp.item(tile))
                    e_next, den, rden = esm[:, par, 1], esm[:, par, 2], esm[:, par, 3]
                    nc.vector.tensor_tensor(den, otok[:, par, :, 8], e_next, ALU.add).then_inc(t_den.sem, 1)
                    wide = e_next.rearrange("p (h a) -> p h a", a=1).to_broadcast([P, H, DH])
                    nc.vector.tensor_tensor(t4[:, par * 2].rearrange("p (h d) -> p h d", h=H),
                                            vnext[:, one].rearrange("p a (h d) -> p (a h) d", h=H), wide, ALU.mult)\
                        .then_inc(t_v.sem, 1)
                    dve.wait_ge(t_den.sem, t_den.item(tile))
                    nc.vector.reciprocal(rden, den).then_inc(t_rden.sem, 1)
                    dve.wait_ge(t_v.sem, t_v.item(tile))
                    nc.vector.tensor_tensor(t4[:, par * 2 + 1].rearrange("p (h d) -> p h d", h=H),
                                            t4[:, par * 2].rearrange("p (h d) -> p h d", h=H),
                                            otok[:, par, :, 0:DH], ALU.add).then_inc(t_sum.sem, 1)
                    dve.wait_ge(t_rden.sem, t_rden.item(tile))
                    dve.wait_ge(t_sum.sem, t_sum.item(tile))
                    nc.vector.tensor_tensor(on[:, one].rearrange("p a (h d) -> p (a h) d", h=H),
                                            t4[:, par * 2 + 1].rearrange("p (h d) -> p h d", h=H),
                                            rden.rearrange("p (h a) -> p h a", a=1).to_broadcast([P, H, DH]), ALU.mult)\
                        .then_inc(t_on.sem, 1)

                def output_rows(i, k):
                    tile = i * (BODY // HG) + (k - 6) // HG
                    dve.wait_ge(s_ot.sem, s_ot.item(tile))
                    dve.wait_ge(t_on.sem, t_on.spare(tile, 2))
                    nc.vector.tensor_copy(otok[:, ((k - 6) // HG) % 2],
                                          PS[:, 4].rearrange("p (h w) -> p h w", w=VW)[:, :, 0:DH + 1])\
                                              .then_inc(s_otc.sem, 1)

                def tile_arg(i, k):
                    kk = k % BODY
                    par = (kk // HG) % 2
                    tile = i * (BODY // HG) + kk // HG
                    dve.wait_ge(s_nmax.sem, s_nmax.item(i * BODY + kk))
                    dve.wait_ge(t_on.sem, t_on.spare(tile, 2))
                    nc.vector.tensor_tensor(esm[:, par, 0], nmax[:, par],
                                            nsd[:, bass.ds(tile, 1)].rearrange("p a h -> p (a h)"), ALU.subtract)\
                        .then_inc(t_arg.sem, 1)

                LAG = 4

                def dve_unit(i, k, u_min=None):
                    if k % HG == 2 and (u_min is None or u_min >= 6):
                        output_rows(i, k)
                    if u_min is None or u_min < UNITS:
                        pick_and_max(i, k)
                        if k % HG == HG - 1:
                            tile_arg(i, k) if k < BODY else tile_arg(i + 1, k - BODY)
                    done = k - LAG
                    if done % HG == HG - 1 and (u_min is None or u_min >= LAG):
                        finish_tile(i, done)

                for k in range(LAG):
                    dve_unit(0, k, k)
                with dve.Fori(0, UNITS // BODY - 1) as i:
                    for k in range(LAG, BODY + LAG):
                        dve_unit(i, k)
                last = UNITS // BODY - 1
                for k in range(LAG, BODY + LAG):
                    dve_unit(last, k, last * BODY + k)
                add_banks(b_out, b_res, 4)

            if last_phase >= 3:
                attention()
            if last_phase >= 4:
                ffn(1, 3)

        @block.scalar
        def _(act):
            for sig in [a_raw, a_y, s_exp, b_raw, b_tokv, s_col, s_avc] + \
                    [s[0] for s in (f_gelu, e_gelu, e_hcol)]:
                act.sem_inc(sig.sem, sig.start)

            def col(j):
                return W[:, W_COL + j:W_COL + j + 1]

            def root(l):
                act.wait_ge(ln_var[l].sem, ln_var[l].item(0))
                nc.scalar.activation(small[:, 0], small[:, 6], ACT.Sqrt).then_inc(ln_std[l].sem, 1)

            def stream_columns(l):
                root(l)
                for c in range(NC):
                    act.wait_ge(ln_turned[l].sem, ln_turned[l].item(c))
                    nc.scalar.copy(xT[:, c * CH:(c + 1) * CH], PS[:, c]).then_inc(ln_cols[l].sem, 1)

            stream_columns(0)
            with act.Fori(0, NC) as c:
                for j, dst in enumerate((qT, kT, aT)):
                    act.wait_ge(a_proj.sem, a_proj.item(c * 3 + j))
                    if j < 2:
                        ins = nc.scalar.copy(dst[:, bass.ts(c, CH)], PS[:, 4 + j])
                    else:
                        ins = nc.scalar.activation(dst[:, bass.ts(c, CH)], PS[:, 4 + j], ACT.Sigmoid)
                    ins.then_inc(a_raw.sem, 1)
            with act.Fori(0, NC) as c:
                act.wait_ge(a_sum.sem, a_sum.item(c * DH + (DH - 1)))
                nc.scalar.copy(yT[:, bass.ts(c, CH)], PS[:, 4]).then_inc(a_y.sem, 1)
            root(4)
            act.wait_ge(weights_here.sem, weights_here.moved(1))
            for c in range(NC):
                act.wait_ge(ln_turned[4].sem, ln_turned[4].item(c))
                nc.scalar.activation(ynT[:, c * CH:(c + 1) * CH], PS[:, 4 + c], ACT.Identity,
                                     scale=col(0), bias=col(1)).then_inc(ln_cols[4].sem, 1)

            def ffn(f, l):
                stream_columns(l)
                with act.Fori(0, NC) as c:
                    for k in range(KI):
                        n = c * KI + k
                        act.wait_ge(f_gate[f].sem, f_gate[f].item(n))
                        act.wait_ge(f_hid[f].sem, f_hid[f].spare(n, 2))
                        nc.scalar.activation(gk[:, k % 2], PS[:, k % 2], ACT.Gelu).then_inc(f_gelu[f].sem, 1)

                def gelu(s, k):
                    act.wait_ge(e_gate[f].sem, e_gate[f].item(s))
                    act.wait_ge(e_hid[f].sem, e_hid[f].spare(s, 2))
                    nc.scalar.activation(eg[:, k % 2], PS[:, k % 2], ACT.Gelu).then_inc(e_gelu[f].sem, 1)

                def hidden_columns(s, k):
                    act.wait_ge(e_hturn[f].sem, e_hturn[f].item(s))
                    act.wait_ge(e_out[f].sem, e_out[f].spare(s, 2))
                    nc.scalar.copy(ehT[:, k % 2], PS[:, 4 + k % 2]).then_inc(e_hcol[f].sem, 1)

                gelu(0, 0)
                with act.Fori(0, SLOT_TILES // 4 - 1) as i:
                    for k in range(1, 5):
                        gelu(i * 4 + k, k)
                        hidden_columns(i * 4 + (k - 1), k - 1)
                for s in range(SLOT_TILES - 3, SLOT_TILES + 1):
                    if s < SLOT_TILES:
                        gelu(s, s)
                    hidden_columns(s - 1, s - 1)

            if last_phase >= 2:
                ffn(0, 1)

            def attention():
                stream_columns(2)
                with act.Fori(0, NC // 2) as i:
                    for k in range(2):
                        n = i * 6 + 3 * k
                        act.wait_ge(b_low.sem, b_low.spare(n + 2, 6))
                        act.wait_ge(b_lowp.sem, b_lowp.spare(i * 2 + k, 2))
                        act.wait_ge(b_proj.sem, b_proj.item(n))
                        nc.scalar.activation(raw[:, k, 0], PS[:, 4], ACT.Identity, bias=col(2))
                        nc.scalar.activation(raw[:, k, 1], PS[:, 4], ACT.Identity, bias=col(3)).then_inc(b_raw.sem, 1)
                        act.wait_ge(b_proj.sem, b_proj.item(n + 1))
                        nc.scalar.activation(raw[:, k, 2], PS[:, 5], ACT.Identity, bias=col(4)).then_inc(b_raw.sem, 1)
                        act.wait_ge(b_proj.sem, b_proj.item(n + 2))
                        nc.scalar.copy(raw[:, k, 3], PS[:, 6]).then_inc(b_raw.sem, 1)
                        act.wait_ge(b_parts[k].sem, i * 64 + 64)
                        act.wait_ge(b_raw.sem, b_raw.item(n + 2))
                        nc.scalar.copy(pb[:, k, 0], raw[:, k, 0]).then_inc(b_hi.sem, 1)
                        nc.scalar.copy(pb[:, k, 3], raw[:, k, 3]).then_inc(b_hi.sem, 1)
                        act.wait_ge(b_rot.sem, b_rot.item(n + 2))
                        nc.scalar.copy(pb[:, k, 6], rot[:, k, 0]).then_inc(b_hi.sem, 1)
                        act.wait_ge(b_rotp.sem, b_rotp.item(n + 2))
                        nc.scalar.copy(pb[:, k, 9], rot[:, k, 2]).then_inc(b_hi.sem, 1)
                        for t in range(4):
                            if t < 3:
                                act.wait_ge(b_rest.sem, b_rest.item(n + t))
                            else:
                                act.wait_ge(b_restp.sem, b_restp.item(i * 2 + k))
                            nc.scalar.copy(pb[:, k, 3 * t + 1], rest[:, k, t]).then_inc(b_mid.sem, 1)
                act.wait_ge(b_vpad.sem, 2)
                for n in range(NT):
                    b = 2 * (n % 2)
                    act.wait_ge(b_tok.sem, b_tok.item(n))
                    act.wait_ge(b_vout[n % 2].sem, 16 * (n // 2 + 1))
                    nc.scalar.copy(vpad[:, n % 2, :, 0:DH], PS[:, b + 1, 0:D].rearrange("p (h d) -> p h d", h=H))
                    nc.scalar.copy(vnext[:, n], PS[:, b + 1, D:2 * D]).then_inc(b_tokv.sem, 1)

                def exps(u, k):
                    act.wait_ge(s_nmax.sem, s_nmax.item(u))
                    main = PS[:, 2 * (k % 2):2 * (k % 2) + 2].rearrange("p a (b j) -> p (a b) j", b=2)
                    hg = k % HG
                    for a in range(HG):
                        act.wait_ge(s_turn.sem, s_turn.spare(u * 2 + a // 2, 4))
                        h = HG * hg + a
                        nc.scalar.activation(pr[:, k % 2, a], main[:, a], ACT.Exp, scale=SCALE,
                                             bias=nmax[:, (k // HG) % 2, h:h + 1]).then_inc(s_exp.sem, 1)

                def weight_columns(u, k):
                    for a in range(2):
                        act.wait_ge(s_turn.sem, s_turn.item(u * 2 + a))
                        act.wait_ge(s_av.sem, s_av.spare(u, 2))
                        nc.scalar.copy(prT[:, k % 2, 2 * a:2 * a + 2].rearrange("p a t -> p (a t)"), PS[:, 5 + a])\
                            .then_inc(s_col.sem, 1)

                def outputs(u, k, i):
                    act.wait_ge(s_av.sem, s_av.item(u))
                    tile = i * (BODY // HG) + k // HG
                    act.wait_ge(s_ot.sem, s_ot.spare(tile, 2))
                    nc.scalar.copy(osb[:, k % (2 * HG)], PS[:, 7, 0:P]).then_inc(s_avc.sem, 1)

                def act_unit(i, k, u_min=None):
                    u = i * BODY + k
                    free_run = u_min is None
                    if free_run or u_min < UNITS:
                        exps(u, k)
                    if free_run or 1 <= u_min < UNITS + 1:
                        weight_columns(u - 1, k - 1)
                    if free_run or 2 <= u_min < UNITS + 2:
                        outputs(u - 2, k - 2, i)
                    if k % HG == 0 and (free_run or u_min >= HG):
                        tile = i * (BODY // HG) + (k - HG) // HG
                        act.wait_ge(t_arg.sem, t_arg.item(tile))
                        par = ((k - HG) // HG) % 2
                        nc.scalar.activation(esm[:, par, 1], esm[:, par, 0], ACT.Exp).then_inc(t_exp.sem, 1)

                for k in range(4):
                    act_unit(0, k, k)
                with act.Fori(0, UNITS // BODY - 1) as i:
                    for k in range(4, BODY + 4):
                        act_unit(i, k)
                last = UNITS // BODY - 1
                for k in range(4, BODY + 4):
                    act_unit(last, k, last * BODY + k)
                for c in range(NC):
                    act.wait_ge(b_on_turn.sem, b_on_turn.item(c))
                    nc.scalar.copy(onT[:, c * CH:(c + 1) * CH], PS[:, c]).then_inc(b_on_col.sem, 1)

            if last_phase >= 3:
                attention()
            if last_phase >= 4:
                ffn(1, 3)

        @block.gpsimd
        def _(pool):
            for sig in [a_read, b_lowp]:
                pool.sem_inc(sig.sem, sig.start)
            for sig in [a_sum, s_av, s_turn, s_ot, *b_parts, *b_vout] + [s[0] for s in (f_out, e_up, e_hturn, e_out)]:
                pool.sem_inc(sig.sem, sig.start)
            pool.wait_ge(a_raw.sem, a_raw.item(3 * NC - 1))
            with pool.Fori(0, NC) as c:
                for e in range(DH):
                    n = c * DH + e
                    pool.wait_ge(a_state.sem, a_state.item(n * 2 + 1))
                    pool.wait_ge(a_sum.sem, a_sum.spare(n, 4))
                    take_in(pool)
                    nc.gpsimd.tensor_tensor(zb[:, e % 4], qT[:, bass.ts(c, CH)], hb[:, e % 4], ALU.mult)\
                        .then_inc(a_read.sem, 1)

            def ffn(f):
                pool.wait_ge(ids_set.sem, ids_set.item(0))
                pool.wait_ge(f_cleared[f].sem, f_cleared[f].moved(1))
                pool.wait_ge(f_slots[f].sem, f_slots[f].item(0))
                for n in range(NT):
                    pool.indirect_dma_start(slot_rows[:, :], bass.IndirectOffsetOnAxis(ap=slotu[:, n:n + 1], axis=0),
                                            xn[:, n], None).then_inc(f_sent[f].sem, 16)
                pool.wait_ge(f_ids[f].sem, f_ids[f].moved(1))
                for s in range(SLOT_TILES):
                    pool.wait_ge(e_row[f].sem, e_row[f].item(s))
                    pool.indirect_dma_start(token_out[:, :], bass.IndirectOffsetOnAxis(ap=slot_ids[:, s:s + 1], axis=0),
                                            er[:, s], None, bounds_check=TOK - 1, oob_is_err=False)\
                        .then_inc(e_back[f].sem, 16)

            if last_phase >= 2:
                ffn(0)

            def attention():
                def by_seq(ap):
                    return ap.rearrange("p (b t) -> p b t", t=SEQ)

                def table(col):
                    return C[:, col:col + SEQ].rearrange("p (a t) -> p a t", a=1).to_broadcast([P, SPC, SEQ])

                pool.wait_ge(f_done[0].sem, f_done[0].item(NC - 1))
                nc.gpsimd.memset(vpad.rearrange("p a h w -> p (a h w)"), 0.0).then_inc(b_vpad.sem, 1)
                pool.wait_ge(b_vpad.sem, 1)
                nc.gpsimd.memset(vpad[:, :, :, DH:DH + 1].rearrange("p a h w -> p (a h) w"), 1.0)\
                    .then_inc(b_vpad.sem, 1)
                with pool.Fori(0, NC // 2) as i:
                    for k in range(2):
                        n = i * 6 + 3 * k
                        pool.wait_ge(b_raw.sem, b_raw.item(n + 1))
                        pool.wait_ge(b_lowp.sem, b_lowp.spare(i * 2 + k, 2))
                        nc.gpsimd.tensor_tensor(by_seq(rot[:, k, 2]), by_seq(raw[:, k, 1]), table(C_COS2), ALU.mult)\
                            .then_inc(b_rotp.sem, 1)
                        nc.gpsimd.tensor_tensor(by_seq(rot[:, k, 3]), by_seq(raw[:, k, 2]), table(C_SIN2), ALU.mult)\
                            .then_inc(b_rotp.sem, 1)
                        pool.wait_ge(b_rotp.sem, b_rotp.item(n + 1))
                        nc.gpsimd.tensor_tensor(rot[:, k, 2], rot[:, k, 2], rot[:, k, 3], ALU.add)\
                            .then_inc(b_rotp.sem, 1)
                        pool.wait_ge(b_rotp.sem, b_rotp.item(n + 2))
                        pool.wait_ge(b_hi.sem, b_hi.item(i * 8 + (4 * k + 3)))
                        nc.gpsimd.tensor_tensor(rest[:, k, 3], rot[:, k, 2], pb[:, k, 9], ALU.subtract)\
                            .then_inc(b_restp.sem, 1)
                        pool.wait_ge(b_mid.sem, b_mid.item(i * 8 + (4 * k + 3)))
                        pool.wait_ge(b_restp.sem, b_restp.item(i * 2 + k))
                        nc.gpsimd.tensor_tensor(pb[:, k, 11], rest[:, k, 3], pb[:, k, 10], ALU.subtract)\
                            .then_inc(b_lowp.sem, 1)

            if last_phase >= 3:
                attention()
            if last_phase >= 4:
                ffn(1)


def host_constants():
    f = np.float32
    p = np.arange(P)
    consts = np.zeros((P, C_ALL), f)
    consts[:, C_ID:C_ID + P] = np.eye(P)
    consts[:-1, C_SD:C_SD + P] = -BIG * np.eye(P)[1:]
    consts[:, C_TRI:C_TRI + P] = p[:, None] < p[None, :]
    consts[:, C_ONE:C_ONE + P] = 1
    consts[:, C_IOTA:C_IOTA + NE] = np.arange(NE)
    consts[:, C_THR:C_THR + NE * NT] = np.tile(P * np.arange(NT), NE)
    consts[:, C_SLOT:C_SLOT + SLOT_TILES * NE] = np.repeat(np.arange(SLOT_TILES), NE)
    consts[P - 1, C_LAST:C_LAST + NT] = np.where(np.arange(NT) % QT == QT - 1, -BIG, 0)
    freq = (1.0 / 10000.0 ** (np.arange(0, DH, 2, dtype=f) / f(DH))).astype(f).astype(np.float64)
    pos = np.arange(SEQ)
    half = DH // 2
    row_f = freq[p % half][:, None]
    sign = np.where(p % DH < half, -1.0, 1.0)[:, None]
    for cos_col, sin_col, ahead in ((C_COS1, C_SIN1, 0), (C_COS2, C_SIN2, SEQ)):
        angle = row_f * (pos + ahead)[None, :]
        consts[:, cos_col:cos_col + SEQ] = sign * np.cos(angle)
        consts[:, sin_col:sin_col + SEQ] = np.sin(angle)
    angle = freq[:, None] * pos[None, :]
    positions = np.concatenate([np.sin(angle), np.cos(angle)]).astype(f)
    head_sums = np.zeros((P, DH, P), f)
    for e in range(DH):
        head_sums[p, e, p // DH * DH + e] = 1
    head_sums = head_sums.reshape(P, DH * P)
    rules = np.zeros((2, H, SEQ), "uint16")
    rules[0, :, P - 1] = 0xF149
    rules[1, :, P] = 0x3F80
    rules = rules.reshape(2, H * SEQ).view(f)
    token_ids = (np.arange(NT)[None, :] * P + p[:, None]).astype(np.int32)
    clear_row = np.zeros((P, ROWW), np.int32)
    clear_row[:, D] = NO_TOKEN
    return dict(head_sums=head_sums, consts=consts, positions=positions, row96=rules,
                token_ids=token_ids, clear_row=clear_row.view(f))


LAST_PHASE = 4


def kernel(**inputs):
    import concourse.bacc as bacc
    from concourse.bass_utils import run_bass_kernel_spmd

    a = {k: np.asarray(v) for k, v in inputs.items()}
    A, B, Fn = (lambda n: a["L0_attn_a_" + n]), (lambda n: a["L0_attn_b_" + n]), (lambda n: a["L0_ffn_" + n])
    swap = np.arange(D) ^ (DH // 2)
    columns = np.stack([A("gamma"), A("beta"), B("u").reshape(-1), B("v").reshape(-1), B("v").reshape(-1)[swap]], 1)
    weights = np.concatenate([A("Wq").T, A("Wk").T, A("Wg").T, A("Wo").T, B("Wq")[:, swap], B("Wq"), B("Wv"), B("Wk"),
                              B("Wo"), Fn("Wg"), columns], 1)
    row_head = np.arange(P) // DH * DH
    spread_w = np.stack([A("Wv").T[:, row_head + e] for e in range(DH)], 1).reshape(D, DH * P)
    arrays = dict(
        x_in=A("x").reshape(TOK, D), weights=weights, spread_w=spread_w,
        rows=np.stack([B("u").reshape(-1), B("bo")]),
        w1=Fn("W1"), w2=Fn("W2"), w3=Fn("W3"), w1s=Fn("w1s"), w2s=Fn("w2s"), w3s=Fn("w3s"), **host_constants())
    arrays = {k: np.ascontiguousarray(v) for k, v in arrays.items()}
    nc = bacc.Bacc("TRN2", target_bir_lowering=False, num_devices=1)
    aps, feeds = {}, {}
    for name, v in arrays.items():
        aps[name] = nc.dram_tensor(f"{name}_dram", v.shape, mybir.dt.from_np(v.dtype), kind="ExternalInput").ap()
        feeds[f"{name}_dram"] = v
    aps["row96"] = aps["row96"].bitcast(BF16)
    out = nc.dram_tensor("out_dram", (TOK, D), F32, kind="ExternalOutput").ap()
    build_program(nc, out=out, last_phase=LAST_PHASE, **aps)
    r = run_bass_kernel_spmd(nc, [feeds], core_ids=[0])
    return r.results[0]["out_dram"].reshape(BATCH, SEQ, D)
```

```python
from contextlib import ExitStack

import numpy as np

import concourse.bass as bass
from concourse import mybir

ALU = mybir.AluOpType
ACT = mybir.ActivationFunctionType
AX_X = mybir.AxisListType.X
F32 = mybir.dt.float32
BF16 = mybir.dt.bfloat16
U8 = mybir.dt.uint8
U32 = mybir.dt.uint32
I32 = mybir.dt.int32

P = 128
BATCH, SEQ, D = 8, 256, 128
TOK = BATCH * SEQ
NT = TOK // P
QT = SEQ // P
H, DH = 16, 8
INTER = 512
KI = INTER // P
NE = 8
CH = 512
NC = TOK // CH
SPC = CH // SEQ
SLOT_TILES = NT + NE
SLOTS = SLOT_TILES * P
ROWW = D + 1
NO_TOKEN = 1 << 20
EPS = 1e-5
BIG = 1e30
SCALE = float(DH) ** -0.5
RUNS = [3, 2, 1]
NPROD = sum(RUNS)
HALF = NPROD * DH
STK = 2 * HALF
HG = 4
UPB = QT * (H // HG)
UNITS = BATCH * UPB
BODY = 2 * UPB
VW = 32

C_ID, C_SD, C_TRI, C_ONE = 0, 128, 256, 384
C_IOTA, C_THR, C_SLOT, C_LAST = 512, 520, 648, 840
C_COS1 = 856
C_SIN1, C_COS2, C_SIN2 = C_COS1 + SEQ, C_COS1 + 2 * SEQ, C_COS1 + 3 * SEQ
C_ALL = C_COS1 + 4 * SEQ
W_Q, W_K, W_G, W_O, W_BS, W_BQ, W_BV, W_BK, W_BO, W_R = [128 * j for j in range(10)]
W_COL = W_R + NE
W_ALL = W_COL + 5


class Signal:

    def __init__(self, sem, start=0):
        self.sem, self.start = sem, start

    def item(self, n):
        return n + (self.start + 1)

    def spare(self, n, ring):
        return n + (self.start + 1 - ring)

    def moved(self, n):
        return 16 * n + self.start


def build_program(nc, x_in, weights, spread_w, head_sums, consts, rows, positions, row96,
                  token_ids, clear_row, w1, w2, w3, w1s, w2s, w3s, out, last_phase=4):
    with ExitStack() as ctx:
        def sb(name, shape, dt=F32):
            return ctx.enter_context(nc.sbuf_tensor(name, shape, dt))

        def signal(name, start=0):
            return Signal(ctx.enter_context(nc.semaphore(name)), start)

        def dram(name, shape, dt=F32):
            return nc.dram_tensor(name, shape, dt, kind="Internal").ap()

        def take_in(eng):
            eng.sem_inc(waits_taken.sem, 1)

        x = sb("x", [P, NT, D])
        xn = sb("xn", [P, NT, ROWW])
        xT = sb("xT", [P, TOK + P])
        W = sb("W", [P, W_ALL])
        C = sb("C", [P, C_ALL])
        w12 = sb("w12", [P, NE + 1, 2 * INTER])
        w3t = sb("w3t", [P, NE + 1, KI, D])
        stats = sb("stats", [P, NT, 6])
        small = sb("small", [P, 8, NT])
        cb = sb("cb", [P, 4, P], BF16)
        crow = sb("crow", [P, ROWW])
        one8b = sb("one8b", [P, NT * NE], BF16)
        slotu = sb("slotu", [P, NT], U32)
        slot_ids = sb("slot_ids", [P, SLOT_TILES], U32)
        idsb = sb("idsb", [P, NT], I32)
        eword = sb("eword", [P, SLOT_TILES], I32)
        nsd = sb("nsd", [P, NT, H])
        nmax = sb("nmax", [P, 2, H])
        mxs = sb("mxs", [P, 2, HG])
        esm = sb("esm", [P, 2, 4, H])
        msk = sb("msk", [P, 2, HG, P], U8)
        rowb = sb("rowb", [P, 2, D])
        rpos = sb("rpos", [DH, 2, SEQ])
        rpb = sb("rpb", [DH, 3, SEQ], BF16)
        arena = sb("arena", [P, 24700])
        used = [0]

        def cut(*shape, dt=F32):
            n = int(np.prod(shape))
            words = n if dt == F32 else n // 2
            ap = arena[:, used[0]:used[0] + words]
            used[0] += words
            assert used[0] <= 24700
            if dt != F32:
                ap = ap.bitcast(dt)
            names = "abcd"[:len(shape)]
            if len(shape) == 1:
                return ap
            return ap.rearrange(f"p ({' '.join(names)}) -> p {' '.join(names)}", **dict(zip(names, shape)))

        aT, qT, kT, yT = cut(TOK), cut(TOK), cut(TOK), cut(TOK)
        wv, hsum = cut(DH * P), cut(DH * P)
        kvb, hb, zb = cut(2, CH), cut(4, CH), cut(4, CH)
        ynT = cut(TOK)
        yn = xn[:, :, 0:D]
        used[0] = 0
        gk, hT = cut(2, CH), cut(KI, CH)
        xr, xrT = cut(4, ROWW), cut(4, P)
        eg, eh, ehT, er = cut(2, CH), cut(2, CH), cut(2, CH), cut(SLOT_TILES, D)
        yback = cut(NT, D)
        mx8, ix8f, ixf, one8 = cut(NT, 8), cut(NT, 8), cut(NT), cut(NT, NE)
        ix8 = ix8f.bitcast(U32)
        tot, csum, cmp8 = cut(NE, NT), cut(NE, NT), cut(NE, NT)
        base, work, cnt8 = cut(NE, NT), cut(NT, NE), cut(6, NE)
        slotf, ecmp, eidf = cut(NT), cut(SLOT_TILES, NE), cut(2, SLOT_TILES)
        used[0] = 0
        vnext = cut(NT, D)
        after_shared = used[0]
        raw = cut(2, 4, CH)
        rot = cut(2, 4, CH)
        after_raw = used[0]
        pb = cut(NC, 12, CH, dt=BF16)
        used[0] = after_shared
        prT = cut(2, HG, QT * P)
        vring = cut(2, QT, H * VW)
        pr = cut(2, HG, SEQ)
        osb, otok, t4 = cut(2 * HG, P), cut(2, H, 9), cut(2, D)
        tq = osb.rearrange("p a b -> p (a b)").rearrange("p (g n) -> p g n", g=2)
        assert used[0] <= after_raw
        used[0] = after_raw
        stacks = cut(2, 3, H, SEQ, dt=BF16)
        kst, qlo, qup = stacks[:, :, 0], stacks[:, :, 1], stacks[:, :, 2]
        vals = cut(NT, D)
        on = xn[:, :, 0:D]
        onT = xT[:, 0:TOK]

        PS = ctx.enter_context(nc.psum_tensor("PS", [P, 8, 512], F32))
        ident = C[:, C_ID:C_ID + P]

        slot_rows = dram("slot_rows", [SLOTS, ROWW])
        token_out = dram("token_out", [TOK, D])
        query_parts = dram("query_parts", [3, 3, P, TOK + P], BF16)
        key_parts = dram("key_parts", [NPROD, P, TOK], BF16)
        pos_parts = dram("pos_parts", [NPROD, DH, SEQ], BF16)

        x_here, weights_here, consts_here, ids_here = [signal(n) for n in
            ("x_here", "weights_here", "consts_here", "ids_here")]
        a_here, ffn_here, b_here, clear_here = [signal(n) for n in ("a_here", "ffn_here", "b_here", "clear_here")]
        consts_cast, ids_set = signal("consts_cast"), signal("ids_set")
        out_stored = signal("out_stored")
        pad_set = signal("pad_set")
        waits_taken = signal("waits_taken")
        dve_order = signal("dve_order")
        steps = [0]

        ln_var = [signal(f"ln{l}_var") for l in range(5)]
        ln_std = [signal(f"ln{l}_std") for l in range(5)]
        ln_rows = [signal(f"ln{l}_rows") for l in range(5)]
        ln_turned = [signal(f"ln{l}_turned") for l in range(5)]
        ln_cols = [signal(f"ln{l}_cols") for l in range(5)]

        a_proj, a_raw = signal("a_proj"), signal("a_raw", 3)
        a_value = signal("a_value")
        a_kv = signal("a_kv", 4)
        a_state = signal("a_state", 4)
        a_read = signal("a_read", 4)
        a_sum = signal("a_sum", 4)
        a_y = signal("a_y", 1)
        a_yrow, a_out, a_res = signal("a_yrow"), signal("a_out"), signal("a_res")

        def per_layer(name, items, start=0):
            first = signal(f"f_{name}", start)
            return [first, Signal(first.sem, start + items)]

        f_logits, f_onehot, f_prefix = per_layer("logits", 1), per_layer("onehot", 1), per_layer("prefix", 1)
        f_slots, f_experts = per_layer("slots", 1), per_layer("experts", 1)
        f_cleared, f_sent, f_ids = per_layer("cleared", 16), per_layer("sent", 16 * NT), per_layer("ids", 16)
        f_gate, f_up = per_layer("gate", NC * KI), per_layer("up", NC * KI)
        f_gelu, f_hid = per_layer("gelu", NC * KI, 2), per_layer("hid", NC * KI, 4)
        f_out, f_res = per_layer("out", NC * KI, 4), per_layer("res", NC, 1)
        st = SLOT_TILES
        e_in = list(zip(*[per_layer(f"e_in{k}", 4 * st) for k in range(4)]))
        e_turn, e_col = per_layer("e_turn", st), per_layer("e_col", st, 4)
        e_gate, e_up = per_layer("e_gate", st), per_layer("e_up", st, 4)
        e_gelu, e_hid = per_layer("e_gelu", st, 2), per_layer("e_hid", st, 2)
        e_hturn, e_hcol = per_layer("e_hturn", st, 2), per_layer("e_hcol", st, 2)
        e_out, e_row = per_layer("e_out", st, 2), per_layer("e_row", st, 4)
        e_back = per_layer("e_back", 16 * st)
        f_back, f_done = per_layer("back", 16), per_layer("done", NC)

        b_proj, b_raw = signal("b_proj"), signal("b_raw")
        b_rot, b_rotp = signal("b_rot"), signal("b_rotp")
        b_hi, b_mid = signal("b_hi"), signal("b_mid")
        b_rest, b_restp = signal("b_rest"), signal("b_restp")
        b_low, b_lowp = signal("b_low"), signal("b_lowp")
        b_parts = [signal(f"b_parts{c}") for c in range(NC)]
        b_pos, b_pos_out = signal("b_pos"), signal("b_pos_out")
        b_tok, b_tokv, b_tokd = signal("b_tok"), signal("b_tokv"), signal("b_tokd")
        b_tsum = signal("b_tsum")
        b_vpad, b_vring = signal("b_vpad"), signal("b_vring")
        b_stack = [signal(f"b_stack{k}") for k in range(2)]
        s_scores, s_pick, s_max, s_nmax = signal("s_scores"), signal("s_pick", 1), signal("s_max"), signal("s_nmax")
        s_exp = signal("s_exp", 8)
        s_turn, s_col = signal("s_turn", 4), signal("s_col", 4)
        s_av, s_avc = signal("s_av", 2), signal("s_avc", 1)
        s_ot, s_otc = signal("s_ot", 2), signal("s_otc", 1)
        t_arg, t_exp, t_den, t_rden = signal("t_arg"), signal("t_exp", 2), signal("t_den"), signal("t_rden")
        t_v, t_sum, t_on = signal("t_v"), signal("t_sum"), signal("t_on", 2)
        b_on_turn, b_on_col, b_out, b_res = signal("b_on_turn"), signal("b_on_col"), signal("b_out"), signal("b_res")

        N_STORE = 3 + len(RUNS)
        N_CONST = 3
        N_BATCH = 4 * len(RUNS) + 1

        def rests(c):
            k = c % 2
            return raw[:, k, 0], raw[:, k, 3], rot[:, k, 0], rot[:, k, 2]

        block = ctx.enter_context(nc.Block())

        @block.sync
        def _(sp):
            def load(dst, src, sig):
                sp.dma_start(dst, src).then_inc(sig.sem, 16)

            load(x[:], x_in.rearrange("(n p) d -> p n d", p=P), x_here)
            load(C[:], consts, consts_here)
            load(W[:], weights, weights_here)
            load(wv, spread_w, a_here)
            load(hsum, head_sums, a_here)
            load(idsb[:], token_ids, ids_here)
            load(crow[:], clear_row, clear_here)
            load(w12[:, NE, 0:INTER], w1s, ffn_here)
            load(w12[:, NE, INTER:], w2s, ffn_here)
            load(w3t[:, NE], w3s.rearrange("(k p) n -> p k n", p=P), ffn_here)
            load(w12[:, 0:NE, 0:INTER], w1.rearrange("e d n -> d e n"), ffn_here)
            load(w12[:, 0:NE, INTER:], w2.rearrange("e d n -> d e n"), ffn_here)
            for e in range(NE):
                load(w3t[:, e], w3[e].rearrange("(k p) n -> p k n", p=P), ffn_here)
            load(rowb[:, 0], rows[0:1, :].to_broadcast([P, D]), b_here)
            load(rowb[:, 1], rows[1:2, :].to_broadcast([P, D]), b_here)
            load(rpos[:, 0], positions, b_here)
            rows_v = slot_rows.rearrange("(s p) d -> s p d", p=P)

            def clear(f):
                sp.wait_ge(clear_here.sem, clear_here.moved(1))
                load(slot_rows.rearrange("(s p) d -> p s d", p=P),
                     crow[:].rearrange("p (a d) -> p a d", a=1).to_broadcast([P, SLOT_TILES, ROWW]), f_cleared[f])

            clear(0)

            def ffn(f):
                sp.wait_ge(f_sent[f].sem, f_sent[f].moved(NT))
                for s in range(4):
                    load(xr[:, s], rows_v[s], e_in[f][s])
                with nc.allow_non_contiguous_dma(reason="one number of every slot"):
                    load(slot_ids[:], slot_rows.rearrange("(s p) d -> p s d", p=P)[:, :, D].bitcast(U32), f_ids[f])
                with sp.Fori(1, SLOT_TILES // 4) as i:
                    for k in range(4):
                        sp.wait_ge(e_turn[f].sem, e_turn[f].spare(i * 4 + k, 4))
                        take_in(sp)
                        load(xr[:, k], rows_v[bass.ds(i * 4 + k, 1)].rearrange("a p d -> p (a d)"), e_in[f][k])
                sp.wait_ge(e_back[f].sem, e_back[f].moved(SLOT_TILES))
                load(yback, token_out.rearrange("(n p) d -> p n d", p=P), f_back[f])

            if last_phase >= 2:
                ffn(0)
            if last_phase >= 4:
                for k in range(4):
                    sp.wait_ge(e_in[0][k].sem, e_in[0][k].moved(SLOT_TILES // 4))
                sp.wait_ge(f_ids[0].sem, f_ids[0].moved(1))
                clear(1)
            if last_phase >= 3:
                sp.wait_ge(b_pos.sem, b_pos.item(3))
                def repeated(part, run):
                    rows, wide = part.shape
                    return part.rearrange("p (a t) -> p a t", a=1).to_broadcast([rows, run, wide])

                first = 0
                for j, run in enumerate(RUNS):
                    load(pos_parts[first:first + run].rearrange("c d t -> d c t"), repeated(rpb[:, j], run), b_pos_out)
                    first += run
                sp.wait_ge(pad_set.sem, pad_set.item(0))
                load(query_parts[2].rearrange("c p t -> p c t")[:, :, TOK:TOK + P],
                     repeated(xT[:, TOK:TOK + P].bitcast(BF16)[:, 0:P], 3), b_pos_out)
                def store_parts(c):
                    sp.wait_ge(b_mid.sem, b_mid.item(4 * c + 3))
                    sp.wait_ge(b_low.sem, b_low.item(3 * c + 2))
                    sp.wait_ge(b_lowp.sem, b_lowp.item(c))
                    here = slice(c * CH, (c + 1) * CH)
                    for t, src in enumerate((0, 2, 3)):
                        load(query_parts[t].rearrange("c p t -> p c t")[:, :, here],
                             pb[:, c, 3 * src:3 * src + 3], b_parts[c])
                    first = 0
                    for j, run in enumerate(RUNS):
                        load(key_parts[first:first + run].rearrange("c p t -> p c t")[:, :, here],
                             repeated(pb[:, c, 3 + j], run), b_parts[c])
                        first += run
                def load_stacks(b, par):
                    load(kst[0:HALF, par], key_parts.rearrange("c (d h) t -> (c d) h t", d=DH)[:, :, bass.ds(b * SEQ, SEQ)],
                         b_stack[par])
                    for dst, half, t, ahead in ((qup, 0, 0, 0), (qup, 1, 2, 1), (qlo, 0, 0, 0), (qlo, 1, 1, 0)):
                        r0 = half * HALF
                        for run in RUNS:
                            load(dst[r0:r0 + run * DH, par],
                                 query_parts[t, 0:run].rearrange("c (d h) t -> (c d) h t", d=DH)
                                 [:, :, bass.ds(b * SEQ + ahead, SEQ)], b_stack[par])
                            r0 += run * DH

                for par in range(2):
                    for c in (2 * par, 2 * par + 1):
                        store_parts(c)
                    for c in (2 * par, 2 * par + 1):
                        sp.wait_ge(b_parts[c].sem, b_parts[c].moved(N_STORE))
                    if par == 0:
                        sp.wait_ge(b_pos_out.sem, b_pos_out.moved(len(RUNS) + 1))
                    load(qup[STK:STK + 1, par], row96[0:1].rearrange("a (h t) -> a h t", h=H), b_stack[par])
                    load(kst[STK:STK + 1, par], row96[1:2].rearrange("a (h t) -> a h t", h=H), b_stack[par])
                    load(kst[HALF:STK, par], pos_parts.rearrange("c d (a t) -> (c d) a t", a=1)
                         .to_broadcast([HALF, H, SEQ]), b_stack[par])
                    load_stacks(par, par)
                with sp.Fori(1, BATCH // 2) as i:
                    for par in range(2):
                        sp.wait_ge(s_scores.sem, s_scores.spare(i * BODY + ((par + 1) * UPB - 1), BODY))
                        take_in(sp)
                        load_stacks(i * 2 + par, par)
            if last_phase >= 4:
                ffn(1)
            sp.wait_ge(b_here.sem, b_here.moved(3))
            sp.wait_ge(ffn_here.sem, ffn_here.moved(5 + NE))
            final = {1: a_res, 2: f_done[0], 3: b_res, 4: f_done[1]}[last_phase]
            for c in range(NC):
                sp.wait_ge(final.sem, final.item(c))
                load(out.rearrange("(n p) d -> p n d", p=P)[:, 4 * c:4 * c + 4], x[:, 4 * c:4 * c + 4], out_stored)
            sp.wait_ge(out_stored.sem, out_stored.moved(NC))

        @block.tensor
        def _(pe):
            def turn_tiles(l, src, bank0=0):
                for n in range(NT):
                    pe.wait_ge(ln_rows[l].sem, ln_rows[l].item(n))
                    ins = nc.tensor.transpose(PS[:, bank0 + n // 4, (n % 4) * P:(n % 4 + 1) * P], src(n), ident)
                    if n % 4 == 3:
                        ins.then_inc(ln_turned[l].sem, 1)

            def stream_turn(l):
                turn_tiles(l, lambda n: xn[:, n, 0:D])

            pe.wait_ge(consts_here.sem, consts_here.moved(1))
            stream_turn(0)
            pe.wait_ge(weights_here.sem, weights_here.moved(1))
            with pe.Fori(0, NC) as c:
                pe.wait_ge(ln_cols[0].sem, ln_cols[0].item(c))
                for j, w in enumerate((W_Q, W_K, W_G)):
                    pe.wait_ge(a_raw.sem, a_raw.spare(c * 3 + j, 3))
                    nc.tensor.matmul(PS[:, 4 + j], W[:, w:w + P], xT[:, bass.ts(c, CH)],
                                     start=True, stop=True).then_inc(a_proj.sem, 1)
            pe.wait_ge(a_raw.sem, a_raw.item(3 * NC - 1))
            pe.wait_ge(a_here.sem, a_here.moved(2))

            def spread(c, e):
                pe.wait_ge(a_kv.sem, a_kv.spare(c * DH + e, 4))
                nc.tensor.matmul(PS[:, e % 4], wv[:, e * P:(e + 1) * P], xT[:, bass.ts(c, CH)],
                                 start=True, stop=True).then_inc(a_value.sem, 1)

            def summed(c, e):
                pe.wait_ge(a_read.sem, a_read.item(c * DH + e))
                if e == 0:
                    pe.wait_ge(a_y.sem, a_y.spare(c, 1))
                nc.tensor.matmul(PS[:, 4], hsum[:, e * P:(e + 1) * P], zb[:, e % 4],
                                 start=(e == 0), stop=(e == DH - 1)).then_inc(a_sum.sem, 1)

            for e in range(4):
                spread(0, e)
            with pe.Fori(0, NC - 1) as c:
                for e in range(DH):
                    spread(c if e < 4 else c + 1, (e + 4) % DH)
                    summed(c, e)
            for e in range(DH):
                if e < 4:
                    spread(NC - 1, e + 4)
                summed(NC - 1, e)
            pe.wait_ge(a_kv.sem, a_kv.item(NC * DH - 1))
            for n in range(NT):
                if n % 4 == 0:
                    pe.wait_ge(a_y.sem, a_y.item(n // 4))
                ins = nc.tensor.transpose(PS[:, n // 4, (n % 4) * P:(n % 4 + 1) * P], yT[:, n * P:(n + 1) * P], ident)
                if n % 4 == 3:
                    ins.then_inc(a_yrow.sem, 1)
            turn_tiles(4, lambda n: yn[:, n], bank0=4)
            for n in range(NT):
                if n % 4 == 0:
                    pe.wait_ge(ln_cols[4].sem, ln_cols[4].item(n // 4))
                ins = nc.tensor.matmul(PS[:, n // 4, (n % 4) * P:(n % 4 + 1) * P], ynT[:, n * P:(n + 1) * P],
                                       W[:, W_O:W_O + D], start=True, stop=True)
                if n % 4 == 3:
                    ins.then_inc(a_out.sem, 1)

            def ffn(f, l):
                stream_turn(l)
                for n in range(NT):
                    if n % 4 == 0:
                        pe.wait_ge(ln_cols[l].sem, ln_cols[l].item(n // 4))
                    ins = nc.tensor.matmul(PS[:, 6, n * NE:(n + 1) * NE], xT[:, n * P:(n + 1) * P],
                                           W[:, W_R:W_R + NE], start=True, stop=True)
                ins.then_inc(f_logits[f].sem, 1)
                pe.wait_ge(ffn_here.sem, ffn_here.moved(5 + NE))

                def shared_out(c, k):
                    pe.wait_ge(f_hid[f].sem, f_hid[f].item(c * KI + k))
                    if k == 0:
                        pe.wait_ge(f_res[f].sem, f_res[f].spare(c, 1))
                    for t in range(4):
                        ins = nc.tensor.matmul(PS[:, 4, t * P:(t + 1) * P], hT[:, k, t * P:(t + 1) * P],
                                               w3t[:, NE, k], start=(k == 0 and t == 0), stop=(k == KI - 1),
                                               skip_group_check=True)
                    ins.then_inc(f_out[f].sem, 1)

                def shared(c):
                    for k in range(KI):
                        pe.wait_ge(f_gelu[f].sem, f_gelu[f].spare(c * KI + k, 2))
                        nc.tensor.matmul(PS[:, k % 2], w12[:, NE, k * P:(k + 1) * P], xT[:, bass.ts(c, CH)],
                                         start=True, stop=True).then_inc(f_gate[f].sem, 1)
                        pe.wait_ge(f_hid[f].sem, f_hid[f].spare(c * KI + k, 2))
                        nc.tensor.matmul(PS[:, 2 + k % 2], w12[:, NE, INTER + k * P:INTER + (k + 1) * P],
                                         xT[:, bass.ts(c, CH)], start=True, stop=True).then_inc(f_up[f].sem, 1)
                        if k > 0:
                            shared_out(c, k - 1)
                    shared_out(c, KI - 1)

                shared(0)
                shared(1)
                pe.wait_ge(f_onehot[f].sem, f_onehot[f].item(0))
                pe.wait_ge(consts_cast.sem, consts_cast.item(3))
                nc.tensor.matmul(PS[:, 6, 0:NT * NE], cb[:, 2], one8b[:], start=True, stop=True)
                nc.tensor.matmul(PS[:, 7, 0:NT * NE], cb[:, 3], one8b[:], start=True,
                                 stop=True).then_inc(f_prefix[f].sem, 1)
                with pe.Fori(2, NC) as c:
                    shared(c)

                def turn_in(s, k):
                    wait_tile(s, k)
                    pe.wait_ge(e_col[f].sem, e_col[f].spare(s, 1))
                    nc.tensor.transpose(PS[:, 6, 0:P], xr[:, k, 0:D], ident).then_inc(e_turn[f].sem, 1)

                def wait_tile(s, k):
                    pe.wait_ge(e_in[f][k].sem, (s - k) * 4 + (16 + e_in[f][k].start))

                def gate(s, k, e):
                    pe.wait_ge(e_col[f].sem, e_col[f].item(s))
                    pe.wait_ge(e_gelu[f].sem, e_gelu[f].spare(s, 2))
                    nc.tensor.matmul(PS[:, k % 2], xrT[:, k], w12[:, e, 0:INTER],
                                     start=True, stop=True).then_inc(e_gate[f].sem, 1)

                def up(s, k, e):
                    pe.wait_ge(e_hid[f].sem, e_hid[f].spare(s, 2))
                    nc.tensor.matmul(PS[:, 2 + k % 2], xrT[:, k], w12[:, e, INTER:2 * INTER],
                                     start=True, stop=True).then_inc(e_up[f].sem, 1)

                def turn_hidden(s, k):
                    pe.wait_ge(e_hid[f].sem, e_hid[f].item(s))
                    pe.wait_ge(e_hcol[f].sem, e_hcol[f].spare(s, 2))
                    for j in range(KI):
                        ins = nc.tensor.transpose(PS[:, 4 + k % 2, j * P:(j + 1) * P], eh[:, k % 2, j * P:(j + 1) * P], ident)
                    ins.then_inc(e_hturn[f].sem, 1)

                def down(s, k, e):
                    pe.wait_ge(e_hcol[f].sem, e_hcol[f].item(s))
                    pe.wait_ge(e_row[f].sem, e_row[f].spare(s, 1))
                    for j in range(KI):
                        ins = nc.tensor.matmul(PS[:, 7, 0:P], ehT[:, k % 2, j * P:(j + 1) * P],
                                               w3t[:, e, j], start=(j == 0), stop=(j == KI - 1))
                    ins.then_inc(e_out[f].sem, 1)

                def expert_of(word, j):
                    return (word // NE ** j) % NE

                def step(i, k, word, j0, s_min=None):
                    s = i * 4 + k
                    free_run = s_min is None
                    if free_run or s_min + 1 < SLOT_TILES:
                        turn_in(s + 1, (k + 1) % 4)
                    enters = free_run or s_min < SLOT_TILES
                    if enters:
                        gate(s, k % 4, expert_of(word, k - j0))
                    if free_run or s_min >= 2:
                        down(s - 2, (k - 2) % 4, expert_of(word, k - 2 - j0))
                    if enters:
                        up(s, k % 4, expert_of(word, k - j0))
                    if free_run or 1 <= s_min < SLOT_TILES + 1:
                        turn_hidden(s - 1, (k - 1) % 4)

                def load_word(s):
                    return pe.value_load(eword[0:1, bass.ds(s, 1)], min_val=0, max_val=NE ** 6 - 1)

                pe.wait_ge(f_experts[f].sem, f_experts[f].item(0))
                pe.wait_ge(f_res[f].sem, f_res[f].item(NC - 1))
                pe.wait_ge(f_slots[f].sem, f_slots[f].item(0))
                word = load_word(0)
                turn_in(0, 0)
                for s in range(2):
                    step(0, s, word, 0, s)
                with pe.Fori(0, SLOT_TILES // 4 - 1) as i:
                    word = load_word(i * 4)
                    for k in range(2, 6):
                        step(i, k, word, 0)
                word = load_word(SLOT_TILES - 4)
                for s in range(SLOT_TILES - 2, SLOT_TILES + 2):
                    step(0, s, word, SLOT_TILES - 4, s)

            if last_phase >= 2:
                ffn(0, 1)

            def attention():
                stream_turn(2)
                pe.wait_ge(ln_cols[2].sem, ln_cols[2].item(NC - 1))
                for c in range(NC):
                    for j, w in enumerate((W_BQ, W_BS, W_BK)):
                        if c > 0:
                            pe.wait_ge(b_raw.sem, b_raw.item((c - 1) * 3 + j))
                        nc.tensor.matmul(PS[:, 4 + j], W[:, w:w + P], xT[:, c * CH:(c + 1) * CH],
                                         start=True, stop=True).then_inc(b_proj.sem, 1)
                pe.wait_ge(pad_set.sem, pad_set.item(0))
                for n in range(NT):
                    g, place = n // 4, n % 4 * D
                    b = 4 * (g % 2)
                    if n == 4:
                        pe.wait_ge(b_raw.sem, b_raw.item(3 * NC - 1))
                    if n % 4 == 0 and g >= 2:
                        pe.wait_ge(b_tokd.sem, b_tokd.item(2 * (g - 2) + 1))
                        pe.wait_ge(b_tokv.sem, b_tokv.item(2 * (g - 2) + 1))
                    for j, (ahead, w) in enumerate(((0, W_BQ), (1, W_BK), (0, W_BV), (1, W_BV))):
                        ins = nc.tensor.matmul(PS[:, b + j, place:place + D], xT[:, n * P + ahead:(n + 1) * P + ahead],
                                               W[:, w:w + D], start=True, stop=True)
                    if n % 4 == 3:
                        ins.then_inc(b_tok.sem, 1)
                pe.wait_ge(b_tokd.sem, b_tokd.item(2 * (NT // 4) - 1))
                pe.wait_ge(b_tokv.sem, b_tokv.item(2 * (NT // 4) - 1))

                def scores(i, k, tile_out):
                    u = i * BODY + k
                    k = k % BODY
                    par, qt, hg = k // UPB, (k // HG) % QT, k % HG
                    if k % UPB == 0:
                        pe.wait_ge(b_stack[par].sem, i * (16 * N_BATCH) + 16 * (N_CONST + N_BATCH))
                    q = slice(qt * P, (qt + 1) * P)
                    main = PS[:, 2 * (k % 2):2 * (k % 2) + 2].rearrange("p a (b j) -> p (a b) j", b=2)

                    def all_keys():
                        for a in range(HG):
                            h = HG * hg + a
                            if a % 2 == 0:
                                pe.wait_ge(s_exp.sem, s_exp.spare(u * HG + (a + 1), 2 * HG))
                            if qt == 0:
                                nc.tensor.matmul(main[:, a], qup[0:STK + 1, par, h, q], kst[0:STK + 1, par, h],
                                                 start=(a % 2 == 0), stop=False, skip_group_check=True)
                                ins = nc.tensor.matmul(main[:, a, 0:P], cb[:, 0], cb[:, 1],
                                                       start=False, stop=True, skip_group_check=True)
                            else:
                                ins = nc.tensor.matmul(main[:, a], qlo[0:STK, par, h, q], kst[0:STK, par, h],
                                                       start=(a % 2 == 0), stop=True, skip_group_check=True)
                        return ins

                    def other_side():
                        pe.wait_ge(s_pick.sem, s_pick.spare(u, 1))
                        if tile_out is not None:
                            pe.wait_ge(s_otc.sem, s_otc.item(tile_out))
                        for a in range(HG):
                            h = HG * hg + a
                            other = PS[:, 4, a * P:(a + 1) * P]
                            if qt == 0:
                                ins = nc.tensor.matmul(other, qlo[0:STK, par, h, q], kst[0:STK, par, h, q],
                                                       start=(a == 0), stop=True, skip_group_check=True)
                            else:
                                nc.tensor.matmul(other, qup[0:STK + 1, par, h, q], kst[0:STK + 1, par, h, q],
                                                 start=(a == 0), stop=False, skip_group_check=True)
                                ins = nc.tensor.matmul(other, cb[:, 0], cb[:, 1], start=False, stop=True,
                                                       skip_group_check=True)
                        return ins

                    if tile_out is None:
                        other_side()
                        ins = all_keys()
                    else:
                        all_keys()
                        ins = other_side()
                    ins.then_inc(s_scores.sem, 1)

                def turn(u, k):
                    k = k % BODY
                    for a in range(HG):
                        pe.wait_ge(s_exp.sem, s_exp.item(u * HG + a))
                        if a % 2 == 0:
                            pe.wait_ge(s_col.sem, s_col.spare(u * 2 + a // 2, 2))
                        for j in range(QT):
                            ins = nc.tensor.transpose(PS[:, 5 + a // 2, ((a % 2) * QT + j) * P:((a % 2) * QT + j + 1) * P],
                                                      pr[:, k % 2, a, j * P:(j + 1) * P], ident)
                        if a % 2 == 1:
                            ins.then_inc(s_turn.sem, 1)

                def weigh(i, k):
                    u = i * BODY + k
                    k = k % BODY
                    par, hg = k // UPB, k % HG
                    pe.wait_ge(s_col.sem, s_col.item(u * 2 + 1))
                    if k % UPB == 0:
                        pe.wait_ge(b_vring.sem, b_vring.item(i * 2 + par))
                    pe.wait_ge(s_avc.sem, s_avc.spare(u, 1))
                    for j in range(QT):
                        for a in range(HG):
                            h = HG * hg + a
                            ins = nc.tensor.matmul(PS[VW * a:VW * (a + 1), 7, 0:P],
                                                   vring[:, par, j, h * VW:(h + 1) * VW],
                                                   prT[:, k % 2, a, j * P:(j + 1) * P],
                                                   start=(j == 0), stop=(j == QT - 1), tile_position=(0, VW * a),
                                                   skip_group_check=True)
                    ins.then_inc(s_av.sem, 1)

                def turn_out(i, k, u_min):
                    pe.wait_ge(s_avc.sem, s_avc.item(i * BODY + (k - 5)))
                    pe.wait_ge(s_otc.sem, s_otc.spare(i * (BODY // HG) + (k - 8) // HG, 1))
                    pe.wait_ge(s_pick.sem, s_pick.item(i * BODY + (k - 1) if u_min is None else min(u_min, UNITS) - 1))
                    for a in range(HG):
                        ins = nc.tensor.transpose(PS[:, 4, a * P:(a + 1) * P], osb[:, (k - 8 + a) % (2 * HG)], ident)
                    ins.then_inc(s_ot.sem, 1)

                def step(i, k, u_min=None):
                    u = i * BODY + k
                    free_run = u_min is None
                    turns = k % HG == 0 and (free_run or u_min >= 8)
                    if turns:
                        turn_out(i, k, u_min)
                    if free_run or u_min < UNITS:
                        tile_out = i * (BODY // HG) + (k - 8) // HG if turns else None
                        if k >= BODY:
                            scores(i + 1, k - BODY, tile_out)
                        else:
                            scores(i, k, tile_out)
                    if free_run or 2 <= u_min < UNITS + 2:
                        turn(u - 2, k - 2)
                    if free_run or 3 <= u_min < UNITS + 3:
                        weigh(i, k - 3) if k - 3 < BODY else weigh(i + 1, k - 3 - BODY)

                for k in range(5):
                    step(0, k, k)
                with pe.Fori(0, UNITS // BODY - 1) as i:
                    for k in range(5, BODY + 5):
                        step(i, k)
                last = UNITS // BODY - 1
                for k in range(5, BODY + 5):
                    step(last, k, last * BODY + k)

                for n in range(NT):
                    if n % 4 == 0:
                        pe.wait_ge(t_on.sem, t_on.item(n + 3))
                    ins = nc.tensor.transpose(PS[:, n // 4, (n % 4) * P:(n % 4 + 1) * P], on[:, n], ident)
                    if n % 4 == 3:
                        ins.then_inc(b_on_turn.sem, 1)
                for n in range(NT):
                    if n % 4 == 0:
                        pe.wait_ge(b_on_col.sem, b_on_col.item(n // 4))
                    ins = nc.tensor.matmul(PS[:, 4 + n // 4, (n % 4) * P:(n % 4 + 1) * P], onT[:, n * P:(n + 1) * P],
                                           W[:, W_BO:W_BO + D], start=True, stop=True)
                    if n % 4 == 3:
                        ins.then_inc(b_out.sem, 1)

            if last_phase >= 3:
                attention()
            if last_phase >= 4:
                ffn(1, 3)

        @block.vector
        def _(dve):
            for sig in [a_kv, a_state, s_pick, t_on, s_otc] + \
                    [s[0] for s in (f_res, e_col, e_hid, e_row, f_hid)]:
                dve.sem_inc(sig.sem, sig.start)

            def step():
                steps[0] += 1
                return 1

            nc.vector.memset(xT[:, TOK:TOK + P], 0.0).then_inc(pad_set.sem, 1)

            def spread_stats(l):
                dve.wait_ge(dve_order.sem, steps[0])
                me, mo, qe, qo = [stats[:, :, j] for j in (1, 4, 2, 5)]
                nc.vector.tensor_tensor(small[:, 0], me, mo, ALU.add).then_inc(dve_order.sem, step())
                nc.vector.tensor_tensor(small[:, 1], me, mo, ALU.subtract).then_inc(dve_order.sem, step())
                nc.vector.tensor_tensor(small[:, 2], qe, qo, ALU.add).then_inc(dve_order.sem, step())
                dve.wait_ge(dve_order.sem, steps[0])
                nc.vector.tensor_scalar(small[:, 3], small[:, 0], 0.5, None, ALU.mult).then_inc(dve_order.sem, step())
                nc.vector.scalar_tensor_tensor(out=small[:, 4], in0=small[:, 1], scalar=0.25, in1=small[:, 1],
                                               op0=ALU.mult, op1=ALU.mult).then_inc(dve_order.sem, step())
                nc.vector.tensor_scalar(small[:, 5], small[:, 2], 1.0 / D, EPS, ALU.mult, ALU.add)\
                    .then_inc(dve_order.sem, step())
                dve.wait_ge(dve_order.sem, steps[0])
                nc.vector.tensor_tensor(small[:, 6], small[:, 4], small[:, 5], ALU.add).then_inc(ln_var[l].sem, 1)
                dve.wait_ge(ln_std[l].sem, ln_std[l].item(0))
                nc.vector.reciprocal(small[:, 7], small[:, 0]).then_inc(dve_order.sem, step())
                dve.wait_ge(dve_order.sem, steps[0])

            def norm(l, src, dst):
                for n in range(NT):
                    nc.vector.tensor_scalar(dst(n), src(n), small[:, 3, n:n + 1], small[:, 7, n:n + 1],
                                            ALU.subtract, ALU.mult).then_inc(ln_rows[l].sem, 1)

            def stream_norm(l):
                dve.wait_ge(dve_order.sem, steps[0])
                for n in range(NT):
                    nc.vector.bn_stats(stats[:, n], x[:, n]).then_inc(dve_order.sem, step())
                spread_stats(l)
                norm(l, lambda n: x[:, n], lambda n: xn[:, n, 0:D])

            dve.wait_ge(x_here.sem, x_here.moved(1))
            stream_norm(0)
            dve.wait_ge(ids_here.sem, ids_here.moved(1))
            nc.vector.tensor_copy(xn[:, :, D].bitcast(I32), idsb[:]).then_inc(ids_set.sem, 1)
            dve.wait_ge(consts_here.sem, consts_here.moved(1))
            for j, col in enumerate((C_ID, C_SD, C_TRI, C_ONE)):
                nc.vector.tensor_copy(cb[:, j], C[:, col:col + P]).then_inc(consts_cast.sem, 1)

            tri = C[:, C_TRI:C_TRI + P].rearrange("p (a k) -> p a k", a=1).to_broadcast([P, HG, P])
            nc.vector.tensor_scalar(msk[:, 0], tri, 0.0, None, ALU.is_equal).then_inc(dve_order.sem, step())
            nc.vector.tensor_scalar(msk[:, 1], tri, 0.0, None, ALU.is_gt).then_inc(dve_order.sem, step())

            dve.wait_ge(a_raw.sem, a_raw.item(3 * NC - 1))
            with dve.Fori(0, NC) as c:
                def product(e):
                    n = c * DH + e
                    dve.wait_ge(a_value.sem, a_value.item(n))
                    dve.wait_ge(a_state.sem, a_state.spare(n * 2 + 1, 4))
                    nc.vector.tensor_tensor(kvb[:, e % 2], kT[:, bass.ts(c, CH)], PS[:, e % 4], ALU.mult)\
                        .then_inc(a_kv.sem, 1)

                def state(e):
                    n = c * DH + e
                    dve.wait_ge(a_kv.sem, a_kv.item(n))
                    dve.wait_ge(a_read.sem, a_read.spare(n, 4))
                    for j in range(SPC):
                        nc.vector.tensor_tensor_scan(
                            hb[:, e % 4, j * SEQ:(j + 1) * SEQ], aT[:, bass.ds(c * CH + j * SEQ, SEQ)],
                            kvb[:, e % 2, j * SEQ:(j + 1) * SEQ], 0.0, ALU.mult, ALU.add).then_inc(a_state.sem, 1)

                product(0)
                for e in range(DH):
                    if e + 1 < DH:
                        product(e + 1)
                    state(e)
            for n in range(NT):
                if n % 4 == 0:
                    dve.wait_ge(a_yrow.sem, a_yrow.item(n // 4))
                nc.vector.bn_stats(stats[:, n], PS[:, n // 4, (n % 4) * P:(n % 4 + 1) * P])\
                    .then_inc(dve_order.sem, step())
            spread_stats(4)
            norm(4, lambda n: PS[:, n // 4, (n % 4) * P:(n % 4 + 1) * P], lambda n: yn[:, n])

            def add_banks(sig, done, bank0):
                for c in range(NC):
                    dve.wait_ge(sig.sem, sig.item(c))
                    part = x[:, 4 * c:4 * c + 4].rearrange("p a b -> p (a b)")
                    nc.vector.tensor_tensor(part, part, PS[:, bank0 + c], ALU.add).then_inc(done.sem, 1)
                dve.wait_ge(done.sem, done.item(NC - 1))

            add_banks(a_out, a_res, 0)

            def ffn(f, l):
                stream_norm(l)

                def hidden(c):
                    for k in range(KI):
                        n = c * KI + k
                        dve.wait_ge(f_gelu[f].sem, f_gelu[f].item(n))
                        dve.wait_ge(f_up[f].sem, f_up[f].item(n))
                        dve.wait_ge(f_out[f].sem, f_out[f].spare(n, 4))
                        nc.vector.tensor_tensor(hT[:, k], gk[:, k % 2], PS[:, 2 + k % 2], ALU.mult)\
                            .then_inc(f_hid[f].sem, 1)
                    dve.wait_ge(f_out[f].sem, f_out[f].item(c * KI + KI - 1))
                    part = x[:, bass.ds(c * 4, 4)].rearrange("p a b -> p (a b)")
                    nc.vector.tensor_tensor(part, part, PS[:, 4], ALU.add).then_inc(f_res[f].sem, 1)

                hidden(0)
                dve.wait_ge(f_logits[f].sem, f_logits[f].item(0))
                for n in range(NT):
                    nc.vector.max(mx8[:, n], PS[:, 6, n * NE:(n + 1) * NE]).then_inc(dve_order.sem, step())
                dve.wait_ge(dve_order.sem, steps[0])
                for n in range(NT):
                    nc.vector.max_index(ix8[:, n], mx8[:, n], PS[:, 6, n * NE:(n + 1) * NE])\
                        .then_inc(dve_order.sem, step())
                dve.wait_ge(dve_order.sem, steps[0])
                nc.vector.tensor_copy(ixf, ix8[:, :, 0]).then_inc(dve_order.sem, step())
                dve.wait_ge(dve_order.sem, steps[0])
                iota = C[:, C_IOTA:C_IOTA + NE].rearrange("p (a e) -> p a e", a=1).to_broadcast([P, NT, NE])
                nc.vector.tensor_tensor(one8, iota, ixf.rearrange("p (n a) -> p n a", a=1).to_broadcast([P, NT, NE]),
                                        ALU.is_equal).then_inc(dve_order.sem, step())
                dve.wait_ge(dve_order.sem, steps[0])
                nc.vector.tensor_copy(one8b[:], one8.rearrange("p a b -> p (a b)")).then_inc(f_onehot[f].sem, 1)
                hidden(1)
                dve.wait_ge(f_prefix[f].sem, f_prefix[f].item(0))
                nc.vector.tensor_copy(tot, PS[:, 7, 0:NT * NE].rearrange("p (n e) -> p e n", e=NE))\
                    .then_inc(dve_order.sem, step())
                dve.wait_ge(dve_order.sem, steps[0])
                nc.vector.tensor_tensor_scan(csum.rearrange("p a b -> p (a b)"), C[:, C_ONE:C_ONE + NE * NT],
                                             tot.rearrange("p a b -> p (a b)"), 0.0, ALU.mult, ALU.add)\
                                                 .then_inc(dve_order.sem, step())
                nc.vector.tensor_reduce(cnt8[:, 0], tot, AX_X, ALU.add).then_inc(dve_order.sem, step())
                dve.wait_ge(dve_order.sem, steps[0])
                thr = C[:, C_THR:C_THR + NE * NT].rearrange("p (a b) -> p a b", a=NE)
                nc.vector.tensor_tensor(cmp8, cnt8[:, 0].rearrange("p (e a) -> p e a", a=1).to_broadcast([P, NE, NT]),
                                        thr, ALU.is_gt).then_inc(dve_order.sem, step())
                nc.vector.tensor_tensor(base, csum, tot, ALU.subtract).then_inc(dve_order.sem, step())
                dve.wait_ge(dve_order.sem, steps[0])
                nc.vector.tensor_reduce(cnt8[:, 1], cmp8, AX_X, ALU.add).then_inc(dve_order.sem, step())
                dve.wait_ge(dve_order.sem, steps[0])
                nc.vector.tensor_tensor_scan(cnt8[:, 2], C[:, C_ONE:C_ONE + NE], cnt8[:, 1], 0.0,
                                             ALU.mult, ALU.add).then_inc(dve_order.sem, step())
                dve.wait_ge(dve_order.sem, steps[0])
                nc.vector.tensor_tensor(cnt8[:, 3], cnt8[:, 2], cnt8[:, 1], ALU.subtract)\
                    .then_inc(dve_order.sem, step())
                slot_no = C[:, C_SLOT:C_SLOT + SLOT_TILES * NE].rearrange("p (s e) -> p s e", e=NE)
                nc.vector.tensor_tensor(ecmp, slot_no,
                                        cnt8[:, 2].rearrange("p (a e) -> p a e", a=1).to_broadcast([P, SLOT_TILES, NE]),
                                        ALU.is_ge).then_inc(dve_order.sem, step())
                dve.wait_ge(dve_order.sem, steps[0])
                nc.vector.scalar_tensor_tensor(out=cnt8[:, 4], in0=cnt8[:, 3], scalar=float(P), in1=base[:, :, 0],
                                               op0=ALU.mult, op1=ALU.subtract).then_inc(dve_order.sem, step())
                nc.vector.tensor_reduce(eidf[:, 0], ecmp, AX_X, ALU.add).then_inc(dve_order.sem, step())
                dve.wait_ge(dve_order.sem, steps[0])
                nc.vector.tensor_tensor(cmp8, base, cnt8[:, 4].rearrange("p (e a) -> p e a", a=1).to_broadcast([P, NE, NT]),
                                        ALU.add).then_inc(dve_order.sem, step())
                nc.vector.tensor_scalar(eidf[:, 0], eidf[:, 0], float(NE - 1), None, ALU.min)\
                    .then_inc(dve_order.sem, step())
                dve.wait_ge(dve_order.sem, steps[0])
                nc.vector.tensor_tensor(work, PS[:, 6, 0:NT * NE].rearrange("p (n e) -> p n e", e=NE),
                                        cmp8.rearrange("p e n -> p n e"), ALU.add).then_inc(dve_order.sem, step())
                nc.vector.tensor_copy(eidf[:, 1], eidf[:, 0]).then_inc(dve_order.sem, step())
                dve.wait_ge(dve_order.sem, steps[0])
                nc.vector.tensor_tensor(work, work, one8, ALU.mult).then_inc(dve_order.sem, step())
                for j in range(1, 6):
                    n = SLOT_TILES - j
                    dve.wait_ge(dve_order.sem, steps[0])
                    nc.vector.scalar_tensor_tensor(out=eidf[:, 1, 0:n], in0=eidf[:, 0, j:], scalar=float(NE ** j),
                                                   in1=eidf[:, 1, 0:n], op0=ALU.mult, op1=ALU.add)\
                                                       .then_inc(dve_order.sem, step())
                    if j == 1:
                        nc.vector.tensor_reduce(slotf, work, AX_X, ALU.add).then_inc(dve_order.sem, step())
                    if j == 2:
                        nc.vector.tensor_copy(slotu[:], slotf).then_inc(f_slots[f].sem, 1)
                dve.wait_ge(dve_order.sem, steps[0])
                nc.vector.tensor_copy(eword[:], eidf[:, 1]).then_inc(f_experts[f].sem, 1)
                with dve.Fori(2, NC) as c:
                    hidden(c)

                def columns(s, k):
                    dve.wait_ge(e_turn[f].sem, e_turn[f].item(s))
                    dve.wait_ge(e_up[f].sem, e_up[f].spare(s, 4))
                    nc.vector.tensor_copy(xrT[:, k], PS[:, 6, 0:P]).then_inc(e_col[f].sem, 1)

                def out_rows(s):
                    dve.wait_ge(e_out[f].sem, e_out[f].item(s))
                    nc.vector.tensor_copy(er[:, bass.ds(s, 1)].rearrange("p a d -> p (a d)"), PS[:, 7, 0:P])\
                        .then_inc(e_row[f].sem, 1)

                def product(s, k):
                    dve.wait_ge(e_gelu[f].sem, e_gelu[f].item(s))
                    dve.wait_ge(e_up[f].sem, e_up[f].item(s))
                    dve.wait_ge(e_hturn[f].sem, e_hturn[f].spare(s, 2))
                    nc.vector.tensor_tensor(eh[:, k % 2], eg[:, k % 2], PS[:, 2 + k % 2], ALU.mult)\
                        .then_inc(e_hid[f].sem, 1)

                def expert_step(i, k, s_min=None):
                    s = i * 4 + k
                    if s_min is None or s_min + 1 < SLOT_TILES:
                        columns(s + 1, (k + 1) % 4)
                    if s_min is None or s_min >= 2:
                        out_rows(s - 2)
                    if s_min is None or s_min < SLOT_TILES:
                        product(s, k % 4)

                columns(0, 0)
                for s in range(2):
                    expert_step(0, s, s)
                with dve.Fori(0, SLOT_TILES // 4 - 1) as i:
                    for k in range(2, 6):
                        expert_step(i, k)
                for s in range(SLOT_TILES - 2, SLOT_TILES + 2):
                    expert_step(0, s, s)
                dve.wait_ge(f_res[f].sem, f_res[f].item(NC - 1))
                dve.wait_ge(f_back[f].sem, f_back[f].moved(1))
                for c in range(NC):
                    part = x[:, 4 * c:4 * c + 4]
                    nc.vector.tensor_tensor(part, part, yback[:, 4 * c:4 * c + 4], ALU.add).then_inc(f_done[f].sem, 1)
                dve.wait_ge(f_done[f].sem, f_done[f].item(NC - 1))

            if last_phase >= 2:
                ffn(0, 1)

            def attention():
                dve.wait_ge(b_here.sem, b_here.moved(3))
                stream_norm(2)
                nc.vector.tensor_copy(rpb[:, 0], rpos[:, 0]).then_inc(b_pos.sem, 1)
                dve.wait_ge(b_pos.sem, b_pos.item(0))
                nc.vector.tensor_tensor(rpos[:, 1], rpos[:, 0], rpb[:, 0], ALU.subtract).then_inc(b_pos.sem, 1)
                dve.wait_ge(b_pos.sem, b_pos.item(1))
                nc.vector.tensor_copy(rpb[:, 1], rpos[:, 1]).then_inc(b_pos.sem, 1)
                dve.wait_ge(b_pos.sem, b_pos.item(2))
                nc.vector.tensor_tensor(rpb[:, 2], rpos[:, 1], rpb[:, 1], ALU.subtract).then_inc(b_pos.sem, 1)

                def by_seq(ap):
                    return ap.rearrange("p (b t) -> p b t", t=SEQ)

                def table(col):
                    return C[:, col:col + SEQ].rearrange("p (a t) -> p a t", a=1).to_broadcast([P, SPC, SEQ])

                def rest_of(c, t):
                    rest = rests(c)[t]
                    dve.wait_ge(b_hi.sem, b_hi.item(4 * c + t))
                    nc.vector.tensor_tensor(rest, rest, pb[:, c, 3 * t], ALU.subtract)\
                        .then_inc(b_rest.sem, 1)

                for c in range(NC + 1):
                    k = c % 2
                    if c < NC:
                        if c >= 2:
                            dve.wait_ge(b_low.sem, b_low.item(3 * (c - 2) + 2))
                        dve.wait_ge(b_raw.sem, b_raw.item(3 * c + 1))
                        nc.vector.tensor_tensor(by_seq(rot[:, k, 0]), by_seq(raw[:, k, 1]), table(C_COS1), ALU.mult)\
                            .then_inc(b_rot.sem, 1)
                        nc.vector.tensor_tensor(by_seq(rot[:, k, 1]), by_seq(raw[:, k, 2]), table(C_SIN1), ALU.mult)\
                            .then_inc(b_rot.sem, 1)
                        rest_of(c, 0)
                        dve.wait_ge(b_rot.sem, b_rot.item(3 * c + 1))
                        nc.vector.tensor_tensor(rot[:, k, 0], rot[:, k, 0], rot[:, k, 1], ALU.add).then_inc(b_rot.sem, 1)
                        rest_of(c, 1)
                    if c > 0:
                        for t in range(3):
                            n = 3 * (c - 1) + t
                            dve.wait_ge(b_mid.sem, b_mid.item(4 * (c - 1) + t))
                            dve.wait_ge(b_rest.sem, b_rest.item(n))
                            nc.vector.tensor_tensor(pb[:, c - 1, 3 * t + 2], rests(c - 1)[t],
                                                    pb[:, c - 1, 3 * t + 1], ALU.subtract).then_inc(b_low.sem, 1)
                    if c < NC:
                        dve.wait_ge(b_rot.sem, b_rot.item(3 * c + 2))
                        rest_of(c, 2)
                dve.wait_ge(ln_rows[2].sem, ln_rows[2].item(NT - 1))
                nc.vector.tensor_tensor(x[:], x[:], rowb[:, 1].rearrange("p (a d) -> p a d", a=1).to_broadcast([P, NT, D]),
                                        ALU.add).then_inc(dve_order.sem, step())
                u_row = rowb[:, 0]
                dve.wait_ge(b_lowp.sem, b_lowp.item(NC - 1))
                dve.wait_ge(b_low.sem, b_low.item(3 * NC - 1))
                for g in range(NT // 4):
                    b, now = 4 * (g % 2), tq[:, g % 2]
                    dve.wait_ge(b_tok.sem, b_tok.item(g))
                    if g >= 2:
                        dve.wait_ge(b_tsum.sem, b_tsum.item(g - 2))
                    nc.vector.tensor_tensor(now.rearrange("p (n d) -> p n d", n=4),
                                            PS[:, b].rearrange("p (n d) -> p n d", n=4),
                                            rowb[:, 0].rearrange("p (a d) -> p a d", a=1).to_broadcast([P, 4, D]),
                                            ALU.add).then_inc(b_tokd.sem, 1)
                    dve.wait_ge(b_tokd.sem, b_tokd.item(2 * g))
                    nc.vector.tensor_tensor(now, now, PS[:, b + 1], ALU.mult).then_inc(b_tokd.sem, 1)
                    dve.wait_ge(b_tokd.sem, b_tokd.item(2 * g + 1))
                    nc.vector.tensor_reduce(nsd[:, 4 * g:4 * g + 4], now.rearrange("p (n d h) -> p n h d", n=4, h=H),
                                            AX_X, ALU.add).then_inc(b_tsum.sem, 1)
                dve.wait_ge(b_tsum.sem, b_tsum.item(NT // 4 - 1))
                last_q = C[:, C_LAST:C_LAST + NT].rearrange("p (n a) -> p n a", a=1).to_broadcast([P, NT, H])
                nc.vector.tensor_tensor(nsd[:], nsd[:], last_q, ALU.add).then_inc(dve_order.sem, step())
                dve.wait_ge(dve_order.sem, steps[0])
                nc.vector.tensor_scalar(nsd[:], nsd[:], -SCALE, None, ALU.mult).then_inc(dve_order.sem, step())
                dve.wait_ge(dve_order.sem, steps[0])

                def pick_and_max(i, k):
                    u = i * BODY + k
                    kk = k % BODY
                    qt, hg = (kk // HG) % QT, kk % HG
                    tile = (i if k < BODY else i + 1) * (BODY // HG) + kk // HG
                    main = PS[:, 2 * (k % 2):2 * (k % 2) + 2].rearrange("p a (b j) -> p (a b) j", b=2)
                    dve.wait_ge(s_scores.sem, s_scores.item(u))
                    take_in(dve)
                    nc.vector.copy_predicated(main[:, :, qt * P:(qt + 1) * P], msk[:, qt],
                                              PS[:, 4].rearrange("p (a j) -> p a j", a=HG)).then_inc(s_pick.sem, 1)
                    dve.wait_ge(s_pick.sem, s_pick.item(u))
                    nc.vector.tensor_reduce(mxs[:, k % 2], main, AX_X, ALU.max).then_inc(s_max.sem, 1)
                    dve.wait_ge(s_max.sem, s_max.item(u))
                    if hg == 0:
                        dve.wait_ge(t_exp.sem, t_exp.spare(tile, 2))
                    nc.vector.scalar_tensor_tensor(
                        out=nmax[:, (k // HG) % 2, hg * HG:(hg + 1) * HG], in0=mxs[:, k % 2], scalar=-SCALE,
                        in1=nsd[:, bass.ds(tile, 1), hg * HG:(hg + 1) * HG].rearrange("p a h -> p (a h)"),
                        op0=ALU.mult, op1=ALU.min).then_inc(s_nmax.sem, 1)

                def finish_tile(i, k):
                    kk = k % BODY
                    par = (kk // HG) % 2
                    tile = i * (BODY // HG) + kk // HG
                    one = bass.ds(tile, 1)
                    dve.wait_ge(s_otc.sem, s_otc.item(tile))
                    dve.wait_ge(t_exp.sem, t_exp.item(tile))
                    e_next, den, rden = esm[:, par, 1], esm[:, par, 2], esm[:, par, 3]
                    nc.vector.tensor_tensor(den, otok[:, par, :, 8], e_next, ALU.add).then_inc(t_den.sem, 1)
                    wide = e_next.rearrange("p (h a) -> p h a", a=1).to_broadcast([P, H, DH])
                    nc.vector.tensor_tensor(t4[:, par].rearrange("p (h d) -> p h d", h=H),
                                            vnext[:, one].rearrange("p a (h d) -> p (a h) d", h=H), wide, ALU.mult)\
                        .then_inc(t_v.sem, 1)
                    dve.wait_ge(t_den.sem, t_den.item(tile))
                    nc.vector.reciprocal(rden, den).then_inc(t_rden.sem, 1)
                    dve.wait_ge(t_v.sem, t_v.item(tile))
                    nc.vector.tensor_tensor(t4[:, par].rearrange("p (h d) -> p h d", h=H),
                                            t4[:, par].rearrange("p (h d) -> p h d", h=H),
                                            otok[:, par, :, 0:DH], ALU.add).then_inc(t_sum.sem, 1)
                    dve.wait_ge(t_rden.sem, t_rden.item(tile))
                    dve.wait_ge(t_sum.sem, t_sum.item(tile))
                    nc.vector.tensor_tensor(on[:, one].rearrange("p a (h d) -> p (a h) d", h=H),
                                            t4[:, par].rearrange("p (h d) -> p h d", h=H),
                                            rden.rearrange("p (h a) -> p h a", a=1).to_broadcast([P, H, DH]), ALU.mult)\
                        .then_inc(t_on.sem, 1)

                def output_rows(i, k):
                    tile = i * (BODY // HG) + (k - 8) // HG
                    dve.wait_ge(s_ot.sem, s_ot.item(tile))
                    dve.wait_ge(t_on.sem, t_on.spare(tile, 2))
                    nc.vector.tensor_copy(otok[:, ((k - 8) // HG) % 2],
                                          PS[:, 4].rearrange("p (h w) -> p h w", w=VW)[:, :, 0:DH + 1])\
                                              .then_inc(s_otc.sem, 1)

                def tile_arg(i, k):
                    kk = k % BODY
                    par = (kk // HG) % 2
                    tile = i * (BODY // HG) + kk // HG
                    dve.wait_ge(s_nmax.sem, s_nmax.item(i * BODY + kk))
                    dve.wait_ge(t_on.sem, t_on.spare(tile, 2))
                    nc.vector.tensor_tensor(esm[:, par, 0], nmax[:, par],
                                            nsd[:, bass.ds(tile, 1)].rearrange("p a h -> p (a h)"), ALU.subtract)\
                        .then_inc(t_arg.sem, 1)

                LAG = 5

                def dve_unit(i, k, u_min=None):
                    if k % HG == 0 and (u_min is None or u_min >= 8):
                        output_rows(i, k)
                    if u_min is None or u_min < UNITS:
                        pick_and_max(i, k)
                        if k % HG == HG - 1:
                            tile_arg(i, k) if k < BODY else tile_arg(i + 1, k - BODY)
                    done = k - LAG
                    if done % HG == HG - 1 and (u_min is None or u_min >= LAG):
                        finish_tile(i, done)

                for k in range(LAG):
                    dve_unit(0, k, k)
                with dve.Fori(0, UNITS // BODY - 1) as i:
                    for k in range(LAG, BODY + LAG):
                        dve_unit(i, k)
                last = UNITS // BODY - 1
                for k in range(LAG, BODY + LAG):
                    dve_unit(last, k, last * BODY + k)
                add_banks(b_out, b_res, 4)

            if last_phase >= 3:
                attention()
            if last_phase >= 4:
                ffn(1, 3)

        @block.scalar
        def _(act):
            for sig in [a_raw, a_y, s_exp, s_col, s_avc, t_exp] + \
                    [s[0] for s in (f_gelu, e_gelu, e_hcol)]:
                act.sem_inc(sig.sem, sig.start)

            def col(j):
                return W[:, W_COL + j:W_COL + j + 1]

            def root(l):
                act.wait_ge(ln_var[l].sem, ln_var[l].item(0))
                nc.scalar.activation(small[:, 0], small[:, 6], ACT.Sqrt).then_inc(ln_std[l].sem, 1)

            def stream_columns(l):
                root(l)
                for c in range(NC):
                    act.wait_ge(ln_turned[l].sem, ln_turned[l].item(c))
                    nc.scalar.copy(xT[:, c * CH:(c + 1) * CH], PS[:, c]).then_inc(ln_cols[l].sem, 1)

            stream_columns(0)
            with act.Fori(0, NC) as c:
                for j, dst in enumerate((qT, kT, aT)):
                    act.wait_ge(a_proj.sem, a_proj.item(c * 3 + j))
                    if j < 2:
                        ins = nc.scalar.copy(dst[:, bass.ts(c, CH)], PS[:, 4 + j])
                    else:
                        ins = nc.scalar.activation(dst[:, bass.ts(c, CH)], PS[:, 4 + j], ACT.Sigmoid)
                    ins.then_inc(a_raw.sem, 1)
            with act.Fori(0, NC) as c:
                act.wait_ge(a_sum.sem, a_sum.item(c * DH + (DH - 1)))
                nc.scalar.copy(yT[:, bass.ts(c, CH)], PS[:, 4]).then_inc(a_y.sem, 1)
            root(4)
            act.wait_ge(weights_here.sem, weights_here.moved(1))
            for c in range(NC):
                act.wait_ge(ln_turned[4].sem, ln_turned[4].item(c))
                nc.scalar.activation(ynT[:, c * CH:(c + 1) * CH], PS[:, 4 + c], ACT.Identity,
                                     scale=col(0), bias=col(1)).then_inc(ln_cols[4].sem, 1)

            def ffn(f, l):
                stream_columns(l)
                with act.Fori(0, NC) as c:
                    for k in range(KI):
                        n = c * KI + k
                        act.wait_ge(f_gate[f].sem, f_gate[f].item(n))
                        act.wait_ge(f_hid[f].sem, f_hid[f].spare(n, 2))
                        nc.scalar.activation(gk[:, k % 2], PS[:, k % 2], ACT.Gelu).then_inc(f_gelu[f].sem, 1)

                def gelu(s, k):
                    act.wait_ge(e_gate[f].sem, e_gate[f].item(s))
                    act.wait_ge(e_hid[f].sem, e_hid[f].spare(s, 2))
                    nc.scalar.activation(eg[:, k % 2], PS[:, k % 2], ACT.Gelu).then_inc(e_gelu[f].sem, 1)

                def hidden_columns(s, k):
                    act.wait_ge(e_hturn[f].sem, e_hturn[f].item(s))
                    act.wait_ge(e_out[f].sem, e_out[f].spare(s, 2))
                    nc.scalar.copy(ehT[:, k % 2], PS[:, 4 + k % 2]).then_inc(e_hcol[f].sem, 1)

                gelu(0, 0)
                with act.Fori(0, SLOT_TILES // 4 - 1) as i:
                    for k in range(1, 5):
                        gelu(i * 4 + k, k)
                        hidden_columns(i * 4 + (k - 1), k - 1)
                for s in range(SLOT_TILES - 3, SLOT_TILES + 1):
                    if s < SLOT_TILES:
                        gelu(s, s)
                    hidden_columns(s - 1, s - 1)

            if last_phase >= 2:
                ffn(0, 1)

            def attention():
                stream_columns(2)
                def high(c, t):
                    nc.scalar.copy(pb[:, c, 3 * t], rests(c)[t]).then_inc(b_hi.sem, 1)

                for c in range(NC + 1):
                    k, n = c % 2, 3 * c
                    if c < NC:
                        if c >= 2:
                            act.wait_ge(b_low.sem, b_low.item(n - 4))
                            act.wait_ge(b_lowp.sem, b_lowp.item(c - 2))
                        act.wait_ge(b_proj.sem, b_proj.item(n))
                        nc.scalar.activation(raw[:, k, 0], PS[:, 4], ACT.Identity, bias=col(2))
                        nc.scalar.activation(raw[:, k, 1], PS[:, 4], ACT.Identity, bias=col(3)).then_inc(b_raw.sem, 1)
                        act.wait_ge(b_proj.sem, b_proj.item(n + 1))
                        nc.scalar.activation(raw[:, k, 2], PS[:, 5], ACT.Identity, bias=col(4)).then_inc(b_raw.sem, 1)
                        act.wait_ge(b_raw.sem, b_raw.item(n))
                        high(c, 0)
                        act.wait_ge(b_proj.sem, b_proj.item(n + 2))
                        nc.scalar.copy(raw[:, k, 3], PS[:, 6]).then_inc(b_raw.sem, 1)
                        act.wait_ge(b_raw.sem, b_raw.item(n + 2))
                        high(c, 1)
                    if c > 0:
                        for t in range(4):
                            if t < 3:
                                act.wait_ge(b_rest.sem, b_rest.item(n - 3 + t))
                            else:
                                act.wait_ge(b_restp.sem, b_restp.item(c - 1))
                            nc.scalar.copy(pb[:, c - 1, 3 * t + 1], rests(c - 1)[t]).then_inc(b_mid.sem, 1)
                    if c < NC:
                        act.wait_ge(b_rot.sem, b_rot.item(n + 2))
                        high(c, 2)
                        act.wait_ge(b_rotp.sem, b_rotp.item(n + 2))
                        high(c, 3)
                act.wait_ge(b_low.sem, b_low.item(3 * NC - 1))
                for g in range(NT // 4):
                    b = 4 * (g % 2) + 2
                    act.wait_ge(b_tok.sem, b_tok.item(g))
                    for j, dst in enumerate((vals, vnext)):
                        nc.scalar.copy(dst[:, 4 * g:4 * g + 4].rearrange("p n d -> p (n d)"), PS[:, b + j])\
                            .then_inc(b_tokv.sem, 1)

                def exps(u, k):
                    act.wait_ge(s_nmax.sem, s_nmax.item(u))
                    main = PS[:, 2 * (k % 2):2 * (k % 2) + 2].rearrange("p a (b j) -> p (a b) j", b=2)
                    hg = k % HG
                    for a in range(HG):
                        act.wait_ge(s_turn.sem, s_turn.spare(u * 2 + a // 2, 4))
                        h = HG * hg + a
                        nc.scalar.activation(pr[:, k % 2, a], main[:, a], ACT.Exp, scale=SCALE,
                                             bias=nmax[:, (k // HG) % 2, h:h + 1]).then_inc(s_exp.sem, 1)

                def weight_columns(u, k):
                    for a in range(2):
                        act.wait_ge(s_turn.sem, s_turn.item(u * 2 + a))
                        act.wait_ge(s_av.sem, s_av.spare(u, 2))
                        nc.scalar.copy(prT[:, k % 2, 2 * a:2 * a + 2].rearrange("p a t -> p (a t)"), PS[:, 5 + a])\
                            .then_inc(s_col.sem, 1)

                def outputs(u, k, i):
                    act.wait_ge(s_av.sem, s_av.item(u))
                    tile = i * (BODY // HG) + k // HG
                    act.wait_ge(s_ot.sem, s_ot.spare(tile, 2))
                    nc.scalar.copy(osb[:, k % (2 * HG)], PS[:, 7, 0:P]).then_inc(s_avc.sem, 1)

                def act_unit(i, k, u_min=None):
                    u = i * BODY + k
                    free_run = u_min is None
                    if free_run or 2 <= u_min < UNITS + 2:
                        weight_columns(u - 2, k - 2)
                    if free_run or 3 <= u_min < UNITS + 3:
                        outputs(u - 3, k - 3, i)
                    if free_run or u_min < UNITS:
                        exps(u, k)
                    if k % HG == 0 and (free_run or u_min >= HG):
                        tile = i * (BODY // HG) + (k - HG) // HG
                        act.wait_ge(t_arg.sem, t_arg.item(tile))
                        par = ((k - HG) // HG) % 2
                        nc.scalar.activation(esm[:, par, 1], esm[:, par, 0], ACT.Exp).then_inc(t_exp.sem, 1)

                for k in range(4):
                    act_unit(0, k, k)
                with act.Fori(0, UNITS // BODY - 1) as i:
                    for k in range(4, BODY + 4):
                        act_unit(i, k)
                last = UNITS // BODY - 1
                for k in range(4, BODY + 4):
                    act_unit(last, k, last * BODY + k)
                for c in range(NC):
                    act.wait_ge(b_on_turn.sem, b_on_turn.item(c))
                    nc.scalar.copy(onT[:, c * CH:(c + 1) * CH], PS[:, c]).then_inc(b_on_col.sem, 1)

            if last_phase >= 3:
                attention()
            if last_phase >= 4:
                ffn(1, 3)

        @block.gpsimd
        def _(pool):
            for sig in [a_read]:
                pool.sem_inc(sig.sem, sig.start)
            for sig in [a_sum, s_av, s_turn, s_ot] + [s[0] for s in (f_out, e_up, e_hturn, e_out)]:
                pool.sem_inc(sig.sem, sig.start)
            pool.wait_ge(a_raw.sem, a_raw.item(3 * NC - 1))
            with pool.Fori(0, NC) as c:
                for e in range(DH):
                    n = c * DH + e
                    pool.wait_ge(a_state.sem, a_state.item(n * 2 + 1))
                    pool.wait_ge(a_sum.sem, a_sum.spare(n, 4))
                    take_in(pool)
                    nc.gpsimd.tensor_tensor(zb[:, e % 4], qT[:, bass.ts(c, CH)], hb[:, e % 4], ALU.mult)\
                        .then_inc(a_read.sem, 1)

            def ffn(f):
                pool.wait_ge(ids_set.sem, ids_set.item(0))
                pool.wait_ge(f_cleared[f].sem, f_cleared[f].moved(1))
                pool.wait_ge(f_slots[f].sem, f_slots[f].item(0))
                for n in range(NT):
                    pool.indirect_dma_start(slot_rows[:, :], bass.IndirectOffsetOnAxis(ap=slotu[:, n:n + 1], axis=0),
                                            xn[:, n], None).then_inc(f_sent[f].sem, 16)
                pool.wait_ge(f_ids[f].sem, f_ids[f].moved(1))
                for s in range(SLOT_TILES):
                    pool.wait_ge(e_row[f].sem, e_row[f].item(s))
                    pool.indirect_dma_start(token_out[:, :], bass.IndirectOffsetOnAxis(ap=slot_ids[:, s:s + 1], axis=0),
                                            er[:, s], None, bounds_check=TOK - 1, oob_is_err=False)\
                        .then_inc(e_back[f].sem, 16)

            if last_phase >= 2:
                ffn(0)

            def attention():
                def by_seq(ap):
                    return ap.rearrange("p (b t) -> p b t", t=SEQ)

                def table(col):
                    return C[:, col:col + SEQ].rearrange("p (a t) -> p a t", a=1).to_broadcast([P, SPC, SEQ])

                for c in range(NC + 1):
                    k, n = c % 2, 3 * c
                    if c < NC:
                        if c >= 2:
                            pool.wait_ge(b_lowp.sem, b_lowp.item(c - 2))
                        pool.wait_ge(b_raw.sem, b_raw.item(n + 1))
                        nc.gpsimd.tensor_tensor(by_seq(rot[:, k, 2]), by_seq(raw[:, k, 1]), table(C_COS2), ALU.mult)\
                            .then_inc(b_rotp.sem, 1)
                        nc.gpsimd.tensor_tensor(by_seq(rot[:, k, 3]), by_seq(raw[:, k, 2]), table(C_SIN2), ALU.mult)\
                            .then_inc(b_rotp.sem, 1)
                        pool.wait_ge(b_rotp.sem, b_rotp.item(n + 1))
                        nc.gpsimd.tensor_tensor(rot[:, k, 2], rot[:, k, 2], rot[:, k, 3], ALU.add).then_inc(b_rotp.sem, 1)
                    if c > 0:
                        pool.wait_ge(b_mid.sem, b_mid.item(4 * c - 1))
                        pool.wait_ge(b_restp.sem, b_restp.item(c - 1))
                        nc.gpsimd.tensor_tensor(pb[:, c - 1, 11], rests(c - 1)[3], pb[:, c - 1, 10], ALU.subtract)\
                            .then_inc(b_lowp.sem, 1)
                    if c < NC:
                        pool.wait_ge(b_rotp.sem, b_rotp.item(n + 2))
                        pool.wait_ge(b_hi.sem, b_hi.item(4 * c + 3))
                        nc.gpsimd.tensor_tensor(rot[:, k, 2], rot[:, k, 2], pb[:, c, 9], ALU.subtract)\
                            .then_inc(b_restp.sem, 1)
                pool.wait_ge(b_low.sem, b_low.item(3 * NC - 1))
                pool.wait_ge(b_lowp.sem, b_lowp.item(NC - 1))
                nc.gpsimd.memset(vring.rearrange("p a b w -> p (a b w)"), 0.0).then_inc(b_vpad.sem, 1)
                pool.wait_ge(b_vpad.sem, b_vpad.item(0))
                padded = vring.rearrange("p a b (h w) -> p a b h w", w=VW)
                nc.gpsimd.memset(padded.rearrange("p a b h w -> p (a b h) w")[:, :, DH:DH + 1], 1.0).then_inc(b_vpad.sem, 1)
                pool.wait_ge(b_vpad.sem, b_vpad.item(1))

                def pad_values(b, par):
                    for j in range(QT):
                        ins = nc.gpsimd.tensor_copy(padded[:, par, j, :, 0:DH],
                                                    vals[:, bass.ds(b * QT + j, 1)].rearrange("p a (h d) -> p (a h) d", h=H))
                    ins.then_inc(b_vring.sem, 1)

                for b in range(2):
                    pool.wait_ge(b_tokv.sem, b_tokv.item(2 * (b * QT // 4)))
                    pad_values(b, b)
                pool.wait_ge(b_tokv.sem, b_tokv.item(2 * (NT // 4) - 1))
                with pool.Fori(1, BATCH // 2) as i:
                    for par in range(2):
                        pool.wait_ge(s_av.sem, s_av.spare(i * BODY + ((par + 1) * UPB - 1), BODY))
                        take_in(pool)
                        pad_values(i * 2 + par, par)

            if last_phase >= 3:
                attention()
            if last_phase >= 4:
                ffn(1)


def host_constants():
    f = np.float32
    p = np.arange(P)
    consts = np.zeros((P, C_ALL), f)
    consts[:, C_ID:C_ID + P] = np.eye(P)
    consts[:-1, C_SD:C_SD + P] = -BIG * np.eye(P)[1:]
    consts[:, C_TRI:C_TRI + P] = p[:, None] < p[None, :]
    consts[:, C_ONE:C_ONE + P] = 1
    consts[:, C_IOTA:C_IOTA + NE] = np.arange(NE)
    consts[:, C_THR:C_THR + NE * NT] = np.tile(P * np.arange(NT), NE)
    consts[:, C_SLOT:C_SLOT + SLOT_TILES * NE] = np.repeat(np.arange(SLOT_TILES), NE)
    consts[P - 1, C_LAST:C_LAST + NT] = np.where(np.arange(NT) % QT == QT - 1, -BIG, 0)
    freq = (1.0 / 10000.0 ** (np.arange(0, DH, 2, dtype=f) / f(DH))).astype(f).astype(np.float64)
    pos = np.arange(SEQ)
    half = DH // 2
    dim = p // H
    row_f = freq[dim % half][:, None]
    sign = np.where(dim < half, -1.0, 1.0)[:, None]
    for cos_col, sin_col, ahead in ((C_COS1, C_SIN1, 0), (C_COS2, C_SIN2, SEQ)):
        angle = row_f * (pos + ahead)[None, :]
        consts[:, cos_col:cos_col + SEQ] = sign * np.cos(angle)
        consts[:, sin_col:sin_col + SEQ] = np.sin(angle)
    angle = freq[:, None] * pos[None, :]
    positions = np.concatenate([np.sin(angle), np.cos(angle)]).astype(f)
    head_sums = np.zeros((P, DH, P), f)
    for e in range(DH):
        head_sums[p, e, p // DH * DH + e] = 1
    head_sums = head_sums.reshape(P, DH * P)
    rules = np.zeros((2, H, SEQ), "uint16")
    rules[0, :, P - 1] = 0xF149
    rules[1, :, P] = 0x3F80
    rules = rules.reshape(2, H * SEQ).view(f)
    token_ids = (np.arange(NT)[None, :] * P + p[:, None]).astype(np.int32)
    clear_row = np.zeros((P, ROWW), np.int32)
    clear_row[:, D] = NO_TOKEN
    return dict(head_sums=head_sums, consts=consts, positions=positions, row96=rules,
                token_ids=token_ids, clear_row=clear_row.view(f))


LAST_PHASE = 4


def kernel(**inputs):
    import concourse.bacc as bacc
    from concourse.bass_utils import run_bass_kernel_spmd

    a = {k: np.asarray(v) for k, v in inputs.items()}
    A, B, Fn = (lambda n: a["L0_attn_a_" + n]), (lambda n: a["L0_attn_b_" + n]), (lambda n: a["L0_ffn_" + n])
    swap = np.arange(D) ^ (DH // 2)
    by_dim = np.arange(D).reshape(H, DH).T.reshape(-1)
    u, v = B("u").reshape(-1), B("v").reshape(-1)
    columns = np.stack([A("gamma"), A("beta"), u[by_dim], v[by_dim], v[swap[by_dim]]], 1)
    weights = np.concatenate([A("Wq").T, A("Wk").T, A("Wg").T, A("Wo").T, B("Wq")[:, swap[by_dim]],
                              B("Wq")[:, by_dim], B("Wv"), B("Wk")[:, by_dim], B("Wo"), Fn("Wg"), columns], 1)
    row_head = np.arange(P) // DH * DH
    spread_w = np.stack([A("Wv").T[:, row_head + e] for e in range(DH)], 1).reshape(D, DH * P)
    arrays = dict(
        x_in=A("x").reshape(TOK, D), weights=weights, spread_w=spread_w,
        rows=np.stack([u[by_dim], B("bo")]),
        w1=Fn("W1"), w2=Fn("W2"), w3=Fn("W3"), w1s=Fn("w1s"), w2s=Fn("w2s"), w3s=Fn("w3s"), **host_constants())
    arrays = {k: np.ascontiguousarray(v) for k, v in arrays.items()}
    nc = bacc.Bacc("TRN2", target_bir_lowering=False, num_devices=1)
    aps, feeds = {}, {}
    for name, v in arrays.items():
        aps[name] = nc.dram_tensor(f"{name}_dram", v.shape, mybir.dt.from_np(v.dtype), kind="ExternalInput").ap()
        feeds[f"{name}_dram"] = v
    aps["row96"] = aps["row96"].bitcast(BF16)
    out = nc.dram_tensor("out_dram", (TOK, D), F32, kind="ExternalOutput").ap()
    build_program(nc, out=out, last_phase=LAST_PHASE, **aps)
    r = run_bass_kernel_spmd(nc, [feeds], core_ids=[0])
    return r.results[0]["out_dram"].reshape(BATCH, SEQ, D)
```

```python
from contextlib import ExitStack

import numpy as np

import concourse.bass as bass
from concourse import mybir

ALU = mybir.AluOpType
ACT = mybir.ActivationFunctionType
AX_X = mybir.AxisListType.X
F32 = mybir.dt.float32
BF16 = mybir.dt.bfloat16
U8 = mybir.dt.uint8
U32 = mybir.dt.uint32
I32 = mybir.dt.int32

P = 128
BATCH, SEQ, D = 8, 256, 128
TOK = BATCH * SEQ
NT = TOK // P
QT = SEQ // P
H, DH = 16, 8
INTER = 512
KI = INTER // P
NE = 8
CH = 512
NC = TOK // CH
SPC = CH // SEQ
SLOT_TILES = NT + NE
SLOTS = SLOT_TILES * P
ROWW = D + 1
NO_TOKEN = 1 << 20
EPS = 1e-5
BIG = 1e30
SCALE = float(DH) ** -0.5
RUNS = [3, 2, 1]
NPROD = sum(RUNS)
HALF = NPROD * DH
STK = 2 * HALF
HG = 4
UPB = QT * (H // HG)
UNITS = BATCH * UPB
BODY = 2 * UPB
VW = 32

C_ID, C_EPS = 0, 128
C_FIRST = 129
C_SD, C_TRI, C_ONE, C_HEADS = [C_FIRST + 128 * j for j in range(4)]
C_IOTA = C_HEADS + 2 * 32
C_THR = C_IOTA + NE
C_SLOT = C_THR + NE * NT
C_LAST = C_SLOT + SLOT_TILES * NE
C_COS1 = C_LAST + NT
C_SIN1, C_COS2, C_SIN2 = C_COS1 + SEQ, C_COS1 + 2 * SEQ, C_COS1 + 3 * SEQ
C_ALL = C_COS1 + 4 * SEQ
W_Q, W_K, W_G, W_O, W_BS, W_BQ, W_BV, W_BK, W_BO, W_R = [128 * j for j in range(10)]
W_COL = W_R + 32
W_ALL = W_COL + 5


class Signal:

    def __init__(self, sem, start=0):
        self.sem, self.start = sem, start

    def item(self, n):
        return n + (self.start + 1)

    def spare(self, n, ring):
        return n + (self.start + 1 - ring)

    def moved(self, n):
        return 16 * n + self.start


def build_program(nc, x_in, weights, spread_w, consts, rows, positions, row96,
                  token_ids, clear_row, w1, w2, w3, w1s, w2s, w3s, out, last_phase=4):
    with ExitStack() as ctx:
        def sb(name, shape, dt=F32):
            return ctx.enter_context(nc.sbuf_tensor(name, shape, dt))

        def signal(name, start=0):
            return Signal(ctx.enter_context(nc.semaphore(name)), start)

        def dram(name, shape, dt=F32):
            return nc.dram_tensor(name, shape, dt, kind="Internal").ap()

        def take_in(eng):
            eng.sem_inc(waits_taken.sem, 1)

        x = sb("x", [P, NT, D])
        xn = sb("xn", [P, NT, ROWW])
        xT = sb("xT", [P, TOK + P])
        W = sb("W", [P, W_ALL])
        C = sb("C", [P, C_ALL])
        w12 = sb("w12", [P, NE + 1, 2 * INTER])
        w3t = sb("w3t", [P, NE + 1, KI, D])
        stats = sb("stats", [P, NT, 6])
        mean_var = sb("mean_var", [P, NT, 2])
        spread = sb("spread", [P, 3, NT])
        cb = sb("cb", [P, 4, P], BF16)
        crow = sb("crow", [P, ROWW])
        one8b = sb("one8b", [P, NT * NE], BF16)
        slotu = sb("slotu", [P, NT], U32)
        slot_ids = sb("slot_ids", [P, SLOT_TILES], U32)
        idsb = sb("idsb", [P, NT], I32)
        eword = sb("eword", [P, SLOT_TILES], I32)
        nsd = sb("nsd", [P, NT, H])
        nsd_now = sb("nsd_now", [P, 2, H])
        nmax = sb("nmax", [P, 2, H])
        mxs = sb("mxs", [P, 2, HG])
        esm = sb("esm", [P, 2, 4, H])
        msk = sb("msk", [P, 2, HG, P], U8)
        rowb = sb("rowb", [P, 2, D])
        rpos = sb("rpos", [DH, 2, SEQ])
        rpb = sb("rpb", [DH, 3, SEQ], BF16)
        arena = sb("arena", [P, 24700])
        used = [0]

        def cut(*shape, dt=F32):
            n = int(np.prod(shape))
            words = n if dt == F32 else n // 2
            ap = arena[:, used[0]:used[0] + words]
            used[0] += words
            assert used[0] <= 24700
            if dt != F32:
                ap = ap.bitcast(dt)
            names = "abcd"[:len(shape)]
            if len(shape) == 1:
                return ap
            return ap.rearrange(f"p ({' '.join(names)}) -> p {' '.join(names)}", **dict(zip(names, shape)))

        aT, qT, kT, yT = cut(TOK), cut(TOK), cut(TOK), cut(TOK)
        wv = cut(DH * P)
        kvb, hb, zb = cut(2, CH), cut(4, CH), cut(8, CH)
        ynT = cut(TOK)
        yn = xn[:, :, 0:D]
        used[0] = 0
        gk, hT, lgT = cut(2, CH), cut(KI, CH), cut(CH)
        xr, xrT = cut(4, ROWW), cut(4, P)
        eg, eh, ehT, er = cut(2, CH), cut(2, CH), cut(2, CH), cut(SLOT_TILES, D)
        yback = cut(NT, D)
        mx8, ix8f, ixf, one8 = cut(NT, 8), cut(NT, 8), cut(NT), cut(NT, NE)
        ix8 = ix8f.bitcast(U32)
        tot, csum, cmp8 = cut(NE, NT), cut(NE, NT), cut(NE, NT)
        base, work, cnt8 = cut(NE, NT), cut(NT, NE), cut(6, NE)
        slotf, ecmp, eidf = cut(NT), cut(SLOT_TILES, NE), cut(2, SLOT_TILES)
        used[0] = 0
        vnext = cut(NT, D)
        after_shared = used[0]
        raw = cut(2, 4, CH)
        rot = cut(2, 4, CH)
        after_raw = used[0]
        pb = cut(NC, 12, CH, dt=BF16)
        used[0] = after_shared
        prT = cut(2, HG, QT * P)
        vring = cut(2, QT, H * VW)
        pr = cut(2, HG, SEQ)
        osb, otok, t4 = cut(2 * HG, P), cut(2, H, 9), cut(2, D)
        assert used[0] <= after_raw
        used[0] = after_raw
        stacks = cut(2, 3, H, SEQ, dt=BF16)
        kst, qlo, qup = stacks[:, :, 0], stacks[:, :, 1], stacks[:, :, 2]
        vals = cut(NT, D)
        on = xn[:, :, 0:D]
        onT = xT[:, 0:TOK]

        PS = ctx.enter_context(nc.psum_tensor("PS", [P, 8, 512], F32))
        ident = C[:, C_ID:C_ID + P]

        slot_rows = dram("slot_rows", [SLOTS, ROWW])
        token_out = dram("token_out", [TOK, D])
        query_parts = dram("query_parts", [3, 3, P, TOK + P], BF16)
        key_parts = dram("key_parts", [NPROD, P, TOK], BF16)
        pos_parts = dram("pos_parts", [NPROD, DH, SEQ], BF16)

        ident_here, weights_here, consts_here, ids_here = [signal(n) for n in
            ("ident_here", "weights_here", "consts_here", "ids_here")]
        x_here = [signal(f"x_here{c}") for c in range(NC)]
        a_here, ffn_here, b_here, clear_here = [signal(n) for n in ("a_here", "ffn_here", "b_here", "clear_here")]
        consts_cast, ids_set = signal("consts_cast"), signal("ids_set")
        out_stored = signal("out_stored")
        pad_set = signal("pad_set")
        waits_taken = signal("waits_taken")
        dve_order = signal("dve_order")
        steps = [0]

        ln_var = [signal(f"ln{l}_var") for l in range(5)]
        ln_std = [signal(f"ln{l}_std") for l in range(5)]
        ln_rstd = [signal(f"ln{l}_rstd") for l in range(5)]
        ln_rows = [signal(f"ln{l}_rows") for l in range(5)]
        ln_turned = [signal(f"ln{l}_turned") for l in range(5)]
        ln_cols = [signal(f"ln{l}_cols") for l in range(5)]

        a_proj = signal("a_proj")
        a_qk, a_gate = signal("a_qk", 2), signal("a_gate", 1)
        a_value = signal("a_value")
        a_kv = signal("a_kv", 4)
        a_state = signal("a_state", 4)
        a_read = signal("a_read", 4)
        a_sum = signal("a_sum", 2)
        a_y = signal("a_y", 1)
        a_yrow, a_out, a_res = signal("a_yrow"), signal("a_out"), signal("a_res")

        def per_layer(name, items, start=0):
            first = signal(f"f_{name}", start)
            return [first, Signal(first.sem, start + items)]

        f_router, f_lgcols = per_layer("router", 1), per_layer("lgcols", 1)
        f_logits, f_onehot, f_prefix = per_layer("logits", 1), per_layer("onehot", 1), per_layer("prefix", 1)
        f_slots, f_experts = per_layer("slots", 1), per_layer("experts", 1)
        f_cleared, f_sent, f_ids = per_layer("cleared", 16), per_layer("sent", 16 * NT), per_layer("ids", 16)
        f_gate, f_up = per_layer("gate", NC * KI), per_layer("up", NC * KI)
        f_gelu, f_hid = per_layer("gelu", NC * KI, 2), per_layer("hid", NC * KI, 4)
        f_out, f_res = per_layer("out", NC * KI, 4), per_layer("res", NC, 1)
        st = SLOT_TILES
        e_in = list(zip(*[per_layer(f"e_in{k}", 4 * st) for k in range(4)]))
        e_turn, e_col = per_layer("e_turn", st), per_layer("e_col", st, 4)
        e_gate, e_up = per_layer("e_gate", st), per_layer("e_up", st, 4)
        e_gelu, e_hid = per_layer("e_gelu", st, 2), per_layer("e_hid", st, 2)
        e_hturn, e_hcol = per_layer("e_hturn", st, 2), per_layer("e_hcol", st, 2)
        e_out, e_row = per_layer("e_out", st, 2), per_layer("e_row", st, 4)
        e_back = per_layer("e_back", 16 * st)
        f_back, f_done = list(zip(*[per_layer(f"back{c}", 16) for c in range(NC)])), per_layer("done", NC)

        b_proj, b_raw = signal("b_proj"), signal("b_raw")
        b_rot, b_rotp = signal("b_rot"), signal("b_rotp")
        b_hi, b_mid = signal("b_hi"), signal("b_mid")
        b_rest, b_restp = signal("b_rest"), signal("b_restp")
        b_low, b_lowp = signal("b_low"), signal("b_lowp")
        b_parts = [signal(f"b_parts{c}") for c in range(NC)]
        b_pos, b_pos_out = signal("b_pos"), signal("b_pos_out")
        b_tok, b_tokv, b_tokd = signal("b_tok"), signal("b_tokv"), signal("b_tokd")
        b_tsum, b_nsd = signal("b_tsum"), signal("b_nsd")
        b_vpad, b_vring = signal("b_vpad"), signal("b_vring")
        b_stack = [signal(f"b_stack{k}") for k in range(2)]
        s_scores, s_pick, s_max, s_nmax = signal("s_scores"), signal("s_pick", 1), signal("s_max"), signal("s_nmax")
        s_exp = signal("s_exp", 8)
        s_turn, s_col = signal("s_turn", 4), signal("s_col", 4)
        s_av, s_avc = signal("s_av", 2), signal("s_avc", 1)
        s_ot, s_otc = signal("s_ot", 2), signal("s_otc", 1)
        t_arg, t_exp, t_den, t_rden = signal("t_arg"), signal("t_exp", 2), signal("t_den"), signal("t_rden")
        t_v, t_sum, t_on = signal("t_v"), signal("t_sum"), signal("t_on", 2)
        t_nsd, t_bias = signal("t_nsd"), signal("t_bias")
        b_on_turn, b_on_col, b_out, b_res = signal("b_on_turn"), signal("b_on_col"), signal("b_out"), signal("b_res")

        N_STORE = 3 + len(RUNS)
        N_CONST = 3
        N_BATCH = 4 * len(RUNS) + 1

        def rests(c):
            k = c % 2
            return raw[:, k, 0], raw[:, k, 3], rot[:, k, 0], rot[:, k, 2]

        block = ctx.enter_context(nc.Block())

        @block.sync
        def _(sp):
            def load(dst, src, sig):
                sp.dma_start(dst, src).then_inc(sig.sem, 16)

            load(C[:, 0:C_FIRST], consts[:, 0:C_FIRST], ident_here)
            for c in range(NC):
                load(x[:, 4 * c:4 * c + 4], x_in.rearrange("(n p) d -> p n d", p=P)[:, 4 * c:4 * c + 4], x_here[c])
            load(W[:], weights, weights_here)
            load(wv, spread_w, a_here)
            load(C[:, C_FIRST:], consts[:, C_FIRST:], consts_here)
            load(idsb[:], token_ids, ids_here)
            load(crow[:], clear_row, clear_here)
            load(w12[:, NE, 0:INTER], w1s, ffn_here)
            load(w12[:, NE, INTER:], w2s, ffn_here)
            load(w3t[:, NE], w3s.rearrange("(k p) n -> p k n", p=P), ffn_here)
            load(w12[:, 0:NE, 0:INTER], w1.rearrange("e d n -> d e n"), ffn_here)
            load(w12[:, 0:NE, INTER:], w2.rearrange("e d n -> d e n"), ffn_here)
            for e in range(NE):
                load(w3t[:, e], w3[e].rearrange("(k p) n -> p k n", p=P), ffn_here)
            load(rowb[:, 0], rows[0:1, :].to_broadcast([P, D]), b_here)
            load(rowb[:, 1], rows[1:2, :].to_broadcast([P, D]), b_here)
            load(rpos[:, 0], positions, b_here)
            rows_v = slot_rows.rearrange("(s p) d -> s p d", p=P)

            def clear(f):
                sp.wait_ge(clear_here.sem, clear_here.moved(1))
                load(slot_rows.rearrange("(s p) d -> p s d", p=P),
                     crow[:].rearrange("p (a d) -> p a d", a=1).to_broadcast([P, SLOT_TILES, ROWW]), f_cleared[f])

            clear(0)

            def ffn(f):
                sp.wait_ge(f_sent[f].sem, f_sent[f].moved(NT))
                for s in range(4):
                    load(xr[:, s], rows_v[s], e_in[f][s])
                with nc.allow_non_contiguous_dma(reason="one number of every slot"):
                    load(slot_ids[:], slot_rows.rearrange("(s p) d -> p s d", p=P)[:, :, D].bitcast(U32), f_ids[f])
                with sp.Fori(1, SLOT_TILES // 4) as i:
                    for k in range(4):
                        sp.wait_ge(e_turn[f].sem, e_turn[f].spare(i * 4 + k, 4))
                        take_in(sp)
                        load(xr[:, k], rows_v[bass.ds(i * 4 + k, 1)].rearrange("a p d -> p (a d)"), e_in[f][k])
                sp.wait_ge(e_back[f].sem, e_back[f].moved(SLOT_TILES))
                for c in range(NC):
                    load(yback[:, 4 * c:4 * c + 4], token_out.rearrange("(n p) d -> p n d", p=P)[:, 4 * c:4 * c + 4],
                         f_back[f][c])

            if last_phase >= 2:
                ffn(0)
            if last_phase >= 4:
                for k in range(4):
                    sp.wait_ge(e_in[0][k].sem, e_in[0][k].moved(SLOT_TILES // 4))
                sp.wait_ge(f_ids[0].sem, f_ids[0].moved(1))
                clear(1)
            if last_phase >= 3:
                sp.wait_ge(b_pos.sem, b_pos.item(3))
                def repeated(part, run):
                    rows, wide = part.shape
                    return part.rearrange("p (a t) -> p a t", a=1).to_broadcast([rows, run, wide])

                first = 0
                for j, run in enumerate(RUNS):
                    load(pos_parts[first:first + run].rearrange("c d t -> d c t"), repeated(rpb[:, j], run), b_pos_out)
                    first += run
                sp.wait_ge(pad_set.sem, pad_set.item(0))
                load(query_parts[2].rearrange("c p t -> p c t")[:, :, TOK:TOK + P],
                     repeated(xT[:, TOK:TOK + P].bitcast(BF16)[:, 0:P], 3), b_pos_out)
                def store_parts(c):
                    sp.wait_ge(b_mid.sem, b_mid.item(4 * c + 3))
                    sp.wait_ge(b_low.sem, b_low.item(3 * c + 2))
                    sp.wait_ge(b_lowp.sem, b_lowp.item(c))
                    here = slice(c * CH, (c + 1) * CH)
                    for t, src in enumerate((0, 2, 3)):
                        load(query_parts[t].rearrange("c p t -> p c t")[:, :, here],
                             pb[:, c, 3 * src:3 * src + 3], b_parts[c])
                    first = 0
                    for j, run in enumerate(RUNS):
                        load(key_parts[first:first + run].rearrange("c p t -> p c t")[:, :, here],
                             repeated(pb[:, c, 3 + j], run), b_parts[c])
                        first += run
                def load_stacks(b, par):
                    load(kst[0:HALF, par],
                         key_parts.rearrange("c (d h) t -> (c d) h t", d=DH)[:, :, bass.ds(b * SEQ, SEQ)],
                         b_stack[par])
                    for dst, half, t, ahead in ((qup, 0, 0, 0), (qup, 1, 2, 1), (qlo, 0, 0, 0), (qlo, 1, 1, 0)):
                        r0 = half * HALF
                        for run in RUNS:
                            load(dst[r0:r0 + run * DH, par],
                                 query_parts[t, 0:run].rearrange("c (d h) t -> (c d) h t", d=DH)
                                 [:, :, bass.ds(b * SEQ + ahead, SEQ)], b_stack[par])
                            r0 += run * DH

                for par in range(2):
                    for c in (2 * par, 2 * par + 1):
                        store_parts(c)
                    for c in (2 * par, 2 * par + 1):
                        sp.wait_ge(b_parts[c].sem, b_parts[c].moved(N_STORE))
                    if par == 0:
                        sp.wait_ge(b_pos_out.sem, b_pos_out.moved(len(RUNS) + 1))
                    load(qup[STK:STK + 1, par], row96[0:1].rearrange("a (h t) -> a h t", h=H), b_stack[par])
                    load(kst[STK:STK + 1, par], row96[1:2].rearrange("a (h t) -> a h t", h=H), b_stack[par])
                    load(kst[HALF:STK, par], pos_parts.rearrange("c d (a t) -> (c d) a t", a=1)
                         .to_broadcast([HALF, H, SEQ]), b_stack[par])
                    load_stacks(par, par)
                with sp.Fori(1, BATCH // 2) as i:
                    for par in range(2):
                        sp.wait_ge(s_scores.sem, s_scores.spare(i * BODY + ((par + 1) * UPB - 1), BODY))
                        take_in(sp)
                        load_stacks(i * 2 + par, par)
            if last_phase >= 4:
                ffn(1)
            sp.wait_ge(b_here.sem, b_here.moved(3))
            sp.wait_ge(ffn_here.sem, ffn_here.moved(5 + NE))
            final = {1: a_res, 2: f_done[0], 3: b_res, 4: f_done[1]}[last_phase]
            for c in range(NC):
                sp.wait_ge(final.sem, final.item(c))
                load(out.rearrange("(n p) d -> p n d", p=P)[:, 4 * c:4 * c + 4], x[:, 4 * c:4 * c + 4], out_stored)
            sp.wait_ge(out_stored.sem, out_stored.moved(NC))

        @block.tensor
        def _(pe):
            def turn_tiles(l, c, src, bank0=0):
                pe.wait_ge(ln_rows[l].sem, ln_rows[l].item(c))
                for n in range(4 * c, 4 * c + 4):
                    ins = nc.tensor.transpose(PS[:, bank0 + c, (n % 4) * P:(n % 4 + 1) * P], src(n), ident)
                ins.then_inc(ln_turned[l].sem, 1)

            def stream_turn(l):
                for c in range(NC):
                    turn_tiles(l, c, lambda n: xn[:, n, 0:D])

            pe.wait_ge(ident_here.sem, ident_here.moved(1))
            stream_turn(0)
            pe.wait_ge(weights_here.sem, weights_here.moved(1))

            def project(c, j):
                if j == 0:
                    pe.wait_ge(ln_cols[0].sem, ln_cols[0].item(c))
                if j < 2:
                    pe.wait_ge(a_qk.sem, a_qk.spare(c * 2 + j, 2))
                else:
                    pe.wait_ge(a_gate.sem, a_gate.spare(c, 1))
                w = (W_Q, W_K, W_G)[j]
                nc.tensor.matmul(PS[:, 5 + j], W[:, w:w + P], xT[:, bass.ts(c, CH)],
                                 start=True, stop=True).then_inc(a_proj.sem, 1)

            def spread(c, e):
                pe.wait_ge(a_kv.sem, a_kv.spare(c * DH + e, 4))
                nc.tensor.matmul(PS[:, e % 4], wv[:, e * P:(e + 1) * P], xT[:, bass.ts(c, CH)],
                                 start=True, stop=True).then_inc(a_value.sem, 1)

            def summed(c, g):
                pe.wait_ge(a_read.sem, a_read.item(c * DH + 4 * g + 3))
                if g == 0:
                    pe.wait_ge(a_y.sem, a_y.spare(c, 1))
                for j in range(4):
                    ins = nc.tensor.matmul(PS[32 * j:32 * (j + 1), 4], C[:, C_HEADS + 32 * g:C_HEADS + 32 * (g + 1)],
                                           zb[:, 4 * g + j], start=(g == 0), stop=(g == 1),
                                           tile_position=(0, 32 * j), skip_group_check=True)
                ins.then_inc(a_sum.sem, 1)

            for j in range(3):
                project(0, j)
            pe.wait_ge(a_here.sem, a_here.moved(1))
            for e in range(4):
                pe.wait_ge(ln_cols[0].sem, ln_cols[0].item(e))
                spread(0, e)
            pe.wait_ge(consts_here.sem, consts_here.moved(1))
            with pe.Fori(0, NC - 1) as c:
                for g in range(2):
                    for e in range(4):
                        spread(c + g, 4 * (1 - g) + e)
                        if g == 0 and e < 3:
                            project(c + 1, e)
                    summed(c, g)
            for e in range(4, DH):
                spread(NC - 1, e)
            for g in range(2):
                summed(NC - 1, g)
            pe.wait_ge(a_kv.sem, a_kv.item(NC * DH - 1))
            for n in range(NT):
                if n % 4 == 0:
                    pe.wait_ge(a_y.sem, a_y.item(n // 4))
                ins = nc.tensor.transpose(PS[:, n // 4, (n % 4) * P:(n % 4 + 1) * P], yT[:, n * P:(n + 1) * P], ident)
                if n % 4 == 3:
                    ins.then_inc(a_yrow.sem, 1)
            for c in range(NC + 1):
                if c < NC:
                    turn_tiles(4, c, lambda n: yn[:, n], bank0=4)
                if c > 0:
                    pe.wait_ge(ln_cols[4].sem, ln_cols[4].item(c - 1))
                    for n in range(4 * (c - 1), 4 * c):
                        ins = nc.tensor.matmul(PS[:, n // 4, (n % 4) * P:(n % 4 + 1) * P], ynT[:, n * P:(n + 1) * P],
                                               W[:, W_O:W_O + D], start=True, stop=True)
                    ins.then_inc(a_out.sem, 1)

            def ffn(f, l):
                def shared_out(c, k):
                    pe.wait_ge(f_hid[f].sem, f_hid[f].item(c * KI + k))
                    if k == 0:
                        pe.wait_ge(f_res[f].sem, f_res[f].spare(c, 1))
                    for t in range(4):
                        ins = nc.tensor.matmul(PS[:, 4, t * P:(t + 1) * P], hT[:, k, t * P:(t + 1) * P],
                                               w3t[:, NE, k], start=(k == 0 and t == 0), stop=(k == KI - 1),
                                               skip_group_check=True)
                    ins.then_inc(f_out[f].sem, 1)

                def shared_gate(c, k):
                    pe.wait_ge(f_gelu[f].sem, f_gelu[f].spare(c * KI + k, 2))
                    nc.tensor.matmul(PS[:, k % 2], w12[:, NE, k * P:(k + 1) * P], xT[:, bass.ts(c, CH)],
                                     start=True, stop=True).then_inc(f_gate[f].sem, 1)

                def shared_up(c, k):
                    pe.wait_ge(f_hid[f].sem, f_hid[f].spare(c * KI + k, 2))
                    nc.tensor.matmul(PS[:, 2 + k % 2], w12[:, NE, INTER + k * P:INTER + (k + 1) * P],
                                     xT[:, bass.ts(c, CH)], start=True, stop=True).then_inc(f_up[f].sem, 1)

                def shared_step(c, k):
                    shared_gate(c, k)
                    shared_up(c, k)
                    if k > 0:
                        shared_out(c, k - 1)

                def shared(c):
                    for k in range(KI):
                        shared_step(c, k)
                    shared_out(c, KI - 1)

                for c in range(NC - 1):
                    turn_tiles(l, c, lambda n: xn[:, n, 0:D])
                pe.wait_ge(ffn_here.sem, ffn_here.moved(5 + NE))
                pe.wait_ge(ln_cols[l].sem, ln_cols[l].item(0))
                shared_gate(0, 0)
                turn_tiles(l, NC - 1, lambda n: xn[:, n, 0:D])
                for c in range(NC):
                    pe.wait_ge(ln_cols[l].sem, ln_cols[l].item(c))
                    ins = nc.tensor.matmul(PS[32 * c:32 * (c + 1), 6], W[:, W_R:W_R + 32], xT[:, c * CH:(c + 1) * CH],
                                           start=True, stop=True, tile_position=(0, 32 * c), skip_group_check=True)
                ins.then_inc(f_router[f].sem, 1)
                shared_up(0, 0)
                pe.wait_ge(f_lgcols[f].sem, f_lgcols[f].item(0))
                for b in range(4):
                    ins = nc.tensor.transpose(PS[:, 7, b * P:(b + 1) * P], lgT[:, b * P:(b + 1) * P], ident)
                ins.then_inc(f_logits[f].sem, 1)
                shared_gate(0, 1)
                shared_up(0, 1)
                shared_out(0, 0)
                shared_step(0, 2)
                pe.wait_ge(f_onehot[f].sem, f_onehot[f].item(0))
                pe.wait_ge(consts_cast.sem, consts_cast.item(3))
                nc.tensor.matmul(PS[:, 6, 0:NT * NE], cb[:, 2], one8b[:], start=True, stop=True)
                nc.tensor.matmul(PS[:, 7, 0:NT * NE], cb[:, 3], one8b[:], start=True,
                                 stop=True).then_inc(f_prefix[f].sem, 1)
                shared_step(0, 3)
                shared_out(0, 3)
                shared(1)

                def turn_in(s, k):
                    wait_tile(s, k)
                    pe.wait_ge(e_col[f].sem, e_col[f].spare(s, 1))
                    nc.tensor.transpose(PS[:, 6, 0:P], xr[:, k, 0:D], ident).then_inc(e_turn[f].sem, 1)

                def wait_tile(s, k):
                    pe.wait_ge(e_in[f][k].sem, (s - k) * 4 + (16 + e_in[f][k].start))

                def gate(s, k, e):
                    pe.wait_ge(e_col[f].sem, e_col[f].item(s))
                    pe.wait_ge(e_gelu[f].sem, e_gelu[f].spare(s, 2))
                    nc.tensor.matmul(PS[:, k % 2], xrT[:, k], w12[:, e, 0:INTER],
                                     start=True, stop=True).then_inc(e_gate[f].sem, 1)

                def up(s, k, e):
                    pe.wait_ge(e_hid[f].sem, e_hid[f].spare(s, 2))
                    nc.tensor.matmul(PS[:, 2 + k % 2], xrT[:, k], w12[:, e, INTER:2 * INTER],
                                     start=True, stop=True).then_inc(e_up[f].sem, 1)

                def turn_hidden(s, k):
                    pe.wait_ge(e_hid[f].sem, e_hid[f].item(s))
                    pe.wait_ge(e_hcol[f].sem, e_hcol[f].spare(s, 2))
                    for j in range(KI):
                        ins = nc.tensor.transpose(PS[:, 4 + k % 2, j * P:(j + 1) * P],
                                                  eh[:, k % 2, j * P:(j + 1) * P], ident)
                    ins.then_inc(e_hturn[f].sem, 1)

                def down(s, k, e):
                    pe.wait_ge(e_hcol[f].sem, e_hcol[f].item(s))
                    pe.wait_ge(e_row[f].sem, e_row[f].spare(s, 1))
                    for j in range(KI):
                        ins = nc.tensor.matmul(PS[:, 7, 0:P], ehT[:, k % 2, j * P:(j + 1) * P],
                                               w3t[:, e, j], start=(j == 0), stop=(j == KI - 1))
                    ins.then_inc(e_out[f].sem, 1)

                def expert_of(word, j):
                    return (word // NE ** j) % NE

                def step(i, k, word, j0, s_min=None):
                    s = i * 4 + k
                    free_run = s_min is None
                    if free_run or s_min + 1 < SLOT_TILES:
                        turn_in(s + 1, (k + 1) % 4)
                    enters = free_run or s_min < SLOT_TILES
                    if enters:
                        gate(s, k % 4, expert_of(word, k - j0))
                    if free_run or s_min >= 2:
                        down(s - 2, (k - 2) % 4, expert_of(word, k - 2 - j0))
                    if enters:
                        up(s, k % 4, expert_of(word, k - j0))
                    if free_run or 1 <= s_min < SLOT_TILES + 1:
                        turn_hidden(s - 1, (k - 1) % 4)

                def load_word(s):
                    return pe.value_load(eword[0:1, bass.ds(s, 1)], min_val=0, max_val=NE ** 6 - 1)

                pe.wait_ge(f_experts[f].sem, f_experts[f].item(0))
                word = load_word(0)
                for k in range(KI):
                    shared_step(2, k)
                pe.wait_ge(f_slots[f].sem, f_slots[f].item(0))
                turn_in(0, 0)
                shared_out(2, KI - 1)
                step(0, 0, word, 0, 0)
                pe.wait_ge(f_res[f].sem, f_res[f].item(2))
                step(0, 1, word, 0, 1)
                with pe.Fori(0, SLOT_TILES // 4 - 1) as i:
                    word = load_word(i * 4)
                    for k in range(2, 6):
                        step(i, k, word, 0)
                word = load_word(SLOT_TILES - 4)
                for s in range(SLOT_TILES - 2, SLOT_TILES + 2):
                    step(0, s, word, SLOT_TILES - 4, s)
                shared(NC - 1)

            if last_phase >= 2:
                ffn(0, 1)

            def attention():
                stream_turn(2)
                pe.wait_ge(ln_cols[2].sem, ln_cols[2].item(NC - 1))
                pe.wait_ge(pad_set.sem, pad_set.item(0))
                for c in range(NC + 1):
                    for j, w in enumerate((W_BQ, W_BS, W_BK) if c < NC else ()):
                        if c > 0:
                            pe.wait_ge(b_raw.sem, b_raw.item((c - 1) * 3 + j))
                        nc.tensor.matmul(PS[:, 4 + j], W[:, w:w + P], xT[:, c * CH:(c + 1) * CH],
                                         start=True, stop=True).then_inc(b_proj.sem, 1)
                    if c > 1:
                        pe.wait_ge(b_tokd.sem, b_tokd.item(2 * c - 3))
                        pe.wait_ge(b_tokv.sem, b_tokv.item(2 * c - 3))
                    for n in range(4 * c - 4, 4 * c) if c > 0 else ():
                        for j, (ahead, w) in enumerate(((0, W_BQ), (1, W_BK), (0, W_BV), (1, W_BV))):
                            ins = nc.tensor.matmul(PS[:, j, n % 4 * D:(n % 4 + 1) * D],
                                                   xT[:, n * P + ahead:(n + 1) * P + ahead], W[:, w:w + D],
                                                   start=True, stop=True)
                        if n % 4 == 3:
                            ins.then_inc(b_tok.sem, 1)
                pe.wait_ge(b_tokd.sem, b_tokd.item(2 * (NT // 4) - 1))
                pe.wait_ge(b_tokv.sem, b_tokv.item(2 * (NT // 4) - 1))

                def scores(i, k, tile_out):
                    u = i * BODY + k
                    k = k % BODY
                    par, qt, hg = k // UPB, (k // HG) % QT, k % HG
                    if k % UPB == 0:
                        pe.wait_ge(b_stack[par].sem, i * (16 * N_BATCH) + 16 * (N_CONST + N_BATCH))
                    q = slice(qt * P, (qt + 1) * P)
                    main = PS[:, 2 * (k % 2):2 * (k % 2) + 2].rearrange("p a (b j) -> p (a b) j", b=2)

                    def all_keys():
                        for a in range(HG):
                            h = HG * hg + a
                            if a % 2 == 0:
                                pe.wait_ge(s_exp.sem, s_exp.spare(u * HG + (a + 1), 2 * HG))
                            if qt == 0:
                                nc.tensor.matmul(main[:, a], qup[0:STK + 1, par, h, q], kst[0:STK + 1, par, h],
                                                 start=(a % 2 == 0), stop=False, skip_group_check=True)
                                ins = nc.tensor.matmul(main[:, a, 0:P], cb[:, 0], cb[:, 1],
                                                       start=False, stop=True, skip_group_check=True)
                            else:
                                ins = nc.tensor.matmul(main[:, a], qlo[0:STK, par, h, q], kst[0:STK, par, h],
                                                       start=(a % 2 == 0), stop=True, skip_group_check=True)
                        return ins

                    def other_side():
                        pe.wait_ge(s_pick.sem, s_pick.spare(u, 1))
                        if tile_out is not None:
                            pe.wait_ge(s_otc.sem, s_otc.item(tile_out))
                        for a in range(HG):
                            h = HG * hg + a
                            other = PS[:, 4, a * P:(a + 1) * P]
                            if qt == 0:
                                ins = nc.tensor.matmul(other, qlo[0:STK, par, h, q], kst[0:STK, par, h, q],
                                                       start=(a == 0), stop=True, skip_group_check=True)
                            else:
                                nc.tensor.matmul(other, qup[0:STK + 1, par, h, q], kst[0:STK + 1, par, h, q],
                                                 start=(a == 0), stop=False, skip_group_check=True)
                                ins = nc.tensor.matmul(other, cb[:, 0], cb[:, 1], start=False, stop=True,
                                                       skip_group_check=True)
                        return ins

                    if tile_out is None:
                        other_side()
                        ins = all_keys()
                    else:
                        all_keys()
                        ins = other_side()
                    ins.then_inc(s_scores.sem, 1)

                def turn(u, k):
                    k = k % BODY
                    for a in range(HG):
                        pe.wait_ge(s_exp.sem, s_exp.item(u * HG + a))
                        if a % 2 == 0:
                            pe.wait_ge(s_col.sem, s_col.spare(u * 2 + a // 2, 2))
                        for j in range(QT):
                            ins = nc.tensor.transpose(PS[:, 5 + a // 2, ((a % 2) * QT + j) * P:((a % 2) * QT + j + 1) * P],
                                                      pr[:, k % 2, a, j * P:(j + 1) * P], ident)
                        if a % 2 == 1:
                            ins.then_inc(s_turn.sem, 1)

                def weigh(i, k):
                    u = i * BODY + k
                    k = k % BODY
                    par, hg = k // UPB, k % HG
                    pe.wait_ge(s_col.sem, s_col.item(u * 2 + 1))
                    if k % UPB == 0:
                        pe.wait_ge(b_vring.sem, b_vring.item(i * 2 + par))
                    pe.wait_ge(s_avc.sem, s_avc.spare(u, 1))
                    for j in range(QT):
                        for a in range(HG):
                            h = HG * hg + a
                            ins = nc.tensor.matmul(PS[VW * a:VW * (a + 1), 7, 0:P],
                                                   vring[:, par, j, h * VW:(h + 1) * VW],
                                                   prT[:, k % 2, a, j * P:(j + 1) * P],
                                                   start=(j == 0), stop=(j == QT - 1), tile_position=(0, VW * a),
                                                   skip_group_check=True)
                    ins.then_inc(s_av.sem, 1)

                def turn_out(i, k, u_min):
                    pe.wait_ge(s_avc.sem, s_avc.item(i * BODY + (k - 5)))
                    pe.wait_ge(s_otc.sem, s_otc.spare(i * (BODY // HG) + (k - 8) // HG, 1))
                    pe.wait_ge(s_pick.sem, s_pick.item(i * BODY + (k - 1) if u_min is None else min(u_min, UNITS) - 1))
                    for a in range(HG):
                        ins = nc.tensor.transpose(PS[:, 4, a * P:(a + 1) * P], osb[:, (k - 8 + a) % (2 * HG)], ident)
                    ins.then_inc(s_ot.sem, 1)

                def step(i, k, u_min=None):
                    u = i * BODY + k
                    free_run = u_min is None
                    turns = k % HG == 0 and (free_run or u_min >= 8)
                    if turns:
                        turn_out(i, k, u_min)
                    if free_run or u_min < UNITS:
                        tile_out = i * (BODY // HG) + (k - 8) // HG if turns else None
                        if k >= BODY:
                            scores(i + 1, k - BODY, tile_out)
                        else:
                            scores(i, k, tile_out)
                    if free_run or 2 <= u_min < UNITS + 2:
                        turn(u - 2, k - 2)
                    if free_run or 3 <= u_min < UNITS + 3:
                        weigh(i, k - 3) if k - 3 < BODY else weigh(i + 1, k - 3 - BODY)

                for k in range(5):
                    step(0, k, k)
                with pe.Fori(0, UNITS // BODY - 1) as i:
                    for k in range(5, BODY + 5):
                        step(i, k)
                last = UNITS // BODY - 1
                for k in range(5, BODY + 5):
                    step(last, k, last * BODY + k)

                for n in range(NT):
                    if n % 4 == 0:
                        pe.wait_ge(t_on.sem, t_on.item(n + 3))
                    ins = nc.tensor.transpose(PS[:, n // 4, (n % 4) * P:(n % 4 + 1) * P], on[:, n], ident)
                    if n % 4 == 3:
                        ins.then_inc(b_on_turn.sem, 1)
                for n in range(NT):
                    if n % 4 == 0:
                        pe.wait_ge(b_on_col.sem, b_on_col.item(n // 4))
                    ins = nc.tensor.matmul(PS[:, 4 + n // 4, (n % 4) * P:(n % 4 + 1) * P], onT[:, n * P:(n + 1) * P],
                                           W[:, W_BO:W_BO + D], start=True, stop=True)
                    if n % 4 == 3:
                        ins.then_inc(b_out.sem, 1)

            if last_phase >= 3:
                attention()
            if last_phase >= 4:
                ffn(1, 3)

        @block.vector
        def _(dve):
            for sig in [a_kv, a_state, s_pick, s_otc, s_avc] + \
                    [s[0] for s in (f_res, e_col, e_hid, e_row, f_hid)]:
                dve.sem_inc(sig.sem, sig.start)

            def step():
                steps[0] += 1
                return 1

            nc.vector.memset(xT[:, TOK:TOK + P], 0.0).then_inc(pad_set.sem, 1)

            def norm_begin(l, c, src):
                for n in range(4 * c, 4 * c + 4):
                    nc.vector.bn_stats(stats[:, n], src(n)).then_inc(dve_order.sem, step())
                dve.wait_ge(dve_order.sem, steps[0])
                for n in range(4 * c, 4 * c + 4):
                    ins = nc.vector.bn_aggr(mean_var[:, n], stats[:, n])
                ins.then_inc(ln_var[l].sem, 1)

            def norm_end(l, c):
                here = slice(4 * c, 4 * c + 4)
                dve.wait_ge(ln_std[l].sem, ln_std[l].item(c))
                nc.vector.reciprocal(spread[:, 1, here], spread[:, 0, here]).then_inc(dve_order.sem, step())
                dve.wait_ge(dve_order.sem, steps[0])
                nc.vector.scalar_tensor_tensor(out=spread[:, 2, here], in0=mean_var[:, here, 0], scalar=-1.0,
                                               in1=spread[:, 1, here], op0=ALU.mult, op1=ALU.mult)\
                    .then_inc(ln_rstd[l].sem, 1)

            def stream_norm(l, before):
                for c in range(NC):
                    before(c)
                    norm_begin(l, c, lambda n: x[:, n])
                    if c > 0:
                        norm_end(l, c - 1)
                norm_end(l, NC - 1)

            def x_loaded(c):
                dve.wait_ge(x_here[c].sem, x_here[c].moved(1))

            stream_norm(0, x_loaded)
            dve.wait_ge(ids_here.sem, ids_here.moved(1))
            nc.vector.tensor_copy(xn[:, :, D].bitcast(I32), idsb[:]).then_inc(ids_set.sem, 1)
            dve.wait_ge(consts_here.sem, consts_here.moved(1))
            dve.wait_ge(ident_here.sem, ident_here.moved(1))
            for j, col in enumerate((C_ID, C_SD, C_TRI, C_ONE)):
                nc.vector.tensor_copy(cb[:, j], C[:, col:col + P]).then_inc(consts_cast.sem, 1)

            tri = C[:, C_TRI:C_TRI + P].rearrange("p (a k) -> p a k", a=1).to_broadcast([P, HG, P])
            nc.vector.tensor_scalar(msk[:, 0], tri, 0.0, None, ALU.is_equal).then_inc(dve_order.sem, step())
            nc.vector.tensor_scalar(msk[:, 1], tri, 0.0, None, ALU.is_gt).then_inc(dve_order.sem, step())

            with dve.Fori(0, NC) as c:
                def product(e):
                    n = c * DH + e
                    dve.wait_ge(a_value.sem, a_value.item(n))
                    dve.wait_ge(a_state.sem, a_state.spare(n * 2 + 1, 4))
                    nc.vector.tensor_tensor(kvb[:, e % 2], kT[:, bass.ts(c, CH)], PS[:, e % 4], ALU.mult)\
                        .then_inc(a_kv.sem, 1)

                def state(e):
                    n = c * DH + e
                    dve.wait_ge(a_kv.sem, a_kv.item(n))
                    dve.wait_ge(a_read.sem, a_read.spare(n, 4))
                    for j in range(SPC):
                        nc.vector.tensor_tensor_scan(
                            hb[:, e % 4, j * SEQ:(j + 1) * SEQ], aT[:, bass.ds(c * CH + j * SEQ, SEQ)],
                            kvb[:, e % 2, j * SEQ:(j + 1) * SEQ], 0.0, ALU.mult, ALU.add).then_inc(a_state.sem, 1)

                dve.wait_ge(a_qk.sem, a_qk.item(c * 2 + 1))
                product(0)
                dve.wait_ge(a_gate.sem, a_gate.item(c))
                for e in range(DH):
                    if e + 1 < DH:
                        product(e + 1)
                    state(e)
            def y_rows(n):
                return PS[:, n // 4, (n % 4) * P:(n % 4 + 1) * P]

            for c in range(NC + 1):
                if c < NC:
                    dve.wait_ge(a_yrow.sem, a_yrow.item(c))
                    norm_begin(4, c, y_rows)
                if c > 0:
                    norm_end(4, c - 1)

            def add_bank(sig, done, bank0):
                def add(c):
                    dve.wait_ge(sig.sem, sig.item(c))
                    part = x[:, 4 * c:4 * c + 4].rearrange("p a b -> p (a b)")
                    nc.vector.tensor_tensor(part, part, PS[:, bank0 + c], ALU.add).then_inc(done.sem, 1)
                    dve.wait_ge(done.sem, done.item(c))
                return add

            def ffn(f, l, before):
                stream_norm(l, before)

                def hidden_step(c, k):
                    n = c * KI + k
                    dve.wait_ge(f_gelu[f].sem, f_gelu[f].item(n))
                    dve.wait_ge(f_up[f].sem, f_up[f].item(n))
                    dve.wait_ge(f_out[f].sem, f_out[f].spare(n, 4))
                    nc.vector.tensor_tensor(hT[:, k], gk[:, k % 2], PS[:, 2 + k % 2], ALU.mult)\
                        .then_inc(f_hid[f].sem, 1)

                def add_shared(c):
                    dve.wait_ge(f_out[f].sem, f_out[f].item(c * KI + KI - 1))
                    part = x[:, bass.ds(c * 4, 4)].rearrange("p a b -> p (a b)")
                    nc.vector.tensor_tensor(part, part, PS[:, 4], ALU.add).then_inc(f_res[f].sem, 1)

                dve.wait_ge(f_logits[f].sem, f_logits[f].item(0))

                def logits(n):
                    return PS[:, 7, n % 4 * P + n // 4 * 32:n % 4 * P + n // 4 * 32 + NE]

                for n in range(NT):
                    nc.vector.max(mx8[:, n], logits(n)).then_inc(dve_order.sem, step())
                    if n == NT // 2 - 1:
                        hidden_step(0, 0)
                dve.wait_ge(dve_order.sem, steps[0])
                for n in range(NT):
                    nc.vector.max_index(ix8[:, n], mx8[:, n], logits(n)).then_inc(dve_order.sem, step())
                hidden_step(0, 1)
                dve.wait_ge(dve_order.sem, steps[0])
                nc.vector.tensor_copy(ixf, ix8[:, :, 0]).then_inc(dve_order.sem, step())
                dve.wait_ge(dve_order.sem, steps[0])
                iota = C[:, C_IOTA:C_IOTA + NE].rearrange("p (a e) -> p a e", a=1).to_broadcast([P, NT, NE])
                nc.vector.tensor_tensor(one8, iota, ixf.rearrange("p (n a) -> p n a", a=1).to_broadcast([P, NT, NE]),
                                        ALU.is_equal).then_inc(dve_order.sem, step())
                dve.wait_ge(dve_order.sem, steps[0])
                nc.vector.tensor_copy(one8b[:], one8.rearrange("p a b -> p (a b)")).then_inc(f_onehot[f].sem, 1)
                hidden_step(0, 2)
                dve.wait_ge(f_prefix[f].sem, f_prefix[f].item(0))
                nc.vector.tensor_copy(tot, PS[:, 7, 0:NT * NE].rearrange("p (n e) -> p e n", e=NE))\
                    .then_inc(dve_order.sem, step())
                dve.wait_ge(dve_order.sem, steps[0])
                nc.vector.tensor_tensor_scan(csum.rearrange("p a b -> p (a b)"), C[:, C_ONE:C_ONE + NE * NT],
                                             tot.rearrange("p a b -> p (a b)"), 0.0, ALU.mult, ALU.add)\
                    .then_inc(dve_order.sem, step())
                nc.vector.tensor_reduce(cnt8[:, 0], tot, AX_X, ALU.add).then_inc(dve_order.sem, step())
                dve.wait_ge(dve_order.sem, steps[0])
                thr = C[:, C_THR:C_THR + NE * NT].rearrange("p (a b) -> p a b", a=NE)
                nc.vector.tensor_tensor(cmp8, cnt8[:, 0].rearrange("p (e a) -> p e a", a=1).to_broadcast([P, NE, NT]),
                                        thr, ALU.is_gt).then_inc(dve_order.sem, step())
                nc.vector.tensor_tensor(base, csum, tot, ALU.subtract).then_inc(dve_order.sem, step())
                dve.wait_ge(dve_order.sem, steps[0])
                nc.vector.tensor_reduce(cnt8[:, 1], cmp8, AX_X, ALU.add).then_inc(dve_order.sem, step())
                hidden_step(0, 3)
                dve.wait_ge(dve_order.sem, steps[0])
                nc.vector.tensor_tensor_scan(cnt8[:, 2], C[:, C_ONE:C_ONE + NE], cnt8[:, 1], 0.0,
                                             ALU.mult, ALU.add).then_inc(dve_order.sem, step())
                dve.wait_ge(dve_order.sem, steps[0])
                nc.vector.tensor_tensor(cnt8[:, 3], cnt8[:, 2], cnt8[:, 1], ALU.subtract)\
                    .then_inc(dve_order.sem, step())
                dve.wait_ge(dve_order.sem, steps[0])
                nc.vector.scalar_tensor_tensor(out=cnt8[:, 4], in0=cnt8[:, 3], scalar=float(P), in1=base[:, :, 0],
                                               op0=ALU.mult, op1=ALU.subtract).then_inc(dve_order.sem, step())
                dve.wait_ge(dve_order.sem, steps[0])
                nc.vector.tensor_tensor(cmp8, base,
                                        cnt8[:, 4].rearrange("p (e a) -> p e a", a=1).to_broadcast([P, NE, NT]),
                                        ALU.add).then_inc(dve_order.sem, step())
                dve.wait_ge(dve_order.sem, steps[0])
                nc.vector.tensor_tensor(work, PS[:, 6, 0:NT * NE].rearrange("p (n e) -> p n e", e=NE),
                                        cmp8.rearrange("p e n -> p n e"), ALU.add).then_inc(dve_order.sem, step())
                dve.wait_ge(dve_order.sem, steps[0])
                nc.vector.tensor_tensor(work, work, one8, ALU.mult).then_inc(dve_order.sem, step())
                dve.wait_ge(dve_order.sem, steps[0])
                nc.vector.tensor_reduce(slotf, work, AX_X, ALU.add).then_inc(dve_order.sem, step())
                dve.wait_ge(dve_order.sem, steps[0])
                nc.vector.tensor_copy(slotu[:], slotf).then_inc(f_slots[f].sem, 1)
                add_shared(0)
                hidden_step(1, 0)
                slot_no = C[:, C_SLOT:C_SLOT + SLOT_TILES * NE].rearrange("p (s e) -> p s e", e=NE)
                nc.vector.tensor_tensor(ecmp, slot_no,
                                        cnt8[:, 2].rearrange("p (a e) -> p a e", a=1).to_broadcast([P, SLOT_TILES, NE]),
                                        ALU.is_ge).then_inc(dve_order.sem, step())
                dve.wait_ge(dve_order.sem, steps[0])
                nc.vector.tensor_reduce(eidf[:, 0], ecmp, AX_X, ALU.add).then_inc(dve_order.sem, step())
                dve.wait_ge(dve_order.sem, steps[0])
                nc.vector.tensor_scalar(eidf[:, 0], eidf[:, 0], float(NE - 1), None, ALU.min)\
                    .then_inc(dve_order.sem, step())
                dve.wait_ge(dve_order.sem, steps[0])
                nc.vector.tensor_copy(eidf[:, 1], eidf[:, 0]).then_inc(dve_order.sem, step())
                for j in range(1, 6):
                    n = SLOT_TILES - j
                    dve.wait_ge(dve_order.sem, steps[0])
                    nc.vector.scalar_tensor_tensor(out=eidf[:, 1, 0:n], in0=eidf[:, 0, j:], scalar=float(NE ** j),
                                                   in1=eidf[:, 1, 0:n], op0=ALU.mult, op1=ALU.add)\
                        .then_inc(dve_order.sem, step())
                dve.wait_ge(dve_order.sem, steps[0])
                nc.vector.tensor_copy(eword[:], eidf[:, 1]).then_inc(f_experts[f].sem, 1)
                for k in range(1, KI):
                    hidden_step(1, k)
                add_shared(1)
                for k in range(KI):
                    hidden_step(2, k)

                def columns(s, k):
                    dve.wait_ge(e_turn[f].sem, e_turn[f].item(s))
                    dve.wait_ge(e_up[f].sem, e_up[f].spare(s, 4))
                    nc.vector.tensor_copy(xrT[:, k], PS[:, 6, 0:P]).then_inc(e_col[f].sem, 1)

                def out_rows(s):
                    dve.wait_ge(e_out[f].sem, e_out[f].item(s))
                    nc.vector.tensor_copy(er[:, bass.ds(s, 1)].rearrange("p a d -> p (a d)"), PS[:, 7, 0:P])\
                        .then_inc(e_row[f].sem, 1)

                def product(s, k):
                    dve.wait_ge(e_gelu[f].sem, e_gelu[f].item(s))
                    dve.wait_ge(e_up[f].sem, e_up[f].item(s))
                    dve.wait_ge(e_hturn[f].sem, e_hturn[f].spare(s, 2))
                    nc.vector.tensor_tensor(eh[:, k % 2], eg[:, k % 2], PS[:, 2 + k % 2], ALU.mult)\
                        .then_inc(e_hid[f].sem, 1)

                def expert_step(i, k, s_min=None):
                    s = i * 4 + k
                    if s_min is None or s_min + 1 < SLOT_TILES:
                        columns(s + 1, (k + 1) % 4)
                    if s_min is None or s_min >= 2:
                        out_rows(s - 2)
                    if s_min is None or s_min < SLOT_TILES:
                        product(s, k % 4)

                columns(0, 0)
                add_shared(2)
                for s in range(2):
                    expert_step(0, s, s)
                with dve.Fori(0, SLOT_TILES // 4 - 1) as i:
                    for k in range(2, 6):
                        expert_step(i, k)
                for s in range(SLOT_TILES - 2, SLOT_TILES + 2):
                    expert_step(0, s, s)

                def finish(c):
                    for k in {0: (0, 1), 1: (2,), 2: (3,)}.get(c, ()):
                        hidden_step(NC - 1, k)
                    if c == NC - 1:
                        add_shared(c)
                    dve.wait_ge(f_res[f].sem, f_res[f].item(c))
                    dve.wait_ge(f_back[f][c].sem, f_back[f][c].moved(1))
                    part = x[:, 4 * c:4 * c + 4]
                    nc.vector.tensor_tensor(part, part, yback[:, 4 * c:4 * c + 4], ALU.add).then_inc(f_done[f].sem, 1)
                    dve.wait_ge(f_done[f].sem, f_done[f].item(c))

                return finish

            finish = add_bank(a_out, a_res, 0)
            if last_phase >= 2:
                finish = ffn(0, 1, finish)

            def attention():
                dve.wait_ge(b_here.sem, b_here.moved(3))
                stream_norm(2, finish)
                nc.vector.tensor_copy(rpb[:, 0], rpos[:, 0]).then_inc(b_pos.sem, 1)
                dve.wait_ge(b_pos.sem, b_pos.item(0))
                nc.vector.tensor_tensor(rpos[:, 1], rpos[:, 0], rpb[:, 0], ALU.subtract).then_inc(b_pos.sem, 1)
                dve.wait_ge(b_pos.sem, b_pos.item(1))
                nc.vector.tensor_copy(rpb[:, 1], rpos[:, 1]).then_inc(b_pos.sem, 1)
                dve.wait_ge(b_pos.sem, b_pos.item(2))
                nc.vector.tensor_tensor(rpb[:, 2], rpos[:, 1], rpb[:, 1], ALU.subtract).then_inc(b_pos.sem, 1)

                def by_seq(ap):
                    return ap.rearrange("p (b t) -> p b t", t=SEQ)

                def table(col):
                    return C[:, col:col + SEQ].rearrange("p (a t) -> p a t", a=1).to_broadcast([P, SPC, SEQ])

                def next_keys(g):
                    now = xn[:, 4 * (g % 2):4 * (g % 2) + 4, 0:D]
                    dve.wait_ge(b_tok.sem, b_tok.item(g))
                    if g >= 2:
                        dve.wait_ge(b_tsum.sem, b_tsum.item(g - 2))
                    nc.vector.tensor_tensor(now, PS[:, 0].rearrange("p (n d) -> p n d", n=4),
                                            rowb[:, 0].rearrange("p (a d) -> p a d", a=1).to_broadcast([P, 4, D]),
                                            ALU.add).then_inc(b_tokd.sem, 1)
                    dve.wait_ge(b_tokd.sem, b_tokd.item(2 * g))
                    nc.vector.tensor_tensor(now, now, PS[:, 1].rearrange("p (n d) -> p n d", n=4), ALU.mult)\
                        .then_inc(b_tokd.sem, 1)
                    dve.wait_ge(b_tokd.sem, b_tokd.item(2 * g + 1))
                    nc.vector.tensor_reduce(nsd[:, 4 * g:4 * g + 4], now.rearrange("p n (d h) -> p n h d", h=H),
                                            AX_X, ALU.add).then_inc(b_tsum.sem, 1)

                def rest_of(c, t):
                    rest = rests(c)[t]
                    dve.wait_ge(b_hi.sem, b_hi.item(4 * c + t))
                    nc.vector.tensor_tensor(rest, rest, pb[:, c, 3 * t], ALU.subtract)\
                        .then_inc(b_rest.sem, 1)

                for c in range(NC + 1):
                    k = c % 2
                    if c < NC:
                        if c >= 2:
                            dve.wait_ge(b_low.sem, b_low.item(3 * (c - 2) + 2))
                        dve.wait_ge(b_raw.sem, b_raw.item(3 * c + 1))
                        nc.vector.tensor_tensor(by_seq(rot[:, k, 0]), by_seq(raw[:, k, 1]), table(C_COS1), ALU.mult)\
                            .then_inc(b_rot.sem, 1)
                        nc.vector.tensor_tensor(by_seq(rot[:, k, 1]), by_seq(raw[:, k, 2]), table(C_SIN1), ALU.mult)\
                            .then_inc(b_rot.sem, 1)
                        rest_of(c, 0)
                        dve.wait_ge(b_rot.sem, b_rot.item(3 * c + 1))
                        nc.vector.tensor_tensor(rot[:, k, 0], rot[:, k, 0], rot[:, k, 1], ALU.add)\
                            .then_inc(b_rot.sem, 1)
                        rest_of(c, 1)
                    if c > 0:
                        for t in range(3):
                            n = 3 * (c - 1) + t
                            dve.wait_ge(b_mid.sem, b_mid.item(4 * (c - 1) + t))
                            dve.wait_ge(b_rest.sem, b_rest.item(n))
                            nc.vector.tensor_tensor(pb[:, c - 1, 3 * t + 2], rests(c - 1)[t],
                                                    pb[:, c - 1, 3 * t + 1], ALU.subtract).then_inc(b_low.sem, 1)
                    if c < NC:
                        dve.wait_ge(b_rot.sem, b_rot.item(3 * c + 2))
                        rest_of(c, 2)
                    if c > 0:
                        next_keys(c - 1)
                dve.wait_ge(b_tsum.sem, b_tsum.item(NT // 4 - 1))
                last_q = C[:, C_LAST:C_LAST + NT].rearrange("p (n a) -> p n a", a=1).to_broadcast([P, NT, H])
                nc.vector.tensor_tensor(nsd[:], nsd[:], last_q, ALU.add).then_inc(dve_order.sem, step())
                dve.wait_ge(dve_order.sem, steps[0])
                nc.vector.tensor_scalar(nsd[:], nsd[:], -SCALE, None, ALU.mult).then_inc(b_nsd.sem, 1)

                def pick_and_max(i, k, rows):
                    u = i * BODY + k
                    kk = k % BODY
                    qt, hg = (kk // HG) % QT, kk % HG
                    tile = (i if k < BODY else i + 1) * (BODY // HG) + kk // HG
                    main = PS[:, 2 * (k % 2):2 * (k % 2) + 2].rearrange("p a (b j) -> p (a b) j", b=2)
                    if hg == 0:
                        dve.wait_ge(t_exp.sem, t_exp.spare(tile, 2))
                        dve.wait_ge(t_nsd.sem, t_nsd.item(tile))
                    dve.wait_ge(s_scores.sem, s_scores.item(u))
                    take_in(dve)
                    nc.vector.copy_predicated(main[:, :, qt * P:(qt + 1) * P], msk[:, qt],
                                              PS[:, 4].rearrange("p (a j) -> p a j", a=HG)).then_inc(s_pick.sem, 1)
                    dve.wait_ge(s_pick.sem, s_pick.item(u))
                    nc.vector.tensor_reduce(mxs[:, k % 2], main, AX_X, ALU.max).then_inc(s_max.sem, 1)
                    if rows:
                        output_rows(i, k)
                    dve.wait_ge(s_max.sem, s_max.item(u))
                    nc.vector.scalar_tensor_tensor(
                        out=nmax[:, (k // HG) % 2, hg * HG:(hg + 1) * HG], in0=mxs[:, k % 2], scalar=-SCALE,
                        in1=nsd_now[:, (k // HG) % 2, hg * HG:(hg + 1) * HG],
                        op0=ALU.mult, op1=ALU.min).then_inc(s_nmax.sem, 1)

                def denominators(i, k):
                    par = (k % BODY // HG) % 2
                    tile = i * (BODY // HG) + k % BODY // HG
                    dve.wait_ge(s_otc.sem, s_otc.item(tile))
                    dve.wait_ge(t_exp.sem, t_exp.item(tile))
                    e_next, den, rden = esm[:, par, 1], esm[:, par, 2], esm[:, par, 3]
                    nc.vector.tensor_tensor(den, otok[:, par, :, 8], e_next, ALU.add).then_inc(t_den.sem, 1)
                    dve.wait_ge(t_den.sem, t_den.item(tile))
                    nc.vector.reciprocal(rden, den).then_inc(t_rden.sem, 1)

                def output_rows(i, k):
                    tile = i * (BODY // HG) + (k - 7) // HG
                    dve.wait_ge(s_ot.sem, s_ot.item(tile))
                    dve.wait_ge(t_on.sem, t_on.spare(tile, 2))
                    nc.vector.tensor_copy(otok[:, ((k - 7) // HG) % 2],
                                          PS[:, 4].rearrange("p (h w) -> p h w", w=VW)[:, :, 0:DH + 1])\
                                              .then_inc(s_otc.sem, 1)

                def tile_arg(i, k):
                    kk = k % BODY
                    par = (kk // HG) % 2
                    tile = i * (BODY // HG) + kk // HG
                    dve.wait_ge(s_nmax.sem, s_nmax.item(i * BODY + kk))
                    dve.wait_ge(t_on.sem, t_on.spare(tile, 2))
                    nc.vector.tensor_tensor(esm[:, par, 0], nmax[:, par], nsd_now[:, par], ALU.subtract)\
                        .then_inc(t_arg.sem, 1)

                LAG = 5

                def outputs(i, k):
                    dve.wait_ge(s_av.sem, s_av.item(i * BODY + k))
                    dve.wait_ge(s_ot.sem, s_ot.spare(i * (BODY // HG) + k // HG, 2))
                    nc.vector.tensor_scalar(osb[:, k % (2 * HG)], PS[:, 7, 0:P], 1.0, None, ALU.mult)\
                        .then_inc(s_avc.sem, 1)

                def dve_unit(i, k, u_min=None):
                    rows = k % HG == HG - 1 and (u_min is None or u_min >= 7)
                    if u_min is None or u_min < UNITS:
                        pick_and_max(i, k, rows)
                    elif rows:
                        output_rows(i, k)
                    if u_min is None or u_min < UNITS:
                        if k % HG == HG - 1:
                            tile_arg(i, k) if k < BODY else tile_arg(i + 1, k - BODY)
                    if u_min is None or 3 <= u_min < UNITS + 3:
                        outputs(i, k - 3)
                    done = k - LAG
                    if done % HG == HG - 1 and (u_min is None or u_min >= LAG):
                        denominators(i, done)

                for k in range(LAG):
                    dve_unit(0, k, k)
                with dve.Fori(0, UNITS // BODY - 1) as i:
                    for k in range(LAG, BODY + LAG):
                        dve_unit(i, k)
                last = UNITS // BODY - 1
                for k in range(LAG, BODY + LAG):
                    dve_unit(last, k, last * BODY + k)

            if last_phase >= 3:
                attention()
                dve.wait_ge(t_bias.sem, t_bias.item(NT - 1))
                finish = add_bank(b_out, b_res, 4)
            if last_phase >= 4:
                finish = ffn(1, 3, finish)
            for c in range(NC):
                finish(c)

        @block.scalar
        def _(act):
            for sig in [a_qk, a_gate, a_y, s_exp, s_col, t_exp] + \
                    [s[0] for s in (f_gelu, e_gelu, e_hcol)]:
                act.sem_inc(sig.sem, sig.start)

            def col(j):
                return W[:, W_COL + j:W_COL + j + 1]

            def root(l, c):
                here = slice(4 * c, 4 * c + 4)
                act.wait_ge(ln_var[l].sem, ln_var[l].item(c))
                nc.scalar.activation(spread[:, 0, here], mean_var[:, here, 1], ACT.Sqrt,
                                     bias=C[:, C_EPS:C_EPS + 1]).then_inc(ln_std[l].sem, 1)

            def normalise(l, c, src, dst):
                act.wait_ge(ln_rstd[l].sem, ln_rstd[l].item(c))
                for n in range(4 * c, 4 * c + 4):
                    ins = nc.scalar.activation(dst(n), src(n), ACT.Identity, scale=spread[:, 1, n:n + 1],
                                               bias=spread[:, 2, n:n + 1])
                ins.then_inc(ln_rows[l].sem, 1)

            def norm_columns(l, src, dst, columns):
                for c in range(-1, NC + 1):
                    if c + 1 < NC:
                        root(l, c + 1)
                    if 0 <= c < NC:
                        normalise(l, c, src, dst)
                    if c >= 1:
                        act.wait_ge(ln_turned[l].sem, ln_turned[l].item(c - 1))
                        columns(c - 1).then_inc(ln_cols[l].sem, 1)

            def stream_columns(l):
                norm_columns(l, lambda n: x[:, n], lambda n: xn[:, n, 0:D],
                             lambda c: nc.scalar.copy(xT[:, c * CH:(c + 1) * CH], PS[:, c]))

            act.wait_ge(ident_here.sem, ident_here.moved(1))
            stream_columns(0)
            for c in range(NC + 1):
                if c < NC:
                    for j, dst in enumerate((qT, kT)):
                        act.wait_ge(a_proj.sem, a_proj.item(c * 3 + j))
                        nc.scalar.copy(dst[:, c * CH:(c + 1) * CH], PS[:, 5 + j]).then_inc(a_qk.sem, 1)
                    act.wait_ge(a_proj.sem, a_proj.item(c * 3 + 2))
                    nc.scalar.activation(aT[:, c * CH:(c + 1) * CH], PS[:, 7], ACT.Sigmoid).then_inc(a_gate.sem, 1)
                if c > 0:
                    act.wait_ge(a_sum.sem, a_sum.item(c * 2 - 1))
                    nc.scalar.copy(yT[:, (c - 1) * CH:c * CH], PS[:, 4]).then_inc(a_y.sem, 1)
            act.wait_ge(weights_here.sem, weights_here.moved(1))
            norm_columns(4, lambda n: PS[:, n // 4, (n % 4) * P:(n % 4 + 1) * P], lambda n: yn[:, n],
                         lambda c: nc.scalar.activation(ynT[:, c * CH:(c + 1) * CH], PS[:, 4 + c], ACT.Identity,
                                                        scale=col(0), bias=col(1)))

            def ffn(f, l):
                stream_columns(l)
                act.wait_ge(f_router[f].sem, f_router[f].item(0))
                nc.scalar.copy(lgT, PS[:, 6]).then_inc(f_lgcols[f].sem, 1)

                def shared_gelu(c):
                    for k in range(KI):
                        n = c * KI + k
                        act.wait_ge(f_gate[f].sem, f_gate[f].item(n))
                        act.wait_ge(f_hid[f].sem, f_hid[f].spare(n, 2))
                        nc.scalar.activation(gk[:, k % 2], PS[:, k % 2], ACT.Gelu).then_inc(f_gelu[f].sem, 1)

                with act.Fori(0, NC - 1) as c:
                    shared_gelu(c)

                def gelu(s, k):
                    act.wait_ge(e_gate[f].sem, e_gate[f].item(s))
                    act.wait_ge(e_hid[f].sem, e_hid[f].spare(s, 2))
                    nc.scalar.activation(eg[:, k % 2], PS[:, k % 2], ACT.Gelu).then_inc(e_gelu[f].sem, 1)

                def hidden_columns(s, k):
                    act.wait_ge(e_hturn[f].sem, e_hturn[f].item(s))
                    act.wait_ge(e_out[f].sem, e_out[f].spare(s, 2))
                    nc.scalar.copy(ehT[:, k % 2], PS[:, 4 + k % 2]).then_inc(e_hcol[f].sem, 1)

                gelu(0, 0)
                with act.Fori(0, SLOT_TILES // 4 - 1) as i:
                    for k in range(1, 5):
                        gelu(i * 4 + k, k)
                        hidden_columns(i * 4 + (k - 1), k - 1)
                for s in range(SLOT_TILES - 3, SLOT_TILES + 1):
                    if s < SLOT_TILES:
                        gelu(s, s)
                    hidden_columns(s - 1, s - 1)
                shared_gelu(NC - 1)

            if last_phase >= 2:
                ffn(0, 1)

            def attention():
                stream_columns(2)
                def high(c, t):
                    nc.scalar.copy(pb[:, c, 3 * t], rests(c)[t]).then_inc(b_hi.sem, 1)

                for c in range(NC + 1):
                    k, n = c % 2, 3 * c
                    if c < NC:
                        if c >= 2:
                            act.wait_ge(b_low.sem, b_low.item(n - 4))
                            act.wait_ge(b_lowp.sem, b_lowp.item(c - 2))
                        act.wait_ge(b_proj.sem, b_proj.item(n))
                        nc.scalar.activation(raw[:, k, 0], PS[:, 4], ACT.Identity, bias=col(2))
                        nc.scalar.activation(raw[:, k, 1], PS[:, 4], ACT.Identity, bias=col(3)).then_inc(b_raw.sem, 1)
                        act.wait_ge(b_proj.sem, b_proj.item(n + 1))
                        nc.scalar.activation(raw[:, k, 2], PS[:, 5], ACT.Identity, bias=col(4)).then_inc(b_raw.sem, 1)
                        act.wait_ge(b_raw.sem, b_raw.item(n))
                        high(c, 0)
                        act.wait_ge(b_proj.sem, b_proj.item(n + 2))
                        nc.scalar.copy(raw[:, k, 3], PS[:, 6]).then_inc(b_raw.sem, 1)
                        act.wait_ge(b_raw.sem, b_raw.item(n + 2))
                        high(c, 1)
                    if c > 0:
                        for t in range(4):
                            if t < 3:
                                act.wait_ge(b_rest.sem, b_rest.item(n - 3 + t))
                            else:
                                act.wait_ge(b_restp.sem, b_restp.item(c - 1))
                            nc.scalar.copy(pb[:, c - 1, 3 * t + 1], rests(c - 1)[t]).then_inc(b_mid.sem, 1)
                    if c < NC:
                        act.wait_ge(b_rot.sem, b_rot.item(n + 2))
                        high(c, 2)
                        act.wait_ge(b_rotp.sem, b_rotp.item(n + 2))
                        high(c, 3)
                    if c > 0:
                        act.wait_ge(b_tok.sem, b_tok.item(c - 1))
                        for j, dst in enumerate((vals, vnext)):
                            nc.scalar.copy(dst[:, 4 * c - 4:4 * c].rearrange("p n d -> p (n d)"), PS[:, 2 + j])\
                                .then_inc(b_tokv.sem, 1)

                def exps(u, k):
                    act.wait_ge(s_nmax.sem, s_nmax.item(u))
                    main = PS[:, 2 * (k % 2):2 * (k % 2) + 2].rearrange("p a (b j) -> p (a b) j", b=2)
                    hg = k % HG
                    for a in range(HG):
                        act.wait_ge(s_turn.sem, s_turn.spare(u * 2 + a // 2, 4))
                        h = HG * hg + a
                        nc.scalar.activation(pr[:, k % 2, a], main[:, a], ACT.Exp, scale=SCALE,
                                             bias=nmax[:, (k // HG) % 2, h:h + 1]).then_inc(s_exp.sem, 1)

                def weight_columns(u, k):
                    for a in range(2):
                        act.wait_ge(s_turn.sem, s_turn.item(u * 2 + a))
                        act.wait_ge(s_av.sem, s_av.spare(u, 2))
                        nc.scalar.copy(prT[:, k % 2, 2 * a:2 * a + 2].rearrange("p a t -> p (a t)"), PS[:, 5 + a])\
                            .then_inc(s_col.sem, 1)

                def act_unit(i, k, u_min=None):
                    u = i * BODY + k
                    free_run = u_min is None
                    if free_run or 2 <= u_min < UNITS + 2:
                        weight_columns(u - 2, k - 2)
                    if free_run or u_min < UNITS:
                        exps(u, k)
                    if k % HG == 0 and (free_run or u_min >= HG):
                        tile = i * (BODY // HG) + (k - HG) // HG
                        act.wait_ge(t_arg.sem, t_arg.item(tile))
                        par = ((k - HG) // HG) % 2
                        nc.scalar.activation(esm[:, par, 1], esm[:, par, 0], ACT.Exp).then_inc(t_exp.sem, 1)

                for k in range(4):
                    act_unit(0, k, k)
                with act.Fori(0, UNITS // BODY - 1) as i:
                    for k in range(4, BODY + 4):
                        act_unit(i, k)
                last = UNITS // BODY - 1
                for k in range(4, BODY + 4):
                    act_unit(last, k, last * BODY + k)
                for c in range(NC):
                    act.wait_ge(b_on_turn.sem, b_on_turn.item(c))
                    nc.scalar.copy(onT[:, c * CH:(c + 1) * CH], PS[:, c]).then_inc(b_on_col.sem, 1)

            if last_phase >= 3:
                attention()
            if last_phase >= 4:
                ffn(1, 3)

        @block.gpsimd
        def _(pool):
            for sig in [a_read, t_on]:
                pool.sem_inc(sig.sem, sig.start)
            for sig in [a_sum, s_av, s_turn, s_ot] + [s[0] for s in (f_out, e_up, e_hturn, e_out)]:
                pool.sem_inc(sig.sem, sig.start)

            with pool.Fori(0, NC) as c:
                pool.wait_ge(a_qk.sem, a_qk.item(c * 2 + 1))
                take_in(pool)
                for e in range(DH):
                    n = c * DH + e
                    pool.wait_ge(a_state.sem, a_state.item(n * 2 + 1))
                    pool.wait_ge(a_sum.sem, a_sum.spare(c * 2 + e // 4, 2))
                    take_in(pool)
                    nc.gpsimd.tensor_tensor(zb[:, e], qT[:, bass.ts(c, CH)], hb[:, e % 4], ALU.mult)\
                        .then_inc(a_read.sem, 1)

            def ffn(f, l):
                pool.wait_ge(ids_set.sem, ids_set.item(0))
                pool.wait_ge(f_cleared[f].sem, f_cleared[f].moved(1))
                pool.wait_ge(f_slots[f].sem, f_slots[f].item(0))
                for n in range(NT):
                    pool.indirect_dma_start(slot_rows[:, :], bass.IndirectOffsetOnAxis(ap=slotu[:, n:n + 1], axis=0),
                                            xn[:, n], None).then_inc(f_sent[f].sem, 16)
                pool.wait_ge(f_ids[f].sem, f_ids[f].moved(1))
                for s in range(SLOT_TILES):
                    pool.wait_ge(e_row[f].sem, e_row[f].item(s))
                    pool.indirect_dma_start(token_out[:, :], bass.IndirectOffsetOnAxis(ap=slot_ids[:, s:s + 1], axis=0),
                                            er[:, s], None, bounds_check=TOK - 1, oob_is_err=False)\
                        .then_inc(e_back[f].sem, 16)

            if last_phase >= 2:
                ffn(0, 1)

            def attention():
                def by_seq(ap):
                    return ap.rearrange("p (b t) -> p b t", t=SEQ)

                def table(col):
                    return C[:, col:col + SEQ].rearrange("p (a t) -> p a t", a=1).to_broadcast([P, SPC, SEQ])

                for c in range(NC + 1):
                    k, n = c % 2, 3 * c
                    if c < NC:
                        if c >= 2:
                            pool.wait_ge(b_lowp.sem, b_lowp.item(c - 2))
                        pool.wait_ge(b_raw.sem, b_raw.item(n + 1))
                        nc.gpsimd.tensor_tensor(by_seq(rot[:, k, 2]), by_seq(raw[:, k, 1]), table(C_COS2), ALU.mult)\
                            .then_inc(b_rotp.sem, 1)
                        nc.gpsimd.tensor_tensor(by_seq(rot[:, k, 3]), by_seq(raw[:, k, 2]), table(C_SIN2), ALU.mult)\
                            .then_inc(b_rotp.sem, 1)
                        pool.wait_ge(b_rotp.sem, b_rotp.item(n + 1))
                        nc.gpsimd.tensor_tensor(rot[:, k, 2], rot[:, k, 2], rot[:, k, 3], ALU.add)\
                            .then_inc(b_rotp.sem, 1)
                    if c > 0:
                        pool.wait_ge(b_mid.sem, b_mid.item(4 * c - 1))
                        pool.wait_ge(b_restp.sem, b_restp.item(c - 1))
                        nc.gpsimd.tensor_tensor(pb[:, c - 1, 11], rests(c - 1)[3], pb[:, c - 1, 10], ALU.subtract)\
                            .then_inc(b_lowp.sem, 1)
                    if c < NC:
                        pool.wait_ge(b_rotp.sem, b_rotp.item(n + 2))
                        pool.wait_ge(b_hi.sem, b_hi.item(4 * c + 3))
                        nc.gpsimd.tensor_tensor(rot[:, k, 2], rot[:, k, 2], pb[:, c, 9], ALU.subtract)\
                            .then_inc(b_restp.sem, 1)
                pool.wait_ge(b_low.sem, b_low.item(3 * NC - 1))
                pool.wait_ge(b_lowp.sem, b_lowp.item(NC - 1))
                nc.gpsimd.memset(vring.rearrange("p a b w -> p (a b w)"), 0.0).then_inc(b_vpad.sem, 1)
                pool.wait_ge(b_vpad.sem, b_vpad.item(0))
                padded = vring.rearrange("p a b (h w) -> p a b h w", w=VW)
                nc.gpsimd.memset(padded.rearrange("p a b h w -> p (a b h) w")[:, :, DH:DH + 1], 1.0)\
                    .then_inc(b_vpad.sem, 1)
                pool.wait_ge(b_vpad.sem, b_vpad.item(1))

                def pad_values(b, par):
                    for j in range(QT):
                        ins = nc.gpsimd.tensor_copy(padded[:, par, j, :, 0:DH],
                                                    vals[:, bass.ds(b * QT + j, 1)].rearrange("p a (h d) -> p (a h) d", h=H))
                    ins.then_inc(b_vring.sem, 1)

                def next_scores(tile, par):
                    nc.gpsimd.tensor_copy(nsd_now[:, par], nsd[:, bass.ds(tile, 1)].rearrange("p a h -> p (a h)"))\
                        .then_inc(t_nsd.sem, 1)

                def finish_tile(tile, par):
                    one = bass.ds(tile, 1)
                    e_next, rden = esm[:, par, 1], esm[:, par, 3]
                    now = t4[:, par].rearrange("p (h d) -> p h d", h=H)
                    pool.wait_ge(t_exp.sem, t_exp.item(tile))
                    take_in(pool)
                    nc.gpsimd.tensor_tensor(now, vnext[:, one].rearrange("p a (h d) -> p (a h) d", h=H),
                                            e_next.rearrange("p (h a) -> p h a", a=1).to_broadcast([P, H, DH]),
                                            ALU.mult).then_inc(t_v.sem, 1)
                    pool.wait_ge(s_otc.sem, s_otc.item(tile))
                    pool.wait_ge(t_v.sem, t_v.item(tile))
                    nc.gpsimd.tensor_tensor(now, now, otok[:, par, :, 0:DH], ALU.add).then_inc(t_sum.sem, 1)
                    tile_x = x[:, one].rearrange("p a d -> p (a d)")
                    nc.gpsimd.tensor_tensor(tile_x, tile_x, rowb[:, 1], ALU.add).then_inc(t_bias.sem, 1)
                    pool.wait_ge(t_rden.sem, t_rden.item(tile))
                    pool.wait_ge(t_sum.sem, t_sum.item(tile))
                    take_in(pool)
                    nc.gpsimd.tensor_tensor(on[:, one].rearrange("p a (h d) -> p (a h) d", h=H), now,
                                            rden.rearrange("p (h a) -> p h a", a=1).to_broadcast([P, H, DH]), ALU.mult)\
                        .then_inc(t_on.sem, 1)

                for b in range(2):
                    pool.wait_ge(b_tokv.sem, b_tokv.item(2 * (b * QT // 4)))
                    pad_values(b, b)
                pool.wait_ge(b_tokv.sem, b_tokv.item(2 * (NT // 4) - 1))
                pool.wait_ge(b_nsd.sem, b_nsd.item(0))
                for tile in range(2):
                    next_scores(tile, tile)
                tiles = BODY // HG
                with pool.Fori(0, UNITS // BODY - 1) as i:
                    for j in range(tiles):
                        pool.wait_ge(t_arg.sem, t_arg.item(i * tiles + j))
                        take_in(pool)
                        next_scores(i * tiles + (j + 2), j % 2)
                        finish_tile(i * tiles + j, j % 2)
                        if j % QT == QT - 1:
                            par = j // QT
                            pool.wait_ge(s_av.sem, s_av.item(i * BODY + ((par + 1) * UPB - 1)))
                            take_in(pool)
                            pad_values(i * 2 + (2 + par), par)
                for tile in range(NT - tiles, NT):
                    if tile + 2 < NT:
                        pool.wait_ge(t_arg.sem, t_arg.item(tile))
                        next_scores(tile + 2, tile % 2)
                    finish_tile(tile, tile % 2)

            if last_phase >= 3:
                attention()
            if last_phase >= 4:
                ffn(1, 3)


def host_constants():
    f = np.float32
    p = np.arange(P)
    consts = np.zeros((P, C_ALL), f)
    consts[:, C_ID:C_ID + P] = np.eye(P)
    consts[:, C_EPS] = EPS
    for g in range(2):
        consts[p, C_HEADS + 32 * g + H * g + p // DH] = 1
    consts[:-1, C_SD:C_SD + P] = -BIG * np.eye(P)[1:]
    consts[:, C_TRI:C_TRI + P] = p[:, None] < p[None, :]
    consts[:, C_ONE:C_ONE + P] = 1
    consts[:, C_IOTA:C_IOTA + NE] = np.arange(NE)
    consts[:, C_THR:C_THR + NE * NT] = np.tile(P * np.arange(NT), NE)
    consts[:, C_SLOT:C_SLOT + SLOT_TILES * NE] = np.repeat(np.arange(SLOT_TILES), NE)
    consts[P - 1, C_LAST:C_LAST + NT] = np.where(np.arange(NT) % QT == QT - 1, -BIG, 0)
    freq = (1.0 / 10000.0 ** (np.arange(0, DH, 2, dtype=f) / f(DH))).astype(f).astype(np.float64)
    pos = np.arange(SEQ)
    half = DH // 2
    dim = p // H
    row_f = freq[dim % half][:, None]
    sign = np.where(dim < half, -1.0, 1.0)[:, None]
    for cos_col, sin_col, ahead in ((C_COS1, C_SIN1, 0), (C_COS2, C_SIN2, SEQ)):
        angle = row_f * (pos + ahead)[None, :]
        consts[:, cos_col:cos_col + SEQ] = sign * np.cos(angle)
        consts[:, sin_col:sin_col + SEQ] = np.sin(angle)
    angle = freq[:, None] * pos[None, :]
    positions = np.concatenate([np.sin(angle), np.cos(angle)]).astype(f)
    rules = np.zeros((2, H, SEQ), "uint16")
    rules[0, :, P - 1] = 0xF149
    rules[1, :, P] = 0x3F80
    rules = rules.reshape(2, H * SEQ).view(f)
    token_ids = (np.arange(NT)[None, :] * P + p[:, None]).astype(np.int32)
    clear_row = np.zeros((P, ROWW), np.int32)
    clear_row[:, D] = NO_TOKEN
    return dict(consts=consts, positions=positions, row96=rules,
                token_ids=token_ids, clear_row=clear_row.view(f))


LAST_PHASE = 4


def kernel(**inputs):
    import concourse.bacc as bacc
    from concourse.bass_utils import run_bass_kernel_spmd

    a = {k: np.asarray(v) for k, v in inputs.items()}
    A, B, Fn = (lambda n: a["L0_attn_a_" + n]), (lambda n: a["L0_attn_b_" + n]), (lambda n: a["L0_ffn_" + n])
    swap = np.arange(D) ^ (DH // 2)
    by_dim = np.arange(D).reshape(H, DH).T.reshape(-1)
    by_sum = np.array([hd * DH + 4 * g + j for j in range(4) for g in range(2) for hd in range(H)])
    u, v = B("u").reshape(-1), B("v").reshape(-1)
    columns = np.stack([A("gamma")[by_sum], A("beta")[by_sum], u[by_dim], v[by_dim], v[swap[by_dim]]], 1)
    weights = np.concatenate([A("Wq").T, A("Wk").T, A("Wg").T, A("Wo").T[by_sum], B("Wq")[:, swap[by_dim]],
                              B("Wq")[:, by_dim], B("Wv"), B("Wk")[:, by_dim], B("Wo"),
                              Fn("Wg"), np.zeros((D, 32 - NE), np.float32), columns], 1)
    row_head = np.arange(P) // DH * DH
    spread_w = np.stack([A("Wv").T[:, row_head + e] for e in range(DH)], 1).reshape(D, DH * P)
    arrays = dict(
        x_in=A("x").reshape(TOK, D), weights=weights, spread_w=spread_w,
        rows=np.stack([u[by_dim], B("bo")]),
        w1=Fn("W1"), w2=Fn("W2"), w3=Fn("W3"), w1s=Fn("w1s"), w2s=Fn("w2s"), w3s=Fn("w3s"), **host_constants())
    arrays = {k: np.ascontiguousarray(v) for k, v in arrays.items()}
    nc = bacc.Bacc("TRN2", target_bir_lowering=False, num_devices=1)
    aps, feeds = {}, {}
    for name, v in arrays.items():
        aps[name] = nc.dram_tensor(f"{name}_dram", v.shape, mybir.dt.from_np(v.dtype), kind="ExternalInput").ap()
        feeds[f"{name}_dram"] = v
    aps["row96"] = aps["row96"].bitcast(BF16)
    out = nc.dram_tensor("out_dram", (TOK, D), F32, kind="ExternalOutput").ap()
    build_program(nc, out=out, last_phase=LAST_PHASE, **aps)
    r = run_bass_kernel_spmd(nc, [feeds], core_ids=[0])
    return r.results[0]["out_dram"].reshape(BATCH, SEQ, D)
```
